# Optimizing a Trainium2 kernel written in Bass

```python
import numpy as np
import jax
import jax.numpy as jnp

def _softmax(x, axis=-1):
    return jax.nn.softmax(x, axis=axis)

def _gelu(x):
    return jax.nn.gelu(x, approximate=True)

def _silu(x):
    return jax.nn.silu(x)

def _sigmoid(x):
    return jax.nn.sigmoid(x)

def _layernorm(x, axis=-1, eps=1e-05):
    m = jnp.mean(x, axis=axis, keepdims=True)
    v = jnp.var(x, axis=axis, keepdims=True)
    return (x - m) / jnp.sqrt(v + eps)

def _scatter_add(tgt, idx, src, axis=0):
    return tgt.at[idx].add(src)

def _segment_sum(src, seg, n):
    return jax.ops.segment_sum(src, seg, n)
kernel_name = 'mk_macaron_d2_jaxref_r8_693ff9'

def setup_inputs(seed: int=0):
    np.random.seed(seed)
    _w = jnp.asarray

    def _L0_attn_setup():
        import jax, jax.numpy as jnp
        import numpy as np
        D_MODEL = 128
        D_INNER = 2 * D_MODEL
        D_STATE = 16
        D_CONV = 4
        DT_RANK = (D_MODEL + 15) // 16
        B, L = (1, 256)

        def _causal_depthwise_conv(x, w, b):
            xp = jnp.pad(x, ((0, 0), (D_CONV - 1, 0), (0, 0)))
            y = b[None, None, :]
            for k in range(D_CONV):
                y = y + xp[:, k:k + x.shape[1], :] * w[None, None, :, k]
            return y

        def _selective_scan(x, dt, Bm, Cm, A, D):
            dA = jnp.exp(dt[..., None] * A)
            dBx = (dt * x)[..., None] * Bm[:, :, None, :]

            def step(h, inputs):
                dA_t, dBx_t, C_t = inputs
                h = dA_t * h + dBx_t
                y = jnp.einsum('bdn,bn->bd', h, C_t)
                return (h, y)
            h0 = jnp.zeros((x.shape[0], x.shape[2], A.shape[1]), x.dtype)
            xs = (jnp.swapaxes(dA, 0, 1), jnp.swapaxes(dBx, 0, 1), jnp.swapaxes(Cm, 0, 1))
            _, ys = jax.lax.scan(step, h0, xs)
            return jnp.swapaxes(ys, 0, 1) + x * D[None, None, :]

        def _mamba_dir(h, in_proj_w, conv_w, conv_b, x_proj_w, dt_proj_w, dt_proj_b, A_log, D, out_proj_w):
            xz = h @ in_proj_w.T
            x, z = (xz[..., :D_INNER], xz[..., D_INNER:])
            x = jax.nn.silu(_causal_depthwise_conv(x, conv_w, conv_b))
            x_dbl = x @ x_proj_w.T
            dt = jax.nn.softplus(x_dbl[..., :DT_RANK] @ dt_proj_w.T + dt_proj_b)
            Bm = x_dbl[..., DT_RANK:DT_RANK + D_STATE]
            Cm = x_dbl[..., DT_RANK + D_STATE:]
            A = -jnp.exp(A_log)
            y = _selective_scan(x, dt, Bm, Cm, A, D)
            y = y * jax.nn.silu(z)
            return y @ out_proj_w.T
        key = jax.random.key(seed)
        ks = jax.random.split(key, 16)
        s = 0.02
        inp = {}
        inp['hidden_states'] = jax.random.normal(ks[0], (B, L, D_MODEL), jnp.float32)
        inp['in_proj_w'] = jax.random.normal(ks[1], (2 * D_INNER, D_MODEL), jnp.float32) * s
        inp['out_proj_w'] = jax.random.normal(ks[2], (D_MODEL, D_INNER), jnp.float32) * s
        for tag, off in (('f', 3), ('r', 9)):
            inp[f'conv_w_{tag}'] = jax.random.normal(ks[off + 0], (D_INNER, D_CONV), jnp.float32) * 0.3
            inp[f'conv_b_{tag}'] = jax.random.normal(ks[off + 1], (D_INNER,), jnp.float32) * 0.02
            inp[f'x_proj_w_{tag}'] = jax.random.normal(ks[off + 2], (DT_RANK + 2 * D_STATE, D_INNER), jnp.float32) * s
            inp[f'dt_proj_w_{tag}'] = jax.random.normal(ks[off + 3], (D_INNER, DT_RANK), jnp.float32) * DT_RANK ** (-0.5)
            inp[f'dt_proj_b_{tag}'] = jnp.log(jnp.expm1(jnp.full((D_INNER,), 0.01, jnp.float32)))
            inp[f'A_log_{tag}'] = jnp.log(jnp.broadcast_to(jnp.arange(1, D_STATE + 1, dtype=jnp.float32), (D_INNER, D_STATE)))
            inp[f'D_{tag}'] = jnp.ones((D_INNER,), jnp.float32)
        return inp
    _L0_attn_in = _L0_attn_setup()

    def _L0_ffn_setup():
        import jax, jax.numpy as jnp
        import numpy as np
        B, T, C = (2, 64, 128)
        I = 512
        E = 8
        K = 2
        key = jax.random.key(seed)
        ks = jax.random.split(key, 8)
        s = 0.02
        return {'x': jax.random.normal(ks[0], (B, T, C), jnp.float32), 'Wr1': jax.random.normal(ks[1], (C, C // 4), jnp.float32) * s, 'br1': jnp.zeros((C // 4,), jnp.float32), 'Wr2': jax.random.normal(ks[2], (C // 4, E), jnp.float32) * s, 'br2': jnp.zeros((E,), jnp.float32), 'Ws1': jax.random.normal(ks[3], (C, I), jnp.float32) * s, 'bs1': jnp.zeros((I,), jnp.float32), 'Ws2': jax.random.normal(ks[4], (I, C), jnp.float32) * s, 'bs2': jnp.zeros((C,), jnp.float32), 'We1': jax.random.normal(ks[5], (E, C, I), jnp.float32) * s, 'be1': jnp.zeros((E, I), jnp.float32), 'We2': jax.random.normal(ks[6], (E, I, C), jnp.float32) * s, 'be2': jnp.zeros((E, C), jnp.float32)}
    _L0_ffn_in = _L0_ffn_setup()

    def _L1_attn_setup():
        import jax, jax.numpy as jnp
        import numpy as np
        B, S, E, H = (2, 256, 128, 16)
        key = jax.random.key(seed)
        k0, k1, k2 = jax.random.split(key, 3)
        x = jax.random.normal(k0, (B, S, E), jnp.float32)
        w_in = jax.random.normal(k1, (3 * E, E), jnp.float32) / np.sqrt(E)
        b_in = jnp.zeros((3 * E,), jnp.float32)
        w_out = jax.random.normal(k2, (E, E), jnp.float32) / np.sqrt(E)
        b_out = jnp.zeros((E,), jnp.float32)
        return {'x': x, 'w_in': w_in, 'b_in': b_in, 'w_out': w_out, 'b_out': b_out}
    _L1_attn_in = _L1_attn_setup()

    def _L1_ffn_setup():
        import jax, jax.numpy as jnp
        import numpy as np
        D_IN, D_HID = (128, 512)

        def _ternary(key, shape):
            return jax.random.randint(key, shape, -1, 2).astype(jnp.float32)

        def _tlin(x, w, s):
            return jnp.einsum('bsi,oi->bso', x, w) * s
        key = jax.random.key(seed)
        ks = jax.random.split(key, 12)
        inv = lambda fan: 1.0 / np.sqrt(fan).astype(np.float32)
        return {'x': jax.random.normal(ks[0], (4, 256, D_IN), dtype=jnp.float32), 'w1_w': _ternary(ks[1], (D_HID, D_IN)), 'w1_s': jax.random.uniform(ks[2], (D_HID,), dtype=jnp.float32) * inv(D_IN), 'w2_w': _ternary(ks[3], (D_HID, D_IN)), 'w2_s': jax.random.uniform(ks[4], (D_HID,), dtype=jnp.float32) * inv(D_IN), 'h1_w': _ternary(ks[5], (D_HID, D_HID)), 'h1_s': jax.random.uniform(ks[6], (D_HID,), dtype=jnp.float32) * inv(D_HID), 'h2_w': _ternary(ks[7], (D_HID, D_HID)), 'h2_s': jax.random.uniform(ks[8], (D_HID,), dtype=jnp.float32) * inv(D_HID), 'w3_w': _ternary(ks[9], (D_IN, D_HID)), 'w3_s': jax.random.uniform(ks[10], (D_IN,), dtype=jnp.float32) * inv(D_HID)}
    _L1_ffn_in = _L1_ffn_setup()
    _d = {'L0_attn_hidden_states': _L0_attn_in['hidden_states'], 'L0_attn_in_proj_w': _L0_attn_in['in_proj_w'], 'L0_attn_out_proj_w': _L0_attn_in['out_proj_w'], 'L0_attn_conv_w_f': _L0_attn_in['conv_w_f'], 'L0_attn_conv_b_f': _L0_attn_in['conv_b_f'], 'L0_attn_x_proj_w_f': _L0_attn_in['x_proj_w_f'], 'L0_attn_dt_proj_w_f': _L0_attn_in['dt_proj_w_f'], 'L0_attn_dt_proj_b_f': _L0_attn_in['dt_proj_b_f'], 'L0_attn_A_log_f': _L0_attn_in['A_log_f'], 'L0_attn_D_f': _L0_attn_in['D_f'], 'L0_attn_conv_w_r': _L0_attn_in['conv_w_r'], 'L0_attn_conv_b_r': _L0_attn_in['conv_b_r'], 'L0_attn_x_proj_w_r': _L0_attn_in['x_proj_w_r'], 'L0_attn_dt_proj_w_r': _L0_attn_in['dt_proj_w_r'], 'L0_attn_dt_proj_b_r': _L0_attn_in['dt_proj_b_r'], 'L0_attn_A_log_r': _L0_attn_in['A_log_r'], 'L0_attn_D_r': _L0_attn_in['D_r'], 'L0_ffn_Wr1': _L0_ffn_in['Wr1'], 'L0_ffn_br1': _L0_ffn_in['br1'], 'L0_ffn_Wr2': _L0_ffn_in['Wr2'], 'L0_ffn_br2': _L0_ffn_in['br2'], 'L0_ffn_Ws1': _L0_ffn_in['Ws1'], 'L0_ffn_bs1': _L0_ffn_in['bs1'], 'L0_ffn_Ws2': _L0_ffn_in['Ws2'], 'L0_ffn_bs2': _L0_ffn_in['bs2'], 'L0_ffn_We1': _L0_ffn_in['We1'], 'L0_ffn_be1': _L0_ffn_in['be1'], 'L0_ffn_We2': _L0_ffn_in['We2'], 'L0_ffn_be2': _L0_ffn_in['be2'], 'L1_attn_w_in': _L1_attn_in['w_in'], 'L1_attn_b_in': _L1_attn_in['b_in'], 'L1_attn_w_out': _L1_attn_in['w_out'], 'L1_attn_b_out': _L1_attn_in['b_out'], 'L1_ffn_w1_w': _L1_ffn_in['w1_w'], 'L1_ffn_w1_s': _L1_ffn_in['w1_s'], 'L1_ffn_w2_w': _L1_ffn_in['w2_w'], 'L1_ffn_w2_s': _L1_ffn_in['w2_s'], 'L1_ffn_h1_w': _L1_ffn_in['h1_w'], 'L1_ffn_h1_s': _L1_ffn_in['h1_s'], 'L1_ffn_h2_w': _L1_ffn_in['h2_w'], 'L1_ffn_h2_s': _L1_ffn_in['h2_s'], 'L1_ffn_w3_w': _L1_ffn_in['w3_w'], 'L1_ffn_w3_s': _L1_ffn_in['w3_s']}
    _x0 = _d['L0_attn_hidden_states']
    _d['L0_attn_hidden_states'] = jax.random.normal(jax.random.fold_in(jax.random.key(seed), 1), (4, 1024, 128), dtype=_x0.dtype)
    del _x0
    return _d

def reference(L0_attn_hidden_states, L0_attn_in_proj_w, L0_attn_out_proj_w, L0_attn_conv_w_f, L0_attn_conv_b_f, L0_attn_x_proj_w_f, L0_attn_dt_proj_w_f, L0_attn_dt_proj_b_f, L0_attn_A_log_f, L0_attn_D_f, L0_attn_conv_w_r, L0_attn_conv_b_r, L0_attn_x_proj_w_r, L0_attn_dt_proj_w_r, L0_attn_dt_proj_b_r, L0_attn_A_log_r, L0_attn_D_r, L0_ffn_Wr1, L0_ffn_br1, L0_ffn_Wr2, L0_ffn_br2, L0_ffn_Ws1, L0_ffn_bs1, L0_ffn_Ws2, L0_ffn_bs2, L0_ffn_We1, L0_ffn_be1, L0_ffn_We2, L0_ffn_be2, L1_attn_w_in, L1_attn_b_in, L1_attn_w_out, L1_attn_b_out, L1_ffn_w1_w, L1_ffn_w1_s, L1_ffn_w2_w, L1_ffn_w2_s, L1_ffn_h1_w, L1_ffn_h1_s, L1_ffn_h2_w, L1_ffn_h2_s, L1_ffn_w3_w, L1_ffn_w3_s):

    def _L0_attn_ref(hidden_states, in_proj_w, out_proj_w, conv_w_f, conv_b_f, x_proj_w_f, dt_proj_w_f, dt_proj_b_f, A_log_f, D_f, conv_w_r, conv_b_r, x_proj_w_r, dt_proj_w_r, dt_proj_b_r, A_log_r, D_r):
        import jax, jax.numpy as jnp
        import numpy as np
        D_MODEL = 128
        D_INNER = 2 * D_MODEL
        D_STATE = 16
        D_CONV = 4
        DT_RANK = (D_MODEL + 15) // 16
        B, L = (1, 256)

        def _causal_depthwise_conv(x, w, b):
            xp = jnp.pad(x, ((0, 0), (D_CONV - 1, 0), (0, 0)))
            y = b[None, None, :]
            for k in range(D_CONV):
                y = y + xp[:, k:k + x.shape[1], :] * w[None, None, :, k]
            return y

        def _selective_scan(x, dt, Bm, Cm, A, D):
            dA = jnp.exp(dt[..., None] * A)
            dBx = (dt * x)[..., None] * Bm[:, :, None, :]

            def step(h, inputs):
                dA_t, dBx_t, C_t = inputs
                h = dA_t * h + dBx_t
                y = jnp.einsum('bdn,bn->bd', h, C_t)
                return (h, y)
            h0 = jnp.zeros((x.shape[0], x.shape[2], A.shape[1]), x.dtype)
            xs = (jnp.swapaxes(dA, 0, 1), jnp.swapaxes(dBx, 0, 1), jnp.swapaxes(Cm, 0, 1))
            _, ys = jax.lax.scan(step, h0, xs)
            return jnp.swapaxes(ys, 0, 1) + x * D[None, None, :]

        def _mamba_dir(h, in_proj_w, conv_w, conv_b, x_proj_w, dt_proj_w, dt_proj_b, A_log, D, out_proj_w):
            xz = h @ in_proj_w.T
            x, z = (xz[..., :D_INNER], xz[..., D_INNER:])
            x = jax.nn.silu(_causal_depthwise_conv(x, conv_w, conv_b))
            x_dbl = x @ x_proj_w.T
            dt = jax.nn.softplus(x_dbl[..., :DT_RANK] @ dt_proj_w.T + dt_proj_b)
            Bm = x_dbl[..., DT_RANK:DT_RANK + D_STATE]
            Cm = x_dbl[..., DT_RANK + D_STATE:]
            A = -jnp.exp(A_log)
            y = _selective_scan(x, dt, Bm, Cm, A, D)
            y = y * jax.nn.silu(z)
            return y @ out_proj_w.T
        out_fwd = _mamba_dir(hidden_states, in_proj_w, conv_w_f, conv_b_f, x_proj_w_f, dt_proj_w_f, dt_proj_b_f, A_log_f, D_f, out_proj_w)
        h_rev = jnp.flip(hidden_states, axis=1)
        out_rev = _mamba_dir(h_rev, in_proj_w, conv_w_r, conv_b_r, x_proj_w_r, dt_proj_w_r, dt_proj_b_r, A_log_r, D_r, out_proj_w)
        return out_fwd + jnp.flip(out_rev, axis=1)

    def _L0_ffn_ref(x, Wr1, br1, Wr2, br2, Ws1, bs1, Ws2, bs2, We1, be1, We2, be2):
        import jax, jax.numpy as jnp
        import numpy as np
        B, T, C = (2, 64, 128)
        I = 512
        E = 8
        K = 2
        Bb, Tt, Cc = x.shape
        xf = x.reshape(-1, Cc)
        logits = jax.nn.relu(xf @ Wr1 + br1) @ Wr2 + br2
        gates = jax.nn.softmax(logits, axis=-1)
        tg, ti = jax.lax.top_k(gates, K)
        tg = jax.nn.softmax(tg / K, axis=-1)
        out = jax.nn.silu(xf @ Ws1 + bs1) @ Ws2 + bs2
        for e in range(E):
            h = jax.nn.silu(xf @ We1[e] + be1[e]) @ We2[e] + be2[e]
            w = jnp.sum(tg * (ti == e), axis=-1)
            out = out + w[:, None] * h
        return out.reshape(Bb, Tt, Cc)

    def _L1_attn_ref(x, w_in, b_in, w_out, b_out):
        import jax, jax.numpy as jnp
        import numpy as np
        B, S, E, H = (2, 256, 128, 16)
        bsz, slen, esz = x.shape
        hsz = esz // H
        qkv = x @ w_in.T + b_in
        q, k, v = jnp.split(qkv, 3, axis=-1)

        def to_heads(t):
            return t.reshape(bsz, slen, H, hsz).transpose(0, 2, 1, 3)
        q, k, v = (to_heads(q), to_heads(k), to_heads(v))
        scale = np.float32(1.0 / np.sqrt(hsz))
        scores = jnp.einsum('bhqd,bhkd->bhqk', q * scale, k)
        causal_bias = jnp.where(jnp.tril(jnp.ones((slen, slen), dtype=bool)), 0.0, -jnp.inf).astype(x.dtype)
        scores = scores + causal_bias
        attn = jax.nn.softmax(scores, axis=-1)
        out = jnp.einsum('bhqk,bhkd->bhqd', attn, v)
        out = out.transpose(0, 2, 1, 3).reshape(bsz, slen, esz)
        out = out @ w_out.T + b_out
        out = jnp.where(jnp.isnan(out), jnp.zeros((), out.dtype), out)
        return out

    def _L1_ffn_ref(x, w1_w, w1_s, w2_w, w2_s, h1_w, h1_s, h2_w, h2_s, w3_w, w3_s):
        import jax, jax.numpy as jnp
        import numpy as np
        D_IN, D_HID = (128, 512)

        def _ternary(key, shape):
            return jax.random.randint(key, shape, -1, 2).astype(jnp.float32)

        def _tlin(x, w, s):
            return jnp.einsum('bsi,oi->bso', x, w) * s
        h = jax.nn.silu(_tlin(x, w1_w, w1_s)) * _tlin(x, w2_w, w2_s)
        h = jax.nn.gelu(_tlin(h, h1_w, h1_s), approximate=False)
        h = jax.nn.gelu(_tlin(h, h2_w, h2_s), approximate=False)
        return _tlin(h, w3_w, w3_s)
    x = L0_attn_hidden_states
    x = x + 0.5 * _L0_ffn_ref(_layernorm(x, axis=-1), L0_ffn_Wr1, L0_ffn_br1, L0_ffn_Wr2, L0_ffn_br2, L0_ffn_Ws1, L0_ffn_bs1, L0_ffn_Ws2, L0_ffn_bs2, L0_ffn_We1, L0_ffn_be1, L0_ffn_We2, L0_ffn_be2)
    x = x + _L0_attn_ref(_layernorm(x, axis=-1), L0_attn_in_proj_w, L0_attn_out_proj_w, L0_attn_conv_w_f, L0_attn_conv_b_f, L0_attn_x_proj_w_f, L0_attn_dt_proj_w_f, L0_attn_dt_proj_b_f, L0_attn_A_log_f, L0_attn_D_f, L0_attn_conv_w_r, L0_attn_conv_b_r, L0_attn_x_proj_w_r, L0_attn_dt_proj_w_r, L0_attn_dt_proj_b_r, L0_attn_A_log_r, L0_attn_D_r)
    x = x + 0.5 * _L0_ffn_ref(_layernorm(x, axis=-1), L0_ffn_Wr1, L0_ffn_br1, L0_ffn_Wr2, L0_ffn_br2, L0_ffn_Ws1, L0_ffn_bs1, L0_ffn_Ws2, L0_ffn_bs2, L0_ffn_We1, L0_ffn_be1, L0_ffn_We2, L0_ffn_be2)
    x = x + 0.5 * _L1_ffn_ref(_layernorm(x, axis=-1), L1_ffn_w1_w, L1_ffn_w1_s, L1_ffn_w2_w, L1_ffn_w2_s, L1_ffn_h1_w, L1_ffn_h1_s, L1_ffn_h2_w, L1_ffn_h2_s, L1_ffn_w3_w, L1_ffn_w3_s)
    x = x + _L1_attn_ref(_layernorm(x, axis=-1), L1_attn_w_in, L1_attn_b_in, L1_attn_w_out, L1_attn_b_out)
    x = x + 0.5 * _L1_ffn_ref(_layernorm(x, axis=-1), L1_ffn_w1_w, L1_ffn_w1_s, L1_ffn_w2_w, L1_ffn_w2_s, L1_ffn_h1_w, L1_ffn_h1_s, L1_ffn_h2_w, L1_ffn_h2_s, L1_ffn_w3_w, L1_ffn_w3_s)
    return x

_drawn_inputs = setup_inputs


def setup_inputs(seed=0):
    import zlib

    import numpy as np

    out = dict(_drawn_inputs(seed))
    spreads = {'L0_attn_dt_proj_b_f': (-4.600166320800781, 0.2),
     'L0_attn_D_f': (1.0, 0.2),
     'L0_attn_dt_proj_b_r': (-4.600166320800781, 0.2),
     'L0_attn_D_r': (1.0, 0.2),
     'L0_ffn_br1': (0.0, 0.1),
     'L0_ffn_br2': (0.0, 0.1),
     'L0_ffn_bs1': (0.0, 0.1),
     'L0_ffn_bs2': (0.0, 0.1),
     'L0_ffn_be1': (0.0, 0.1),
     'L0_ffn_be2': (0.0, 0.1),
     'L1_attn_b_in': (0.0, 0.1),
     'L1_attn_b_out': (0.0, 0.1)}
    factors = {}
    for name, (base, spread) in spreads.items():
        noise = np.random.default_rng([zlib.crc32(name.encode()), seed]).standard_normal(out[name].shape)
        drawn = base * np.exp(spread * noise) if base else spread * noise
        out[name] = jnp.asarray(drawn.astype(out[name].dtype))
    for name, factor in factors.items():
        out[name] = (out[name] * factor).astype(out[name].dtype)
    return out
```

```python
from contextlib import ExitStack

import numpy as np

import concourse.bass as bass
from concourse import mybir

F32 = mybir.dt.float32
F32R = mybir.dt.float32r
ACT = mybir.ActivationFunctionType
ALU = mybir.AluOpType
AX = mybir.AxisListType.X

P = 128
NBATCH, SEQ = 4, 1024
TOKENS = NBATCH * SEQ
TILES = TOKENS // P
BLK = 512
NBLK = TOKENS // BLK
TPB = BLK // P
EPS = 1e-5


def wait(eng, sem, value):
    if not isinstance(value, int) or value > 0:
        eng.wait_ge(sem, value)


class Chain:

    def __init__(self, eng, sem, base=0):
        self.eng, self.sem, self.base, self.n = eng, sem, base, 0

    def step(self, ins):
        self.n += 1
        ins.then_inc(self.sem, 1)
        return ins

    def join(self):
        wait(self.eng, self.sem, self.base + self.n)


class Phase:

    def __init__(self, nc, ctx, tag):
        self.nc, self.ctx, self.tag, self.sems = nc, ctx, tag, []

    def sb(self, name, shape, dt=F32):
        return self.ctx.enter_context(self.nc.sbuf_tensor(f"{self.tag}_{name}", shape, dt))

    def ps(self, name, shape, dt=F32):
        return self.ctx.enter_context(self.nc.psum_tensor(f"{self.tag}_{name}", shape, dt))

    def sem(self, name):
        s = self.ctx.enter_context(self.nc.semaphore(f"{self.tag}_{name}"))
        self.sems.append(s)
        return s

    def clear(self):
        with self.nc.Block() as block:
            @block.gpsimd
            def _(pool):
                for s in self.sems:
                    pool.sem_clear(s)


def norm_stats(nc, dve, chain, x_tile, stats, mv, spare):
    n = mv.shape[1]
    for t in range(n):
        last = dve.bn_stats(stats[:, t, :], x_tile(t))
    chain.step(last)
    chain.join()
    dve.tensor_copy(spare[:], stats[:, 0, 0:1])
    for t in range(n):
        last = dve.bn_aggr(mv[:, t, :], stats[:, t, :])
    return last


def moe_ffn(nc, tag, x, ident, w):
    E = 8
    JOBS = E + 1
    KC = 4
    NUP = JOBS * KC
    with ExitStack() as ctx:
        ph = Phase(nc, ctx, tag)
        sb, sem = ph.sb, ph.sem
        w1h, w1l = sb("w1h", [P, JOBS, 512], F32R), sb("w1l", [P, JOBS, 512], F32R)
        w2h, w2l = sb("w2h", [P, JOBS, 512], F32R), sb("w2l", [P, JOBS, 512], F32R)
        NST = 4
        wst = sb("wst", [P, NST, 512])
        wr1s = sb("wr1s", [P, P])
        wr1h, wr1l = sb("wr1h", [P, P], F32R), sb("wr1l", [P, P], F32R)
        wr2 = sb("wr2", [P, E])
        br1 = sb("br1", [P, 1])
        b1 = sb("b1", [P, JOBS, KC])
        bs2 = sb("bs2", [P, 1])
        be2s = sb("be2s", [2 * E, P])
        be2h, be2l = sb("be2h", [2 * E, P], F32R), sb("be2l", [2 * E, P], F32R)
        sels = sb("sels", [2 * E, E, P])
        sel = sb("sel", [2 * E, E, P], F32R)
        rank = sb("rank", [P, TPB, E])
        ebase, ebase2, mhalf = sb("ebase", [P, TPB, E]), sb("ebase2", [P, TPB]), sb("mhalf", [P, TPB])

        stats, mv = sb("stats", [P, TPB, 6]), sb("mv", [P, TPB, 2])
        veps, rstd = sb("veps", [P, TPB]), sb("rstd", [P, TPB])
        eps, spare = sb("eps", [P, TPB]), sb("spare", [P, 1])
        xn = sb("xn", [P, TPB, P])
        xh, xl = sb("xh", [P, 2, BLK], F32R), sb("xl", [P, 2, BLK], F32R)
        r1 = sb("r1", [P, BLK])
        NRAW = 4
        raw = sb("raw", [P, NRAW, BLK])
        hh, hl = sb("hh", [P, 2, KC, BLK], F32R), sb("hl", [P, 2, KC, BLK], F32R)
        wts = sb("wts", [2 * E, BLK], F32R)
        wbc = sb("wbc", [P, 2, BLK])
        prod = sb("prod", [P, 2, BLK])
        acc, accf = sb("acc", [P, BLK]), sb("accf", [P, BLK])
        g8 = lambda n: sb(n, [P, TPB, E])
        g1 = lambda n: sb(n, [P, TPB])
        lg, sh, ex, gt, eq, cc, oh1, gm, oh2, wsum, wtmp, wall = map(g8, (
            "lg", "sh", "ex", "gt", "eq", "cc", "oh1", "gm", "oh2", "wsum", "wtmp", "wall"))
        mx, sm, rs, top1, cm, top2, dd, tt, t1, wa, wb = map(g1, (
            "mx", "sm", "rs", "top1", "cm", "top2", "dd", "tt", "t1", "wa", "wb"))
        w16 = sb("w16", [P, TPB, 2 * E])

        U = ph.ps("U", [P, 4, BLK])
        Y = ph.ps("Y", [P, 2, BLK])
        R = ph.ps("R", [P, BLK])
        T = ph.ps("T", [P, BLK])

        s_small = sem("small")
        s_wst = [sem(f"wst{i}") for i in range(NST)]
        s_wsp = sem("wsp")
        s_wsc = sem("wsc")
        s_cst = sem("cst")
        s_pre = sem("pre")
        s_mv = sem("mv")
        s_ve = sem("ve")
        s_rstd = sem("rstd")
        s_xn = sem("xn")
        s_xT = sem("xT")
        s_xh, s_xl = sem("xh"), sem("xl")
        s_r1p, s_r1 = sem("r1p"), sem("r1")
        s_lg = sem("lg")
        s_gch = sem("gch")
        s_sh, s_ex = sem("sh"), sem("ex")
        s_dd, s_tt = sem("dd"), sem("tt")
        s_w = sem("w")
        s_wT, s_wTs = sem("wT"), sem("wTs")
        s_bc, s_wbc = sem("bc"), sem("wbc")
        s_up = sem("up")
        s_raw, s_hh = sem("raw"), sem("hh")
        s_hl = sem("hl")
        s_dn = sem("dn")
        s_yc = sem("yc")
        s_acc = sem("acc")
        s_aT, s_x = sem("aT"), sem("x")

        pieces = [(kind, j) for j in range(JOBS) for kind in (0, 1)]

        with nc.Block() as block:
            @block.sync
            def _(sp):
                for dst, src in ((wr1s[:], w["wr1"]), (wr2[:], w["wr2"]), (br1[:], w["br1"]),
                                 (b1[:], w["b1"]), (bs2[:], w["bs2"]), (be2s[:], w["be2"]),
                                 (sels[:], w["route_sel"]), (rank[:], w["rank"])):
                    sp.dma_start(dst, src).then_inc(s_small, 16)
                for n, (kind, j) in enumerate(pieces):
                    if n >= NST:
                        sp.wait_ge(s_wsp, n - NST + 1)
                    src = (w["w1"], w["w2"])[kind][j]
                    sp.dma_start(wst[:, n % NST, :], src).then_inc(s_wst[n % NST], 16)

            @block.tensor
            def _(pe):
                def up(b, par, j):
                    for k in range(KC):
                        n = NUP * b + KC * j + k
                        if k < KC - 1:
                            wait(pe, s_hh, 3 * JOBS * b + 3 * j + k + 1 - 3)
                        else:
                            wait(pe, s_raw, n - 3)
                        c = slice(k * P, (k + 1) * P)
                        pe.matmul(U[:, k, :], w1h[:, j, c], xh[:, par, :], start=True, stop=False)
                        pe.matmul(U[:, k, :], w1l[:, j, c], xh[:, par, :], start=False, stop=False)
                        pe.matmul(U[:, k, :], w1h[:, j, c], xl[:, par, :], start=False, stop=True)\
                          .then_inc(s_up, 1)

                def down(b, par, j):
                    q = (par + j) % 2
                    wait(pe, s_yc, JOBS * b + j - 1)
                    for k in range(KC):
                        wait(pe, s_hl, NUP * b + KC * j + k + 1)
                        c = slice(k * P, (k + 1) * P)
                        pe.matmul(Y[:, q, :], w2h[:, j, c], hh[:, q, k, :], start=(k == 0), stop=False)
                        pe.matmul(Y[:, q, :], w2l[:, j, c], hh[:, q, k, :], start=False, stop=False)
                        last = k == KC - 1 and j < E
                        mm = pe.matmul(Y[:, q, :], w2h[:, j, c], hl[:, q, k, :], start=False, stop=last)
                    if j == E:
                        pe.matmul(Y[:, q, :], be2h[:], wts[:], start=False, stop=False)
                        mm = pe.matmul(Y[:, q, :], be2l[:], wts[:], start=False, stop=True)
                    mm.then_inc(s_dn, 1)

                def norm_T(b):
                    wait(pe, s_xn, b + 1)
                    for t in range(TPB):
                        mm = pe.transpose(T[:, t * P:(t + 1) * P], xn[:, t, :], ident[:])
                    mm.then_inc(s_xT, 1)

                def sum_T(b):
                    wait(pe, s_yc, JOBS * (b + 1))
                    for t in range(TPB):
                        mm = pe.transpose(T[:, t * P:(t + 1) * P], accf[:, t * P:(t + 1) * P], ident[:])
                    mm.then_inc(s_aT, 1)

                def bcast(b, e):
                    wait(pe, s_wbc, E * b + e)
                    pe.matmul(R[:], sel[:, e, :], wts[:], start=True, stop=True).then_inc(s_bc, 1)

                def router(b, par):
                    wait(pe, s_xh, b + 1)
                    wait(pe, s_xl, b + 1)
                    wait(pe, s_wbc, E * b - 6)
                    pe.matmul(R[:], wr1h[:], xh[:, par, :], start=True, stop=False)
                    pe.matmul(R[:], wr1l[:], xh[:, par, :], start=False, stop=False)
                    pe.matmul(R[:], wr1h[:], xl[:, par, :], start=False, stop=True).then_inc(s_r1p, 1)

                def logits(b):
                    wait(pe, s_r1, b + 1)
                    for t in range(TPB):
                        mm = pe.matmul(R[:, t * E:(t + 1) * E], r1[:, t * P:(t + 1) * P], wr2[:],
                                       start=True, stop=True)
                    mm.then_inc(s_lg, 1)

                def run_block(b, par, first=False):
                    if first:
                        pe.wait_ge(s_wsp, 1)
                    up(b, par, 0)
                    if first:
                        pe.wait_ge(s_wsp, len(pieces))
                    up(b, par, 1)
                    down(b, par, 0)
                    if not first:
                        sum_T(b - 1)
                    up(b, par, 2)
                    wait(pe, s_w, b + 1)
                    wait(pe, s_x, b)
                    for t in range(TPB):
                        mm = pe.transpose(T[0:2 * E, t * P:(t + 1) * P], w16[:, t, :], ident[:])
                    mm.then_inc(s_wT, 1)
                    wait(pe, s_wTs, b + 1)
                    bcast(b, 0)
                    norm_T(b + 1)
                    down(b, par, 1)
                    for j in range(3, JOBS):
                        if j == 4:
                            router(b + 1, 1 - par)
                        up(b, par, j)
                        if j == 4:
                            logits(b + 1)
                            down(b, par, j - 1)
                            wait(pe, s_sh, b + 2)
                        bcast(b, j - 2)
                        if j != 4:
                            down(b, par, j - 1)
                    bcast(b, E - 1)
                    down(b, par, E)

                pe.wait_ge(s_pre, 5)
                norm_T(0)
                router(0, 0)
                logits(0)
                run_block(0, 0, first=True)
                run_block(1, 1)
                with pe.Fori(1, NBLK // 2) as i:
                    run_block(i * 2, 0)
                    run_block(i * 2 + 1, 1)
                pe.wait_ge(s_xh, NBLK + 1)
                pe.wait_ge(s_xl, NBLK + 1)
                sum_T(NBLK - 1)

            @block.scalar
            def _(act):
                def split_x(b, par):
                    wait(act, s_xT, b + 1)
                    wait(act, s_up, NUP * (b - 1))
                    act.activation(xh[:, par, :], T[:], ACT.Copy).then_inc(s_xh, 1)

                def bcast(b, e):
                    wait(act, s_bc, E * b + e + 1)
                    wait(act, s_yc, JOBS * b + e - 1 if e >= 2 else JOBS * b)
                    act.activation(wbc[:, e % 2, :], R[:], ACT.Copy).then_inc(s_wbc, 1)

                def router(b):
                    wait(act, s_r1p, b + 1)
                    wait(act, s_lg, b)
                    act.activation(r1[:], R[:], ACT.Relu, bias=br1[:]).then_inc(s_r1, 1)

                def run_block(b, par):
                    for j in range(JOBS):
                        q = (par + j) % 2
                        for k in range(KC):
                            n = NUP * b + KC * j + k
                            wait(act, s_up, n + 1)
                            wait(act, s_hl, n - 3)
                            act.activation(raw[:, k, :], U[:, k, :], ACT.Silu, bias=b1[:, j, k:k + 1])\
                               .then_inc(s_raw, 1)
                            if k < KC - 1:
                                if k == 0:
                                    wait(act, s_dn, JOBS * b + j - 1)
                                act.activation(hh[:, q, k, :], U[:, k, :], ACT.Silu,
                                               bias=b1[:, j, k:k + 1]).then_inc(s_hh, 1)
                        if j == 2:
                            wait(act, s_wT, b + 1)
                            wait(act, s_dn, JOBS * b)
                            act.activation(wts[:], T[0:2 * E, :], ACT.Copy).then_inc(s_wTs, 1)
                        if j >= 2:
                            bcast(b, j - 2)
                        if j == 2:
                            split_x(b + 1, 1 - par)
                        if j == 3:
                            router(b + 1)
                    bcast(b, E - 1)

                act.wait_ge(s_pre, 5)
                split_x(0, 0)
                router(0)
                for n, (kind, j) in enumerate(pieces):
                    act.wait_ge(s_wst[n % NST], 16 * (n // NST + 1))
                    act.activation((w1h, w2h)[kind][:, j, :], wst[:, n % NST, :], ACT.Copy).then_inc(s_wsc, 1)
                run_block(0, 0)
                run_block(1, 1)
                with act.Fori(1, NBLK // 2) as i:
                    run_block(i * 2, 0)
                    run_block(i * 2 + 1, 1)

            @block.vector
            def _(dve):
                def bc(a):
                    return a[:].rearrange("p (t o) -> p t o", o=1).broadcast_to([P, TPB, E])

                def norm(b, ch):
                    last = norm_stats(nc, dve, ch, lambda t: x[:, bass.ds((b * TPB + t) * P, P)], stats, mv, spare)
                    last.then_inc(s_mv, 1)

                def normalize(b):
                    wait(dve, s_rstd, b + 1)
                    wait(dve, s_xT, b)
                    for t in range(TPB):
                        last = dve.tensor_scalar(xn[:, t, :], x[:, bass.ds((b * TPB + t) * P, P)],
                                                 mv[:, t, 0:1], rstd[:, t:t + 1], ALU.subtract, ALU.mult)
                    last.then_inc(s_xn, 1)

                def split_x(b, par):
                    wait(dve, s_xh, b + 1)
                    dve.tensor_tensor(xl[:, par, :], T[:], xh[:, par, :].bitcast(F32), ALU.subtract)\
                       .then_inc(s_xl, 1)

                def gate(b, ch, n):
                    def first_of_equals(of, top, hot, m):
                        if m == 0:
                            return dve.tensor_reduce(top[:], of[:], AX, ALU.max)
                        if m == 1:
                            return dve.tensor_tensor(eq[:], of[:], bc(top), ALU.is_equal)
                        if m == 2:
                            return dve.tensor_tensor(cc[:], eq[:], rank[:], ALU.mult)
                        if m == 3:
                            return dve.tensor_reduce(cm[:], cc[:], AX, ALU.max)
                        return dve.tensor_tensor(hot[:], cc[:], bc(cm), ALU.is_equal)

                    if n == 0:
                        wait(dve, s_lg, b + 1)
                        ins = dve.tensor_copy(lg[:].rearrange("p t e -> p (t e)"), R[:, 0:TPB * E])
                        ch.step(ins)
                        return
                    ch.join()
                    if n == 1:
                        ins = dve.tensor_reduce(mx[:], lg[:], AX, ALU.max)
                    if n == 2:
                        dve.tensor_tensor(sh[:], lg[:], bc(mx), ALU.subtract).then_inc(s_sh, 1)
                        return
                    if n == 3:
                        wait(dve, s_ex, b + 1)
                        ins = dve.tensor_reduce(sm[:], ex[:], AX, ALU.add)
                    if n == 4:
                        ins = dve.reciprocal(rs[:], sm[:])
                    if n == 5:
                        ins = dve.tensor_tensor(gt[:], ex[:], bc(rs), ALU.mult)
                    if 6 <= n <= 10:
                        ins = first_of_equals(gt, top1, oh1, n - 6)
                    if n == 11:
                        ins = dve.scalar_tensor_tensor(gm[:], oh1[:], -2.0, gt[:], ALU.mult, ALU.add)
                    if 12 <= n <= 16:
                        ins = first_of_equals(gm, top2, oh2, n - 12)
                    if n == 17:
                        dve.tensor_tensor(dd[:], top2[:], top1[:], ALU.subtract).then_inc(s_dd, 1)
                        return
                    if n == 18:
                        wait(dve, s_tt, b + 1)
                        ins = dve.tensor_scalar(t1[:], tt[:], 1.0, None, ALU.add)
                    if n == 19:
                        ins = dve.reciprocal(wa[:], t1[:])
                    if n == 20:
                        ch.step(dve.tensor_tensor(wb[:], tt[:], wa[:], ALU.mult))
                        ins = dve.tensor_tensor(wtmp[:], oh1[:], bc(wa), ALU.mult)
                    if n == 21:
                        ins = dve.tensor_tensor(wsum[:], oh2[:], bc(wb), ALU.mult)
                    if n == 22:
                        ins = dve.tensor_tensor(wall[:], wsum[:], wtmp[:], ALU.add)
                    if n == 23:
                        wait(dve, s_wT, b)
                        ins = dve.tensor_copy(w16[:, :, 0:E].bitcast(F32R), wall[:])
                    if n == 24:
                        dve.tensor_tensor(w16[:, :, E:2 * E], wall[:], w16[:, :, 0:E], ALU.subtract)\
                           .then_inc(s_w, 1)
                        return
                    ch.step(ins)

                def update(b):
                    wait(dve, s_aT, b + 1)
                    xb = x[:, bass.ds(b * BLK, BLK)]
                    dve.scalar_tensor_tensor(xb, T[:], 0.5, xb, ALU.mult, ALU.add).then_inc(s_x, 1)

                def take(b, par, e):
                    q = (par + e) % 2
                    wait(dve, s_dn, JOBS * b + e + 1)
                    wait(dve, s_wbc, E * b + e + 1)
                    wait(dve, s_acc, 7 * b + (max(1, e - 2) if e >= 2 else 0))
                    dve.tensor_tensor(prod[:, e % 2, :], Y[:, q, :], wbc[:, e % 2, :], ALU.mult)\
                       .then_inc(s_yc, 1)

                def total(b, par):
                    wait(dve, s_dn, JOBS * (b + 1))
                    wait(dve, s_acc, 7 * (b + 1))
                    dve.scalar_tensor_tensor(accf[:], Y[:, (par + E) % 2, :], bs2[:], acc[:],
                                             ALU.add, ALU.add).then_inc(s_yc, 1)

                def run_block(b, par, first=False):
                    ch = Chain(dve, s_gch, GATED + CHAIN * b)
                    for j in range(JOBS):
                        q = (par + j) % 2
                        for k in range(KC):
                            n = NUP * b + KC * j + k
                            if k < KC - 1:
                                wait(dve, s_hh, 3 * JOBS * b + 3 * j + k + 1)
                            else:
                                wait(dve, s_raw, n + 1)
                                ch.step(dve.tensor_copy(hh[:, q, k, :], raw[:, k, :]))
                                ch.join()
                            if k == 0:
                                wait(dve, s_dn, JOBS * b + j - 1)
                            dve.tensor_tensor(hl[:, q, k, :], raw[:, k, :], hh[:, q, k, :].bitcast(F32),
                                              ALU.subtract).then_inc(s_hl, 1)
                            if j == 4 and k < 3:
                                gate(b + 1, ch, k)
                            if j >= 6:
                                gate(b + 1, ch, 3 + KC * (j - 6) + k)
                            for step in GATE.get((j, k), ()):
                                gate(b, ch, step)
                            if (j, k) == (0, 1) and not first:
                                total(b - 1, 1 - par)
                            if (j, k) == (2, 0) and not first:
                                update(b - 1)
                        if j == 0:
                            norm(b + 1, ch)
                        if j == 1:
                            normalize(b + 1)
                        if j == 2:
                            split_x(b + 1, 1 - par)
                        if j >= 2:
                            take(b, par, j - 2)
                    take(b, par, E - 1)
                    assert ch.n == CHAIN, ch.n

                GATE = {(0, 0): (15,), (0, 1): (16,), (0, 2): (17,), (1, 0): (18, 19), (1, 1): (20, 21),
                        (1, 2): (22, 23), (1, 3): (24,)}
                CHAIN, GATED = JOBS + 1 + 23, 15
                ch = Chain(dve, s_gch)
                norm(0, ch)
                dve.wait_ge(s_small, 16 * 8)
                dve.tensor_copy(wr1h[:], wr1s[:]).then_inc(s_pre, 1)
                dve.tensor_copy(be2h[:], be2s[:]).then_inc(s_pre, 1)
                dve.tensor_copy(sel[:], sels[:]).then_inc(s_pre, 1)
                dve.wait_ge(s_pre, 2)
                dve.tensor_tensor(wr1l[:], wr1s[:], wr1h[:].bitcast(F32), ALU.subtract).then_inc(s_pre, 1)
                dve.tensor_tensor(be2l[:], be2s[:], be2h[:].bitcast(F32), ALU.subtract).then_inc(s_pre, 1)
                normalize(0)
                split_x(0, 0)
                for n, (kind, j) in enumerate(pieces):
                    dve.wait_ge(s_wsc, n + 1)
                    dve.tensor_tensor((w1l, w2l)[kind][:, j, :], wst[:, n % NST, :],
                                      (w1h, w2h)[kind][:, j, :].bitcast(F32), ALU.subtract).then_inc(s_wsp, 1)
                for n in range(15):
                    gate(0, ch, n)
                assert ch.n == GATED
                run_block(0, 0, first=True)
                run_block(1, 1)
                with dve.Fori(1, NBLK // 2) as i:
                    run_block(i * 2, 0)
                    run_block(i * 2 + 1, 1)
                total(NBLK - 1, 1)
                update(NBLK - 1)

            @block.gpsimd
            def _(pool):
                def rstd_of(b):
                    wait(pool, s_mv, b + 1)
                    pool.tensor_tensor(veps[:], mv[:, :, 1], eps[:], ALU.add).then_inc(s_ve, 1)
                    wait(pool, s_ve, b + 1)
                    wait(pool, s_xn, b)
                    pool.tensor_tensor(rstd[:], veps[:], mhalf[:], ALU.pow).then_inc(s_rstd, 1)

                def exps(b):
                    wait(pool, s_sh, b + 1)
                    pool.tensor_tensor(ex[:], ebase[:], sh[:], ALU.pow).then_inc(s_ex, 1)

                def exp_second(b):
                    wait(pool, s_dd, b + 1)
                    pool.tensor_tensor(tt[:], ebase2[:], dd[:], ALU.pow).then_inc(s_tt, 1)

                def run_block(b, par):
                    exp_second(b)
                    rstd_of(b + 1)
                    for e in range(1, E):
                        if e == 3:
                            exps(b + 1)
                        wait(pool, s_yc, JOBS * b + e + 1)
                        if e > 1:
                            wait(pool, s_acc, 7 * b + e - 1)
                        src = prod[:, 0, :] if e == 1 else acc[:]
                        pool.tensor_tensor(acc[:], src, prod[:, e % 2, :], ALU.add).then_inc(s_acc, 1)

                pool.memset(ebase[:], float(np.exp(1.0)))
                pool.memset(ebase2[:], float(np.exp(0.5)))
                pool.memset(mhalf[:], -0.5).then_inc(s_cst, 1)
                pool.memset(eps[:], EPS).then_inc(s_cst, 1)
                pool.wait_ge(s_cst, 2)
                rstd_of(0)
                exps(0)
                run_block(0, 0)
                run_block(1, 1)
                with pool.Fori(1, NBLK // 2) as i:
                    run_block(i * 2, 0)
                    run_block(i * 2 + 1, 1)
        ph.clear()


def ternary_ffn(nc, tag, x, ident, w):
    KC = 4
    NPAIR = NBLK // 2
    NHID = 6 * KC
    NPROD = 8 * KC
    with ExitStack() as ctx:
        ph = Phase(nc, ctx, tag)
        sb, sem = ph.sb, ph.sem
        NW = 2 + KC + KC + 1
        wh, wl = sb("wh", [P, NW, 512], F32R), sb("wl", [P, NW, 512], F32R)
        wst = sb("wst", [P, 4, 512])
        scal = sb("scal", [P, 4 * KC + 1])
        mhalf = sb("mhalf", [P, TPB])
        stats, mv = sb("stats", [P, TPB, 6]), sb("mv", [P, TPB, 2])
        veps, rstd = sb("veps", [P, TPB]), sb("rstd", [P, TPB])
        eps, spare = sb("eps", [P, TPB]), sb("spare", [P, 1])
        xn = sb("xn", [P, TPB, P])
        xh, xl = sb("xh", [P, 2, BLK], F32R), sb("xl", [P, 2, BLK], F32R)
        raw, hf = sb("raw", [P, KC, BLK]), sb("hf", [P, KC, BLK])
        hh, hl = sb("hh", [P, 2, 2, KC, BLK], F32R), sb("hl", [P, 2, 2, KC, BLK], F32R)
        outT = sb("outT", [P, 2, BLK])

        U = ph.ps("U", [P, 4, BLK])
        Y = ph.ps("Y", [P, 2, BLK])
        T = ph.ps("T", [P, BLK])

        s_small = sem("small")
        s_wst = [sem(f"wst{i}") for i in range(4)]
        s_wsc, s_wsp = sem("wsc"), sem("wsp")
        s_cst = sem("cst")
        s_gch = sem("gch")
        s_mv, s_ve, s_rstd, s_xn = sem("mv"), sem("ve"), sem("rstd"), sem("xn")
        s_xT, s_xh, s_xl = sem("xT"), sem("xh"), sem("xl")
        s_up = sem("up")
        s_ua, s_ud = sem("ua"), sem("ud")
        s_raw = sem("raw")
        s_hh, s_hl = sem("hh"), sem("hl")
        s_y, s_yc = sem("y"), sem("yc")
        s_aT, s_x = sem("aT"), sem("x")

        order = [(s, a) for s in range(3) for a in range(2)]
        readers = []
        for s, a in order:
            for k in range(KC):
                readers += ["act", "dve"] if s == 0 else ["act"]
        first_prod = {}
        n = 0
        for s, a in order:
            first_prod[s, a] = n
            n += 2 * KC if s == 0 else KC
        ACT_READS, DVE_READS = readers.count("act"), readers.count("dve")

        def hid(s, a, k):
            return (2 * s + a) * KC + k

        def bank_free(eng, i, n):
            m = n - 4
            if m < 0:
                i, m = i - 1, m + NPROD
            who = readers[m]
            count = readers[:m + 1].count(who)
            if who == "act":
                wait(eng, s_ua, i * ACT_READS + count)
            else:
                wait(eng, s_ud, i * DVE_READS + count)

        with nc.Block() as block:
            @block.sync
            def _(sp):
                sp.dma_start(scal[:], w["scales"]).then_inc(s_small, 16)
                for n in range(NW):
                    if n >= 4:
                        sp.wait_ge(s_wsp, n - 3)
                    sp.dma_start(wst[:, n % 4, :], w["w"][n]).then_inc(s_wst[n % 4], 16)

            @block.tensor
            def _(pe):
                def passes(out, piece, c, a, rhs_h, rhs_l, start, stop):
                    c = slice(c * P, (c + 1) * P)
                    pe.matmul(out, wh[:, piece, c], rhs_h, start=start, stop=False)
                    pe.matmul(out, wl[:, piece, c], rhs_h, start=False, stop=False)
                    return pe.matmul(out, wh[:, piece, c], rhs_l, start=False, stop=stop)

                def stage(i, s, a):
                    if s == 0:
                        wait(pe, s_xh, 2 * i + a + 1)
                        wait(pe, s_xl, 2 * i + a + 1)
                    for k in range(KC):
                        if s == 0:
                            for v in range(2):
                                n = first_prod[s, a] + 2 * k + v
                                bank_free(pe, i, n)
                                passes(U[:, n % 4, :], v, k, a, xh[:, a, :], xl[:, a, :], True, True)\
                                    .then_inc(s_up, 1)
                        else:
                            n = first_prod[s, a] + k
                            bank_free(pe, i, n)
                            src = (s + 1) % 2
                            for c in range(KC):
                                wait(pe, s_hl, i * NHID + hid(s - 1, a, c) + 1)
                                mm = passes(U[:, n % 4, :], 2 + KC * (s - 1) + c, k, a, hh[:, a, src, c, :],
                                            hl[:, a, src, c, :], c == 0, c == KC - 1)
                            mm.then_inc(s_up, 1)

                def output(i, a):
                    wait(pe, s_yc, 2 * (i - 1) + a + 1)
                    for c in range(KC):
                        wait(pe, s_hl, i * NHID + hid(2, a, c) + 1)
                        mm = passes(Y[:, a, :], NW - 1, c, a, hh[:, a, 0, c, :], hl[:, a, 0, c, :],
                                    c == 0, c == KC - 1)
                    mm.then_inc(s_y, 1)

                def norm_T(i, a):
                    wait(pe, s_xn, 2 * i + a + 1)
                    if a == 0:
                        wait(pe, s_x, 2 * (i - 1))
                    else:
                        wait(pe, s_xl, 2 * i + 1)
                    for t in range(TPB):
                        mm = pe.transpose(T[:, t * P:(t + 1) * P], xn[:, t, :], ident[:])
                    mm.then_inc(s_xT, 1)

                def sum_T(i, a):
                    wait(pe, s_yc, 2 * i + a + 1)
                    if a == 0:
                        wait(pe, s_xl, 2 * (i + 1) + 2)
                    else:
                        wait(pe, s_x, 2 * i + 1)
                    for t in range(TPB):
                        mm = pe.transpose(T[:, t * P:(t + 1) * P], outT[:, a, t * P:(t + 1) * P], ident[:])
                    mm.then_inc(s_aT, 1)

                def pair(i, first=False):
                    for a in range(2):
                        if first and a == 0:
                            pe.wait_ge(s_wsp, 2)
                        stage(i, 0, a)
                        if not first:
                            sum_T(i - 1, a)
                    if first:
                        pe.wait_ge(s_wsp, NW)
                    for a in range(2):
                        stage(i, 1, a)
                        norm_T(i + 1, a)
                    stage(i, 2, 0)
                    stage(i, 2, 1)
                    output(i, 0)
                    output(i, 1)

                norm_T(0, 0)
                norm_T(0, 1)
                pair(0, first=True)
                with pe.Fori(1, NPAIR) as i:
                    pair(i)
                sum_T(NPAIR - 1, 0)
                sum_T(NPAIR - 1, 1)

            @block.scalar
            def _(act):
                def split_x(i, a):
                    wait(act, s_xT, 2 * i + a + 1)
                    wait(act, s_up, (i - 1) * NPROD + first_prod[0, a] + 2 * KC)
                    act.activation(xh[:, a, :], T[:], ACT.Copy).then_inc(s_xh, 1)

                def high(i, a, k):
                    wait(act, s_ud, i * DVE_READS + KC * a + k + 1)
                    act.activation(hh[:, a, 0, k, :], hf[:, k, :], ACT.Copy).then_inc(s_hh, 1)

                def stage(i, s, a):
                    for k in range(KC):
                        h = hid(s, a, k)
                        n = first_prod[s, a] + (2 * k if s == 0 else k)
                        sc = scal[:, (0, 2 * KC, 3 * KC)[s] + k:(0, 2 * KC, 3 * KC)[s] + k + 1]
                        wait(act, s_up, i * NPROD + n + 1)
                        wait(act, s_hl, i * NHID + h - 3)
                        if s == 0:
                            ins = act.activation(raw[:, k, :], U[:, n % 4, :], ACT.Silu, scale=sc)
                            ins.then_inc(s_ua, 1)
                            if k:
                                high(i, a, k - 1)
                        else:
                            act.activation(raw[:, k, :], U[:, n % 4, :], ACT.Gelu, scale=sc).then_inc(s_raw, 1)
                            act.activation(hh[:, a, s % 2, k, :], U[:, n % 4, :], ACT.Gelu, scale=sc)\
                               .then_inc(s_ua, 1)
                    if s == 0:
                        high(i, a, KC - 1)

                def output(i, a):
                    wait(act, s_y, 2 * i + a + 1)
                    wait(act, s_aT, 2 * (i - 1) + a + 1)
                    act.activation(outT[:, a, :], Y[:, a, :], ACT.Copy, scale=scal[:, 4 * KC:4 * KC + 1])\
                       .then_inc(s_yc, 1)

                def pair(i):
                    for a in range(2):
                        stage(i, 0, a)
                    for a in range(2):
                        stage(i, 1, a)
                        split_x(i + 1, a)
                    stage(i, 2, 0)
                    stage(i, 2, 1)
                    output(i, 0)
                    output(i, 1)

                split_x(0, 0)
                split_x(0, 1)
                for n in range(NW):
                    act.wait_ge(s_wst[n % 4], 16 * (n // 4 + 1))
                    act.activation(wh[:, n, :], wst[:, n % 4, :], ACT.Copy).then_inc(s_wsc, 1)
                act.wait_ge(s_small, 16)
                pair(0)
                with act.Fori(1, NPAIR) as i:
                    pair(i)

            @block.vector
            def _(dve):
                def norm(i, a, ch):
                    b = 2 * i + a
                    norm_stats(nc, dve, ch, lambda t: x[:, bass.ds((b * TPB + t) * P, P)], stats, mv, spare)\
                        .then_inc(s_mv, 1)
                    wait(dve, s_rstd, b + 1)
                    wait(dve, s_xT, b)
                    for t in range(TPB):
                        last = dve.tensor_scalar(xn[:, t, :], x[:, bass.ds((b * TPB + t) * P, P)],
                                                 mv[:, t, 0:1], rstd[:, t:t + 1], ALU.subtract, ALU.mult)
                    last.then_inc(s_xn, 1)

                def split_x(i, a):
                    wait(dve, s_xh, 2 * i + a + 1)
                    dve.tensor_tensor(xl[:, a, :], T[:], xh[:, a, :].bitcast(F32), ALU.subtract)\
                       .then_inc(s_xl, 1)

                def stage(i, s, a):
                    for k in range(KC):
                        h = hid(s, a, k)
                        if s == 0:
                            n = first_prod[s, a] + 2 * k
                            wait(dve, s_ua, i * ACT_READS + KC * a + k + 1)
                            wait(dve, s_up, i * NPROD + n + 2)
                            wait(dve, s_hl, i * NHID + h - 3)
                            dve.scalar_tensor_tensor(hf[:, k, :], U[:, (n + 1) % 4, :],
                                                     scal[:, KC + k:KC + k + 1], raw[:, k, :],
                                                     ALU.mult, ALU.mult).then_inc(s_ud, 1)
                            if k:
                                low(i, s, a, k - 1)
                        else:
                            low(i, s, a, k)
                    if s == 0:
                        low(i, s, a, KC - 1)

                def low(i, s, a, k):
                    if s == 0:
                        wait(dve, s_hh, i * 2 * KC + KC * a + k + 1)
                    else:
                        wait(dve, s_ua, i * ACT_READS + 2 * KC + (2 * (s - 1) + a) * KC + k + 1)
                    src = hf if s == 0 else raw
                    dve.tensor_tensor(hl[:, a, s % 2, k, :], src[:, k, :], hh[:, a, s % 2, k, :].bitcast(F32),
                                      ALU.subtract).then_inc(s_hl, 1)

                def update(i, a):
                    wait(dve, s_aT, 2 * i + a + 1)
                    xb = x[:, bass.ds((2 * i + a) * BLK, BLK)]
                    dve.scalar_tensor_tensor(xb, T[:], 0.5, xb, ALU.mult, ALU.add).then_inc(s_x, 1)

                def pair(i, first=False):
                    ch = Chain(dve, s_gch, 2 + 2 * i)
                    for a in range(2):
                        stage(i, 0, a)
                        if not first:
                            update(i - 1, a)
                    for a in range(2):
                        norm(i + 1, a, ch)
                        stage(i, 1, a)
                        split_x(i + 1, a)
                    stage(i, 2, 0)
                    stage(i, 2, 1)

                ch = Chain(dve, s_gch)
                norm(0, 0, ch)
                split_x(0, 0)
                norm(0, 1, ch)
                split_x(0, 1)
                for n in range(NW):
                    dve.wait_ge(s_wsc, n + 1)
                    dve.tensor_tensor(wl[:, n, :], wst[:, n % 4, :], wh[:, n, :].bitcast(F32), ALU.subtract)\
                       .then_inc(s_wsp, 1)
                dve.wait_ge(s_small, 16)
                pair(0, first=True)
                with dve.Fori(1, NPAIR) as i:
                    pair(i)
                update(NPAIR - 1, 0)
                update(NPAIR - 1, 1)

            @block.gpsimd
            def _(pool):
                def rstd_of(b):
                    wait(pool, s_mv, b + 1)
                    pool.tensor_tensor(veps[:], mv[:, :, 1], eps[:], ALU.add).then_inc(s_ve, 1)
                    wait(pool, s_ve, b + 1)
                    wait(pool, s_xn, b)
                    pool.tensor_tensor(rstd[:], veps[:], mhalf[:], ALU.pow).then_inc(s_rstd, 1)

                pool.memset(mhalf[:], -0.5).then_inc(s_cst, 1)
                pool.memset(eps[:], EPS).then_inc(s_cst, 1)
                pool.wait_ge(s_cst, 2)
                rstd_of(0)
                rstd_of(1)
                with pool.Fori(1, NPAIR + 1) as i:
                    rstd_of(2 * i)
                    rstd_of(2 * i + 1)
        ph.clear()
def mamba(nc, tag, x, ident, w):
    NS = 16
    DBC = 2 * 2 * NS
    DBL = DBC + 8
    HALF = 2
    NCH = SEQ // BLK
    TPS = SEQ // P
    PADW = 3
    PAIRS = 2 * NS * NCH
    UNITS = PAIRS * HALF
    PRE = 2 + 8
    with ExitStack() as ctx:
        ph = Phase(nc, ctx, tag)
        sb, sem = ph.sb, ph.sem
        wi = sb("wi", [P, 512])
        wih, wil = sb("wih", [P, 512], F32R), sb("wil", [P, 512], F32R)
        convw = sb("convw", [P, 2, HALF, 4])
        vecs = sb("vecs", [P, 3, 2, HALF])
        xpw = sb("xpw", [P, 2, HALF, DBL])
        dtw = sb("dtw", [DBL, 2, HALF, P])
        alog, aneg = sb("alog", [P, 2, HALF, NS]), sb("aneg", [P, 2, HALF, NS])
        wo = sb("wo", [P, HALF, P])
        sels = sb("sels", [DBC, 4, P])
        sel = sb("sel", [DBC, 2 * NS, P], F32R)
        mhalf, one = sb("mhalf", [P, TILES]), sb("one", [P, 1])
        stats, mv = sb("stats", [P, TILES, 6]), sb("mv", [P, TILES, 2])
        veps, rstd = sb("veps", [P, TILES]), sb("rstd", [P, TILES])
        xn = sb("xn", [P, TPS, P])
        xh, xl = sb("xh", [P, SEQ], F32R), sb("xl", [P, SEQ], F32R)
        xpad = sb("xpad", [P, HALF, SEQ + 2 * PADW])
        zs = sb("zs", [P, HALF, SEQ])
        xs = sb("xs", [P, 2, HALF, SEQ])
        dbl = sb("dbl", [DBL, 2, SEQ])
        bcs = sb("bcs", [DBC, 2, SEQ], F32R)
        dt, u = sb("dt", [P, 2, HALF, SEQ]), sb("u", [P, 2, HALF, SEQ])
        RING = 4
        dA, bx = sb("dA", [P, RING, BLK]), sb("bx", [P, RING, BLK])
        H, hc = sb("H", [P, RING, BLK]), sb("hc", [P, RING, BLK])
        cb = sb("cb", [P, RING, BLK])
        two = lambda t: t[:].rearrange("p (a b) c -> p a (b c)", a=2)
        ab, ee = two(dA)[:, 0, :], two(dA)[:, 1, :]
        ln, uu = two(bx)[:, 0, :], two(bx)[:, 1, :]
        rl, cv = two(H), two(hc)
        ys = sb("ys", [P, HALF, NCH, BLK])

        Y = ph.ps("Y", [P, 4, BLK])
        Bp = ph.ps("Bp", [P, 2, BLK])
        Cp = ph.ps("Cp", [P, BLK])
        O = ph.ps("O", [P, BLK])

        s_ld, s_sel = sem("ld"), sem("sel")
        s_cst, s_aexp, s_pre = sem("cst"), sem("aexp"), sem("pre")
        s_mv, s_ve, s_rstd = sem("mv"), sem("ve"), sem("rstd")
        s_gch = sem("gch")
        s_xn, s_pp = sem("xn"), sem("pp")
        s_xh, s_xl = sem("xh"), sem("xl")
        s_ip = sem("ip")
        s_cv, s_xs = sem("cv"), sem("xs")
        s_dbl, s_bcs = sem("dbl"), sem("bcs")
        s_ab, s_rl, s_ee, s_ln = sem("ab"), sem("rl"), sem("ee"), sem("ln")
        s_dt = sem("dt")
        s_B, s_C, s_cb = sem("B"), sem("C"), sem("cb")
        s_dA, s_bx, s_scan = sem("dA"), sem("bx"), sem("scan")
        s_hc, s_y = sem("hc"), sem("y")
        s_g = sem("g")
        s_o, s_x = sem("o"), sem("x")

        LOADS = ((wi[:], w["in_proj"]), (convw[:], w["conv_w"]), (vecs[:], w["vecs"]),
                 (xpw[:], w["x_proj"]), (dtw[:], w["dt_proj"]), (alog[:], w["A_log"]),
                 (wo[:], w["out_proj"]))
        NSEL = 2 * NS // 4
        units = []
        for d in range(2):
            for n in range(NS):
                for c in (range(NCH) if d == 0 else range(NCH - 1, -1, -1)):
                    for h in range(HALF):
                        units.append((d, n, c, h))

        def chunk(c):
            return slice(c * BLK, (c + 1) * BLK)

        with nc.Block() as block:
            @block.sync
            def _(sp):
                for dst, src in LOADS:
                    sp.dma_start(dst, src).then_inc(s_ld, 16)
                for k in range(NSEL):
                    if k:
                        sp.wait_ge(s_pre, k)
                    sp.dma_start(sels[:], w["bc_sel"][:, 4 * k:4 * k + 4, :]).then_inc(s_sel, 16)

            @block.tensor
            def _(pe):
                def xproj(i, d):
                    for c in range(NCH):
                        n = PRE + 6 * d + c
                        if c == 0:
                            wait(pe, s_xs, 4 * i + 2 * d + 2)
                            if d:
                                wait(pe, s_rl, 4 * i + 1)
                        for h in range(HALF):
                            mm = pe.matmul(Y[0:DBL, n % 4, :], xpw[:, d, h, :], xs[:, d, h, chunk(c)],
                                           start=h == 0, stop=h == 1)
                        mm.then_inc(s_pp, 1)

                def dtproj(i, d):
                    for h in range(HALF):
                        for c in range(NCH):
                            n = PRE + 6 * d + 2 + 2 * h + c
                            if c == 0:
                                wait(pe, s_dbl, 4 * i + 2 * d + 2)
                                if (d, h) == (1, 0):
                                    wait(pe, s_rl, 4 * i + 2)
                            pe.matmul(Y[:, n % 4, :], dtw[:, d, h, :], dbl[:, d, chunk(c)],
                                      start=True, stop=True).then_inc(s_pp, 1)

                def rows(i, q):
                    d, n, c, _ = units[2 * q]
                    Q = i * PAIRS + q
                    wait(pe, s_bx, 2 * (Q - 1))
                    pe.matmul(Bp[:, q % 2, :], sel[:, n, :], bcs[:, d, chunk(c)], start=True, stop=True)\
                      .then_inc(s_B, 1)
                    wait(pe, s_cb, Q)
                    pe.matmul(Cp[:], sel[:, NS + n, :], bcs[:, d, chunk(c)], start=True, stop=True)\
                      .then_inc(s_C, 1)

                def batch(i):
                    wait(pe, s_xn, i + 1)
                    for c in range(NCH):
                        for t in range(TPB):
                            mm = pe.transpose(Y[:, c, t * P:(t + 1) * P], xn[:, TPB * c + t, :], ident[:])
                        mm.then_inc(s_pp, 1)
                    for m in range(4):
                        for c in range(NCH):
                            n = 2 + 2 * m + c
                            wait(pe, s_xl, 2 * i + 2)
                            if n >= 6:
                                wait(pe, s_ip, 8 * i + n - 5)
                            f = slice(m * P, (m + 1) * P)
                            pe.matmul(Y[:, n % 4, :], wih[:, f], xh[:, chunk(c)], start=True, stop=False)
                            pe.matmul(Y[:, n % 4, :], wil[:, f], xh[:, chunk(c)], start=False, stop=False)
                            pe.matmul(Y[:, n % 4, :], wih[:, f], xl[:, chunk(c)], start=False, stop=True)\
                              .then_inc(s_pp, 1)
                    wait(pe, s_ip, 8 * i + 8)
                    for d in range(2):
                        xproj(i, d)
                        dtproj(i, d)
                    wait(pe, s_bcs, 2 * i + 2)
                    rows(i, 0)
                    rows(i, 1)
                    for q in range(PAIRS):
                        if q + 2 < PAIRS:
                            rows(i, q + 2)
                        for h in range(HALF):
                            g = 2 * q + h
                            d, n, c, _ = units[g]
                            wait(pe, s_hc, i * UNITS + g + 1)
                            pe.matmul(Y[:, 2 * c + h, :], ident[:], hc[:, g % RING, :],
                                      start=d == 0 and n == 0, stop=d == 1 and n == NS - 1).then_inc(s_y, 1)
                    for c in range(NCH):
                        if c:
                            wait(pe, s_x, NCH * i + c)
                        wait(pe, s_g, 4 * i + 2 * c + 2)
                        for t in range(TPB):
                            for h in range(HALF):
                                mm = pe.matmul(O[:, t * P:(t + 1) * P], ys[:, h, c, t * P:(t + 1) * P],
                                               wo[:, h, :], start=h == 0, stop=h == 1)
                        mm.then_inc(s_o, 1)

                pe.wait_ge(s_pre, NSEL + 2)
                batch(0)
                with pe.Fori(1, NBATCH) as i:
                    batch(i)

            @block.scalar
            def _(act):
                nc.scalar.preload_act_table_set("natural_log_exp_and_others")
                act.wait_ge(s_ld, 16 * len(LOADS))
                act.activation(aneg[:], alog[:], ACT.Exp).then_inc(s_aexp, 1)
                act.activation(wih[:], wi[:], ACT.Copy).then_inc(s_aexp, 1)
                act.wait_ge(s_cst, 3)

                def batch(i):
                    base = 22 * i
                    nc.scalar.preload_act_table_set("silu_and_others")
                    for c in range(NCH):
                        wait(act, s_pp, base + c + 1)
                        act.activation(xh[:, chunk(c)], Y[:, c, :], ACT.Copy).then_inc(s_xh, 1)
                    for m in range(4):
                        for c in range(NCH):
                            n = 2 + 2 * m + c
                            wait(act, s_pp, base + n + 1)
                            if m < 2:
                                act.activation(xpad[:, m, PADW + c * BLK:PADW + (c + 1) * BLK], Y[:, n % 4, :],
                                               ACT.Copy).then_inc(s_ip, 1)
                            else:
                                act.activation(zs[:, m - 2, chunk(c)], Y[:, n % 4, :], ACT.Silu)\
                                   .then_inc(s_ip, 1)
                    for k in range(4):
                        d, h = k // 2, k % 2
                        wait(act, s_cv, 4 * i + k + 1)
                        act.activation(xs[:, d, h, :], cv[:, k % 2, :], ACT.Silu, bias=vecs[:, 0, d, h:h + 1])\
                           .then_inc(s_xs, 1)
                    nc.scalar.preload_act_table_set("natural_log_exp_and_others")
                    for d in range(2):
                        for c in range(NCH):
                            n = PRE + 6 * d + c
                            wait(act, s_pp, base + n + 1)
                            act.activation(dbl[:, d, chunk(c)], Y[0:DBL, n % 4, :], ACT.Copy).then_inc(s_dbl, 1)
                        for h in range(HALF):
                            k = 2 * d + h
                            n = PRE + 6 * d + 2 + 2 * h
                            src = Y[:, n % 4:n % 4 + 2, :].rearrange("p a b -> p (a b)")
                            b = vecs[:, 1, d, h:h + 1]
                            wait(act, s_pp, base + n + 2)
                            wait(act, s_ee, 4 * i + k)
                            act.activation(ab, src, ACT.Abs, bias=b).then_inc(s_ab, 1)
                            wait(act, s_dt, 4 * i + k - 1)
                            act.activation(rl[:, k % 2, :], src, ACT.Relu, bias=b).then_inc(s_rl, 1)
                            wait(act, s_ab, 4 * i + k + 1)
                            wait(act, s_dt, 4 * i + k)
                            act.activation(ee, ab, ACT.Exp, scale=-1.0).then_inc(s_ee, 1)
                            wait(act, s_ee, 4 * i + k + 1)
                            act.activation(ln, ee, ACT.Ln, bias=one[:]).then_inc(s_ln, 1)
                    for g in range(UNITS):
                        d, n, c, h = units[g]
                        G, Q = i * UNITS + g, i * PAIRS + g // 2
                        if h == 0:
                            wait(act, s_C, Q + 1)
                            wait(act, s_hc, 2 * (Q - RING) + 2)
                            act.activation(cb[:, (g // 2) % RING, :], Cp[:], ACT.Copy).then_inc(s_cb, 1)
                        if g == 0:
                            wait(act, s_dt, 4 * i + 4)
                        wait(act, s_scan, G - RING + 1)
                        act.activation(dA[:, g % RING, :], dt[:, d, h, chunk(c)], ACT.Exp,
                                       scale=aneg[:, d, h, n:n + 1]).then_inc(s_dA, 1)

                batch(0)
                with act.Fori(1, NBATCH) as i:
                    batch(i)

            @block.vector
            def _(dve):
                dve.wait_ge(s_cst, 3)
                ch = Chain(dve, s_gch)
                for t in range(TILES):
                    last = dve.bn_stats(stats[:, t, :], x[:, t * P:(t + 1) * P])
                ch.step(last)
                ch.join()
                for t in range(TILES):
                    last = dve.bn_aggr(mv[:, t, :], stats[:, t, :])
                last.then_inc(s_mv, 1)
                dve.wait_ge(s_aexp, 2)
                for k in range(NSEL):
                    dve.wait_ge(s_sel, 16 * (k + 1))
                    dve.tensor_copy(sel[:, 4 * k:4 * k + 4, :], sels[:]).then_inc(s_pre, 1)
                dve.tensor_scalar(aneg[:], aneg[:], -1.0, None, ALU.mult).then_inc(s_pre, 1)
                dve.tensor_tensor(wil[:], wi[:], wih[:].bitcast(F32), ALU.subtract).then_inc(s_pre, 1)
                dve.wait_ge(s_rstd, 1)

                CONV, SPLIT, SOFT, GATE = 3, 1, 4, 2
                PER = 4 * CONV + 2 * SPLIT + 4 * SOFT + 4 * GATE

                def batch(i):
                    ch = Chain(dve, s_gch, 1 + PER * i)
                    for t in range(TPS):
                        last = dve.tensor_scalar(xn[:, t, :], x[:, bass.ds((i * TPS + t) * P, P)],
                                                 mv[:, bass.ds(i * TPS + t, 1), 0:1].rearrange("p a b -> p (a b)"),
                                                 rstd[:, bass.ds(i * TPS + t, 1)], ALU.subtract, ALU.mult)
                    last.then_inc(s_xn, 1)
                    for c in range(NCH):
                        wait(dve, s_xh, 2 * i + c + 1)
                        dve.tensor_tensor(xl[:, chunk(c)], Y[:, c, :], xh[:, chunk(c)].bitcast(F32),
                                          ALU.subtract).then_inc(s_xl, 1)
                    for k in range(4):
                        d, h = k // 2, k % 2
                        wait(dve, s_ip, 8 * i + 2 * h + 2)
                        wait(dve, s_xs, 4 * i + k - 1)
                        for s in range(4):
                            off = PADW - s if d == 0 else PADW + s
                            src = xpad[:, h, off:off + SEQ]
                            tap = convw[:, d, h, 3 - s:4 - s]
                            if s == 0:
                                ins = dve.tensor_scalar(cv[:, k % 2, :], src, tap, None, ALU.mult)
                            else:
                                ins = dve.scalar_tensor_tensor(cv[:, k % 2, :], src, tap, cv[:, k % 2, :],
                                                               ALU.mult, ALU.add)
                            if s < 3:
                                ch.step(ins)
                                ch.join()
                            else:
                                ins.then_inc(s_cv, 1)
                    for d in range(2):
                        wait(dve, s_dbl, 4 * i + 2 * d + 2)
                        ch.step(dve.tensor_copy(bcs[:, d, :], dbl[0:DBC, d, :]))
                        ch.join()
                        dve.tensor_tensor(bcs[32:64, d, :], dbl[32:64, d, :],
                                          bcs[32:64, d, :].bitcast(F32), ALU.subtract).then_inc(s_bcs, 1)
                        for h in range(HALF):
                            k = 2 * d + h
                            wait(dve, s_ee, 4 * i + k + 1)
                            ch.step(dve.tensor_scalar(uu, ee, 1.0, None, ALU.add))
                            ch.join()
                            ch.step(dve.scalar_tensor_tensor(uu, uu, 1.0, ee, ALU.subtract,
                                                             ALU.subtract))
                            ch.join()
                            wait(dve, s_ln, 4 * i + k + 1)
                            ch.step(dve.tensor_tensor(uu, ln, uu, ALU.subtract))
                            ch.join()
                            ch.step(dve.tensor_tensor(dt[:, d, h, :], uu, rl[:, k % 2, :], ALU.add))
                            ch.join()
                            dve.tensor_tensor(u[:, d, h, :], dt[:, d, h, :], xs[:, d, h, :], ALU.mult)\
                               .then_inc(s_dt, 1)
                    wait(dve, s_dt, 4 * i + 4)
                    for g in range(UNITS):
                        d, n, c, h = units[g]
                        G, Q = i * UNITS + g, i * PAIRS + g // 2
                        wait(dve, s_B, Q + 1)
                        dve.tensor_tensor(bx[:, g % RING, :], u[:, d, h, chunk(c)], Bp[:, (g // 2) % 2, :],
                                          ALU.mult).then_inc(s_bx, 1)
                        if g:
                            scan(i, g - 1)
                    scan(i, UNITS - 1)
                    for k in range(4):
                        c, h = k // 2, k % 2
                        if k == 0:
                            wait(dve, s_y, (i + 1) * UNITS)
                        ch.step(dve.scalar_tensor_tensor(ys[:, h, c, :], xs[:, 0, h, chunk(c)],
                                                         vecs[:, 2, 0, h:h + 1], Y[:, 2 * c + h, :],
                                                         ALU.mult, ALU.add))
                        ch.join()
                        ch.step(dve.scalar_tensor_tensor(ys[:, h, c, :], xs[:, 1, h, chunk(c)],
                                                         vecs[:, 2, 1, h:h + 1], ys[:, h, c, :],
                                                         ALU.mult, ALU.add))
                        ch.join()
                        dve.tensor_tensor(ys[:, h, c, :], ys[:, h, c, :], zs[:, h, chunk(c)], ALU.mult)\
                           .then_inc(s_g, 1)
                    for c in range(NCH):
                        wait(dve, s_o, NCH * i + c + 1)
                        xb = x[:, bass.ds(i * SEQ + c * BLK, BLK)]
                        dve.tensor_tensor(xb, xb, O[:], ALU.add).then_inc(s_x, 1)

                def scan(i, g):
                    d, n, c, h = units[g]
                    G = i * UNITS + g
                    wait(dve, s_dA, G + 1)
                    wait(dve, s_bx, G + 1)
                    wait(dve, s_hc, G - RING + 1)
                    s = g % RING
                    if c == (0 if d == 0 else NCH - 1):
                        init = 0.0
                    else:
                        wait(dve, s_scan, G - 1)
                        prev = (g - 2) % RING
                        init = H[:, prev, BLK - 1:BLK] if d == 0 else H[:, prev, 0:1]
                    if d == 0:
                        dve.tensor_tensor_scan(H[:, s, :], dA[:, s, :], bx[:, s, :], init, ALU.mult, ALU.add)\
                           .then_inc(s_scan, 1)
                    else:
                        dve.tensor_tensor_scan(H[:, s, ::-1], dA[:, s, ::-1], bx[:, s, ::-1], init,
                                               ALU.mult, ALU.add).then_inc(s_scan, 1)

                batch(0)
                with dve.Fori(1, NBATCH) as i:
                    batch(i)

            @block.gpsimd
            def _(pool):
                pool.memset(mhalf[:], -0.5).then_inc(s_cst, 1)
                pool.memset(one[:], 1.0).then_inc(s_cst, 1)
                pool.memset(xpad[:], 0.0).then_inc(s_cst, 1)
                pool.wait_ge(s_cst, 3)
                pool.wait_ge(s_mv, 1)
                pool.tensor_scalar(veps[:], mv[:, :, 1], EPS, None, ALU.add).then_inc(s_ve, 1)
                pool.wait_ge(s_ve, 1)
                pool.tensor_tensor(rstd[:], veps[:], mhalf[:], ALU.pow).then_inc(s_rstd, 1)

                def batch(i):
                    for g in range(UNITS):
                        G, Q = i * UNITS + g, i * PAIRS + g // 2
                        wait(pool, s_scan, G + 1)
                        wait(pool, s_cb, Q + 1)
                        wait(pool, s_y, G - RING + 1)
                        pool.tensor_tensor(hc[:, g % RING, :], H[:, g % RING, :], cb[:, (g // 2) % RING, :],
                                           ALU.mult).then_inc(s_hc, 1)

                batch(0)
                with pool.Fori(1, NBATCH) as i:
                    batch(i)
        ph.clear()
def attention(nc, tag, x, ident, w):
    GROUPS, GH = 4, 4
    HD = 8
    ROWS = P // GH
    NCH, TPS = SEQ // BLK, SEQ // P
    VW = HD + 1
    NPP = NCH + 2 * GROUPS * NCH + TPS // 2
    PR = 2 * GH
    SU = [(t, c, j) for t in range(TPS) for c in range(t // TPB + 1) for j in range(GH)]
    STEPS = [(c, kt) for c in range(NCH) for kt in range(TPB * (c + 1))]
    NS, NT = len(SU), len(STEPS)
    SPS = NS // NT
    DIAG = [v for v, (c, kt) in enumerate(STEPS) if kt >= TPB * c]

    def m_uses(g):
        uses = {}
        if 0 <= g < GROUPS:
            uses[1], uses[9] = ("max", g, 1), ("norm", g, 0)
        if 0 <= g - 1 < GROUPS:
            uses[3] = ("norm", g - 1, 1)
        if g + 1 < GROUPS:
            uses[7] = ("max", g + 1, 0)
        return uses
    M_ORDER = [u for g in range(-1, GROUPS + 1) for _, u in sorted(m_uses(g).items())]
    NM = len(M_ORDER)

    with ExitStack() as ctx:
        ph = Phase(nc, ctx, tag)
        sb, sem = ph.sb, ph.sem
        NW = 2 * GROUPS
        wst = sb("wst", [P, NW, P])
        wh, wl = sb("wh", [P, NW, P], F32R), sb("wl", [P, NW, P], F32R)
        wvs = sb("wvs", [P, GROUPS * GH * VW])
        wvh, wvl = sb("wvh", [P, GROUPS * GH * VW], F32R), sb("wvl", [P, GROUPS * GH * VW], F32R)
        vb = sb("vb", [P, GROUPS * GH * VW])
        bias, scale, low = sb("bias", [P, NW]), sb("scale", [P, NW]), sb("low", [P, NW])
        bsc = sb("bsc", [P, NW])
        wo, bo = sb("wo", [P, P]), sb("bo", [P, P])
        mask = sb("mask", [P, P])
        idr, mneg = sb("idr", [P, P], F32R), sb("mneg", [P, P], F32R)
        mhalf, zero = sb("mhalf", [P, TILES]), sb("zero", [P, TPB, GH])
        spare = sb("spare", [P, 4])
        stats, mv = sb("stats", [P, TILES, 6]), sb("mv", [P, TILES, 2])
        veps, rstd = sb("veps", [P, TILES]), sb("rstd", [P, TILES])
        xn = sb("xn", [P, TPS, P])
        xh, xl = sb("xh", [P, SEQ], F32R), sb("xl", [P, SEQ], F32R)
        qf, qh = sb("qf", [P, 2, BLK]), sb("qh", [P, 2, BLK], F32R)
        QK = sb("QK", [P, 2, GROUPS, SEQ], F32R)
        V = sb("V", [P, TPS, GROUPS * GH, ROWS])
        mx, mx0, mxh = sb("mx", [P, 2, TPS, GH]), sb("mx0", [P, 2, GH]), sb("mxh", [P, 2, TPB, GH], F32R)
        mt = sb("mt", [P, NCH, TPB, P])
        pt = sb("pt", [P, PR, BLK])
        ov = sb("ov", [P, NCH, BLK])
        rs = sb("rs", [P, TPB, GH])
        on = sb("on", [P, TPS, P])
        oT = sb("oT", [P, NCH, BLK])
        att, pos = sb("att", [P, BLK]), sb("pos", [P, BLK])

        W = ph.ps("W", [P, 5, BLK])
        PV = ph.ps("PV", [P, NCH, BLK])
        M = ph.ps("M", [P, BLK])

        s_ld, s_cst, s_wh, s_pre = sem("ld"), sem("cst"), sem("wh"), sem("pre")
        s_mv, s_ve, s_rstd = sem("mv"), sem("ve"), sem("rstd")
        s_gch, s_pch = sem("gch"), sem("pch")
        s_xn, s_pp = sem("xn"), sem("pp")
        s_xh, s_xl = sem("xh"), sem("xl")
        s_qf, s_qh, s_st = sem("qf"), sem("qh"), sem("st")
        s_v = sem("v")
        s_S, s_max = sem("S"), sem("max")
        s_mx, s_sp = sem("mx"), sem("sp")
        s_M, s_Mr = sem("M"), sem("Mr")
        s_T, s_exp, s_pm = sem("T"), sem("exp"), sem("pm")
        s_pv, s_ov = sem("pv"), sem("ov")
        s_onT, s_oT = sem("onT"), sem("oTs")
        s_o, s_x = sem("o"), sem("x")

        LOADS = ((wst[:], w["w_qk"]), (wvs[:], w["w_v"]), (vb[:], w["b_v"]), (bias[:], w["b_qk"]),
                 (scale[:], w["scale"]), (low[:], w["low"]), (wo[:], w["w_out"]), (bo[:], w["b_out"]),
                 (mask[:], w["mask"]))

        def chunk(c):
            return slice(c * BLK, (c + 1) * BLK)

        def tile(t):
            return slice(t * P, (t + 1) * P)

        def head(j):
            return slice(ROWS * j, ROWS * (j + 1))

        def m_index(i, use):
            return NM * i + M_ORDER.index(use)

        with nc.Block() as block:
            @block.sync
            def _(sp):
                for dst, src in LOADS:
                    sp.dma_start(dst, src).then_inc(s_ld, 16)

            @block.tensor
            def _(pe):
                def passes(out, ah, al, bh, bl):
                    pe.matmul(out, ah, bh, start=True, stop=False)
                    pe.matmul(out, al, bh, start=False, stop=False)
                    return pe.matmul(out, ah, bl, start=False, stop=True)

                def prologue(i):
                    wait(pe, s_xn, i + 1)
                    for c in range(NCH):
                        for t in range(TPB):
                            mm = pe.transpose(W[:, c, tile(t)], xn[:, TPB * c + t, :], ident[:])
                        mm.then_inc(s_pp, 1)
                    wait(pe, s_xl, 2 * i + 2)
                    n = NCH
                    for k in range(NW):
                        for c in range(NCH):
                            if n >= 6:
                                wait(pe, s_qf, 16 * i + n - 5)
                            passes(W[:, n % 4, :], wh[:, k, :], wl[:, k, :], xh[:, chunk(c)], xl[:, chunk(c)])\
                                .then_inc(s_pp, 1)
                            n += 1
                    for k in range(TPS // 2):
                        wait(pe, s_qf, 16 * i + n - 5)
                        for a in range(2):
                            t = tile(2 * k + a)
                            mm = passes(W[:, n % 4, a * GROUPS * GH * VW:(a + 1) * GROUPS * GH * VW],
                                        xh[:, t], xl[:, t], wvh[:], wvl[:])
                        mm.then_inc(s_pp, 1)
                        n += 1

                def max_unit(i, g, s):
                    t, c, j = SU[s]
                    n = (i * GROUPS + g) * NS + s
                    cols = min(BLK, (t + 1) * P - c * BLK)
                    diag = c == t // TPB
                    wait(pe, s_max, n - 1)
                    out = W[:, s % 2, 0:cols]
                    mm = pe.matmul(out, QK[head(j), 0, g, tile(t)], QK[head(j), 1, g, c * BLK:c * BLK + cols],
                                   start=True, stop=not diag)
                    if diag:
                        mm = pe.matmul(W[:, s % 2, cols - P:cols], idr[:], mneg[:], start=False, stop=True)
                    mm.then_inc(s_S, 1)

                def exp_step(i, g, v):
                    c, kt = STEPS[v]
                    r = max(0, kt - TPB * c)
                    if kt == 0:
                        wait(pe, s_Mr, m_index(i, ("max", g, c)) + 1)
                    for j in range(GH):
                        u = v * GH + j
                        n = (i * GROUPS + g) * NT * GH + u
                        wait(pe, s_exp, n - 2)
                        pe.matmul(W[:, 2 + u % 3, 0:BLK - r * P], QK[head(j), 1, g, tile(kt)],
                                  QK[head(j), 0, g, c * BLK + r * P:(c + 1) * BLK],
                                  start=True, stop=True).then_inc(s_T, 1)

                def value_step(i, g, v):
                    c, kt = STEPS[v]
                    r = max(0, kt - TPB * c)
                    if kt == 0:
                        wait(pe, s_ov, 8 * i + 2 * (g - 1) + c + 1)
                    for j in range(GH):
                        u = v * GH + j
                        n = (i * GROUPS + g) * NT * GH + u
                        if v in DIAG:
                            wait(pe, s_pm, (i * GROUPS + g) * len(DIAG) + DIAG.index(v) + 1)
                        else:
                            wait(pe, s_exp, n + 1)
                        pe.matmul(PV[head(j), c, r * P:], V[:, kt, g * GH + j, :], pt[:, u % PR, 0:BLK - r * P],
                                  start=kt == 0, stop=kt == TPB * (c + 1) - 1).then_inc(s_pv, 1)

                def m_use(i, use):
                    kind, g, c = use
                    if kind == "max":
                        wait(pe, s_sp, 8 * i + 2 * g + c + 1)
                    else:
                        wait(pe, s_ov, 8 * i + 2 * g + c + 1)
                    wait(pe, s_Mr, m_index(i, use))
                    for t in range(TPB):
                        src = mt[:, c, t, :] if kind == "max" else ov[:, c, tile(t)]
                        mm = pe.transpose(M[:, tile(t)], src, ident[:])
                    mm.then_inc(s_M, 1)

                def batch(i):
                    prologue(i)
                    wait(pe, s_st, 16 * (i + 1))
                    wait(pe, s_v, (TPS // 2) * (i + 1))
                    for g in range(-1, GROUPS + 1):
                        uses = m_uses(g)
                        for v in range(NT):
                            if 0 <= g < GROUPS:
                                exp_step(i, g, v)
                            if g + 1 < GROUPS:
                                for s in range(SPS * v, SPS * (v + 1)):
                                    max_unit(i, g + 1, s)
                            if v in uses:
                                m_use(i, uses[v])
                            if 0 < v and 0 <= g < GROUPS:
                                value_step(i, g, v - 1)
                            if v == 0 and 0 <= g - 1:
                                value_step(i, g - 1, NT - 1)
                    wait(pe, s_Mr, NM * (i + 1))
                    for c in range(NCH):
                        for t in range(TPB):
                            mm = pe.transpose(W[:, 2 + c, tile(t)], on[:, TPB * c + t, :], ident[:])
                        mm.then_inc(s_onT, 1)
                    for c in range(NCH):
                        wait(pe, s_oT, 2 * i + c + 1)
                        for t in range(TPB):
                            mm = pe.matmul(W[:, c, tile(t)], oT[:, c, tile(t)], wo[:], start=True, stop=True)
                        mm.then_inc(s_o, 1)

                pe.wait_ge(s_pre, 3)
                batch(0)
                with pe.Fori(1, NBATCH) as i:
                    batch(i)

            @block.scalar
            def _(act):
                act.wait_ge(s_ld, 16 * len(LOADS))
                act.activation(wh[:], wst[:], ACT.Copy).then_inc(s_wh, 1)
                act.activation(wvh[:], wvs[:], ACT.Copy).then_inc(s_wh, 1)
                act.wait_ge(s_pre, 3)

                def exp_step(i, g, v):
                    c, kt = STEPS[v]
                    r = max(0, kt - TPB * c)
                    for j in range(GH):
                        u = v * GH + j
                        n = (i * GROUPS + g) * NT * GH + u
                        wait(act, s_T, n + 1)
                        wait(act, s_pv, n - PR + 1)
                        act.activation(pt[:, u % PR, 0:BLK - r * P], W[:, 2 + u % 3, 0:BLK - r * P],
                                       ACT.Exp).then_inc(s_exp, 1)

                def take_out(i, g, c):
                    wait(act, s_pv, ((i * GROUPS + g) * NT + (TPB if c == 0 else NT)) * GH)
                    if g:
                        wait(act, s_M, m_index(i, ("norm", g - 1, c)) + 1)
                    act.activation(ov[:, c, :], PV[:, c, :], ACT.Copy).then_inc(s_ov, 1)

                def batch(i):
                    for c in range(NCH):
                        wait(act, s_pp, NPP * i + c + 1)
                        act.activation(xh[:, chunk(c)], W[:, c, :], ACT.Copy).then_inc(s_xh, 1)
                    for k in range(NW):
                        for c in range(NCH):
                            m = 2 * k + c
                            n = NCH + m
                            wait(act, s_pp, NPP * i + n + 1)
                            wait(act, s_st, 16 * i + m - 1)
                            act.activation(qf[:, m % 2, :], W[:, n % 4, :], ACT.Identity,
                                           bias=bsc[:, k:k + 1], scale=scale[:, k:k + 1]).then_inc(s_qf, 1)
                    for g in range(GROUPS + 1):
                        for v in range(NT):
                            if g < GROUPS:
                                exp_step(i, g, v)
                            if v == 5 and g < GROUPS:
                                take_out(i, g, 0)
                            if v == 1 and g:
                                take_out(i, g - 1, 1)
                    for c in range(NCH):
                        wait(act, s_onT, 2 * i + c + 1)
                        act.activation(oT[:, c, :], W[:, 2 + c, :], ACT.Copy).then_inc(s_oT, 1)

                batch(0)
                with act.Fori(1, NBATCH) as i:
                    batch(i)

            @block.vector
            def _(dve):
                dve.wait_ge(s_ld, 16 * len(LOADS))
                ch = Chain(dve, s_gch)
                for t in range(TILES):
                    last = dve.bn_stats(stats[:, t, :], x[:, tile(t)])
                ch.step(last)
                ch.join()
                for t in range(TILES):
                    last = dve.bn_aggr(mv[:, t, :], stats[:, t, :])
                last.then_inc(s_mv, 1)
                dve.tensor_tensor(bsc[:], bias[:], scale[:], ALU.mult)
                dve.tensor_copy(idr[:], ident[:])
                dve.tensor_copy(mneg[:], mask[:]).then_inc(s_pre, 1)
                dve.wait_ge(s_wh, 2)
                dve.tensor_tensor(wl[:], wst[:], wh[:].bitcast(F32), ALU.subtract).then_inc(s_pre, 1)
                dve.tensor_tensor(wvl[:], wvs[:], wvh[:].bitcast(F32), ALU.subtract).then_inc(s_pre, 1)
                dve.wait_ge(s_cst, 4)
                dve.wait_ge(s_rstd, 1)
                PER = 8 * 1 + NCH * 3

                def max_unit(i, g, s):
                    t, c, j = SU[s]
                    n = (i * GROUPS + g) * NS + s
                    wait(dve, s_S, n + 1)
                    if s == 0:
                        wait(dve, s_sp, 8 * i + 2 * (g - 1))
                    last = c == t // TPB
                    dst = mx[:, g % 2, t, j:j + 1] if last else mx0[:, t % 2, j:j + 1]
                    dve.tensor_reduce(dst, W[:, s % 2, 0:min(BLK, (t + 1) * P - c * BLK)], AX, ALU.max)\
                       .then_inc(s_max, 1)

                def both_chunks(i, g, t):
                    n = max(s for s in range(NS) if SU[s][0] == t)
                    wait(dve, s_max, (i * GROUPS + g) * NS + n + 1)
                    dve.tensor_tensor(mx[:, g % 2, t, :], mx[:, g % 2, t, :], mx0[:, t % 2, :], ALU.max)\
                       .then_inc(s_mx, 1)

                def m_use(i, use, ch):
                    kind, g, c = use
                    wait(dve, s_M, m_index(i, use) + 1)
                    if kind == "max":
                        q = QK[:, 0, g, chunk(c)]
                        dve.tensor_tensor(q, q.bitcast(F32), M[:], ALU.add).then_inc(s_Mr, 1)
                    else:
                        m4 = M[:].rearrange("p (t j r) -> p t j r", t=TPB, j=GH)
                        ch.step(dve.reciprocal(rs[:], m4[:, :, :, HD]))
                        ch.join()
                        out = on[:, TPB * c:TPB * (c + 1), g * GH * HD:(g + 1) * GH * HD]
                        dve.tensor_tensor(out.rearrange("p t (j d) -> p t j d", j=GH), m4[:, :, :, 0:HD],
                                          rs[:].unsqueeze(3).broadcast_to((P, TPB, GH, HD)), ALU.mult)\
                           .then_inc(s_Mr, 1)

                def batch(i):
                    ch = Chain(dve, s_gch, 1 + PER * i)
                    for t in range(TPS):
                        last = dve.tensor_scalar(xn[:, t, :], x[:, bass.ds((i * TPS + t) * P, P)],
                                                 mv[:, bass.ds(i * TPS + t, 1), 0:1].rearrange("p a b -> p (a b)"),
                                                 rstd[:, bass.ds(i * TPS + t, 1)], ALU.subtract, ALU.mult)
                    last.then_inc(s_xn, 1)
                    for c in range(NCH):
                        wait(dve, s_xh, 2 * i + c + 1)
                        dve.tensor_tensor(xl[:, chunk(c)], W[:, c, :], xh[:, chunk(c)].bitcast(F32),
                                          ALU.subtract).then_inc(s_xl, 1)
                    for m in range(2 * NW + 1):
                        if m < 2 * NW:
                            wait(dve, s_qf, 16 * i + m + 1)
                            dve.tensor_copy(qh[:, m % 2, :], qf[:, m % 2, :]).then_inc(s_qh, 1)
                        if m:
                            k, c, s = (m - 1) // 2, (m - 1) % 2, (m - 1) % 2
                            wait(dve, s_qh, 16 * i + m)
                            dve.scalar_tensor_tensor(QK[:, k // GROUPS, k % GROUPS, chunk(c)],
                                                     qh[:, s, :].bitcast(F32), low[:, k:k + 1], qf[:, s, :],
                                                     ALU.mult, ALU.add).then_inc(s_st, 1)
                    for k in range(TPS // 2):
                        n = NCH + 2 * NW + k
                        wait(dve, s_pp, NPP * i + n + 1)
                        for a in range(2):
                            src = W[:, n % 4, a * GROUPS * GH * VW:(a + 1) * GROUPS * GH * VW]
                            last = dve.tensor_tensor(V[:, 2 * k + a, :, 0:VW],
                                                     src.rearrange("p (h e) -> p h e", e=VW),
                                                     vb[:].rearrange("p (h e) -> p h e", e=VW), ALU.add)
                        last.then_inc(s_v, 1)
                    for g in range(-1, GROUPS + 1):
                        uses = m_uses(g)
                        for v in range(NT):
                            if v - 1 in uses:
                                m_use(i, uses[v - 1], ch)
                            if g + 1 < GROUPS:
                                for s in range(SPS * v, SPS * (v + 1)):
                                    max_unit(i, g + 1, s)
                                    t = SU[s][0]
                                    if t > TPB and SU[s - 1][0] == t - 1:
                                        both_chunks(i, g + 1, t - 1)
                        if g + 1 < GROUPS:
                            both_chunks(i, g + 1, TPS - 1)
                    for c in range(NCH):
                        wait(dve, s_o, 2 * i + c + 1)
                        ch.step(dve.tensor_tensor(att[:].rearrange("p (t f) -> p t f", t=TPB),
                                                  W[:, c, :].rearrange("p (t f) -> p t f", t=TPB),
                                                  bo[:].unsqueeze(1).broadcast_to((P, TPB, P)), ALU.add))
                        ch.join()
                        xb = x[:, bass.ds(i * SEQ + c * BLK, BLK)]
                        ch.step(dve.scalar_tensor_tensor(pos[:], att[:], 0.0, xb, ALU.max, ALU.add))
                        ch.join()
                        ch.step(dve.scalar_tensor_tensor(xb, att[:], 0.0, pos[:], ALU.min, ALU.add))
                        ch.join()

                batch(0)
                with dve.Fori(1, NBATCH) as i:
                    batch(i)

            @block.gpsimd
            def _(pool):
                pool.memset(mhalf[:], -0.5).then_inc(s_cst, 1)
                pool.memset(V[:], 0.0).then_inc(s_cst, 1)
                pool.memset(mt[:], 0.0).then_inc(s_cst, 1)
                pool.memset(zero[:], 0.0).then_inc(s_cst, 1)
                pool.wait_ge(s_cst, 4)
                pool.wait_ge(s_mv, 1)
                pool.tensor_scalar(veps[:], mv[:, :, 1], EPS, None, ALU.add).then_inc(s_ve, 1)
                pool.wait_ge(s_ve, 1)
                pool.tensor_tensor(rstd[:], veps[:], mhalf[:], ALU.pow).then_inc(s_rstd, 1)

                def split_max(i, g, c):
                    if c == 0:
                        wait(pool, s_max, (i * GROUPS + g) * NS + TPB * GH)
                    else:
                        wait(pool, s_mx, (i * GROUPS + g + 1) * TPB)
                    if g:
                        wait(pool, s_M, m_index(i, ("max", g - 1, c)) + 1)
                    src = mx[:, g % 2, TPB * c:TPB * (c + 1), :]
                    m4 = mt[:, c, :, :].rearrange("p t (j r) -> p t j r", j=GH)
                    pool.tensor_tensor(mxh[:, c, :, :], src, zero[:], ALU.add).then_inc(s_pch, 1)
                    wait(pool, s_pch, 8 * i + 2 * g + c + 1)
                    high = mxh[:, c, :, :].bitcast(F32)
                    pool.tensor_tensor(m4[:, :, :, 3 * HD], zero[:], high, ALU.subtract)
                    pool.tensor_tensor(m4[:, :, :, 3 * HD + 1], high, src, ALU.subtract).then_inc(s_sp, 1)

                def mask_step(i, g, v):
                    wait(pool, s_exp, ((i * GROUPS + g) * NT + v + 1) * GH)
                    pool.tensor_tensor(spare[:, DIAG.index(v) % 4:DIAG.index(v) % 4 + 1], zero[:, 0, 0:1], zero[:, 0, 0:1],
                                       ALU.add)
                    d = pt[:, (v % 2) * GH:(v % 2 + 1) * GH, 0:P]
                    pool.affine_select(out=d, in_=d, compare_op=ALU.is_ge, fill=0.0, base=0,
                                       pattern=[[0, GH], [1, P]], channel_multiplier=-1).then_inc(s_pm, 1)

                def batch(i):
                    split_max(i, 0, 0)
                    for g in range(GROUPS):
                        split_max(i, g, 1)
                        for v in DIAG:
                            if v == DIAG[TPB] and g + 1 < GROUPS:
                                split_max(i, g + 1, 0)
                            mask_step(i, g, v)

                batch(0)
                with pool.Fori(1, NBATCH) as i:
                    batch(i)
        ph.clear()
def macaron_program(nc, hidden, identity, out, moe, mam, tern, att):
    PAD = 2 * TPB
    with ExitStack() as ctx:
        x = ctx.enter_context(nc.sbuf_tensor("x", [P, (TILES + PAD) * P], F32))
        ident = ctx.enter_context(nc.sbuf_tensor("ident", [P, P], F32))
        s_load = ctx.enter_context(nc.semaphore("load"))
        s_store = ctx.enter_context(nc.semaphore("store"))
        x_tiles = x[:, 0:TOKENS].rearrange("p (t c) -> p t c", t=TILES)

        with nc.Block() as block:
            @block.sync
            def _(sp):
                sp.dma_start(x_tiles, hidden.rearrange("b (t p) c -> p (b t) c", p=P)).then_inc(s_load, 16)
                sp.dma_start(ident[:], identity).then_inc(s_load, 16)
                sp.wait_ge(s_load, 32)

            @block.gpsimd
            def _(pool):
                pool.memset(x[:, TOKENS:], 0.0)

        moe_ffn(nc, "m0", x, ident, moe)
        mamba(nc, "a0", x, ident, mam)
        moe_ffn(nc, "m1", x, ident, moe)
        ternary_ffn(nc, "t0", x, ident, tern)
        attention(nc, "a1", x, ident, att)
        ternary_ffn(nc, "t1", x, ident, tern)

        with nc.Block() as block:
            @block.sync
            def _(sp):
                sp.dma_start(out.rearrange("b (t p) c -> p (b t) c", p=P), x_tiles).then_inc(s_store, 16)
                sp.wait_ge(s_store, 16)


def stacked(a, parts):
    return a.reshape(parts, P, *a.shape[1:]).swapaxes(0, 1)


def moe_layout(inp):
    g = lambda n: inp["L0_ffn_" + n]
    E, H, HID = g("be2").shape[0], g("Wr1").shape[1], g("Ws1").shape[1]
    wr1, wr2, br1 = np.zeros((P, P), np.float32), np.zeros((P, E), np.float32), np.zeros((P, 1), np.float32)
    wr1[:, :H] = g("Wr1")
    wr2[:H] = g("Wr2")
    wr2[H] = g("br2")
    br1[:H, 0] = g("br1")
    br1[H] = 1
    b1 = np.concatenate([g("be1"), g("bs1")[None]])
    w2 = np.concatenate([g("We2"), g("Ws2")[None]])
    sel = np.zeros((2, E, E, P), np.float32)
    for e in range(E):
        sel[:, e, e] = 1
    return {
        "wr1": wr1, "wr2": wr2, "br1": br1,
        "b1": b1.reshape(E + 1, HID // P, P).transpose(2, 0, 1),
        "bs2": g("bs2").reshape(P, 1),
        "be2": np.concatenate([g("be2"), g("be2")]),
        "w1": np.concatenate([g("We1"), g("Ws1")[None]]),
        "w2": w2.reshape(E + 1, HID // P, P, P).transpose(0, 2, 1, 3).reshape(E + 1, P, HID),
        "route_sel": sel.reshape(2 * E, E, P),
        "rank": np.broadcast_to(E - np.arange(E, dtype=np.float32), (P, TPB, E)),
    }


def mamba_layout(inp):
    g = lambda n: inp["L0_attn_" + n]
    both = lambda n: np.stack([g(n + "f"), g(n + "r")])
    ns, rank = g("A_log_f").shape[1], g("dt_proj_w_f").shape[1]
    dbc = 4 * ns
    b, c = np.arange(rank, rank + ns), np.arange(rank + ns, rank + 2 * ns)
    rows = np.concatenate([b, c, b, c, np.arange(rank)])
    dtw = np.zeros((dbc + rank, 2, 2, P), np.float32)
    dtw[dbc:] = both("dt_proj_w_").transpose(2, 0, 1).reshape(rank, 2, 2, P)
    sel = np.zeros((2, 2 * ns, 2 * ns, P), np.float32)
    for n in range(2 * ns):
        sel[:, n, n] = 1
    halves = lambda a: a.reshape(2, 2, P, -1).transpose(2, 0, 1, 3)
    return {
        "in_proj": g("in_proj_w").T,
        "conv_w": halves(both("conv_w_")),
        "vecs": np.stack([halves(both(n))[..., 0] for n in ("conv_b_", "dt_proj_b_", "D_")], 1),
        "x_proj": both("x_proj_w_")[:, rows].reshape(2, dbc + rank, 2, P).transpose(3, 0, 2, 1),
        "dt_proj": dtw,
        "A_log": halves(both("A_log_")),
        "out_proj": stacked(g("out_proj_w").T, 2),
        "bc_sel": sel.reshape(dbc, 2 * ns, P),
    }


def ternary_layout(inp):
    g = lambda n: inp["L1_ffn_" + n]
    square = lambda n: g(n).T.reshape(4, P, 4 * P)
    w3 = stacked(g("w3_w").T, 4).reshape(1, P, 4 * P)
    return {
        "w": np.concatenate([g("w1_w").T[None], g("w2_w").T[None], square("h1_w"), square("h2_w"), w3]),
        "scales": np.concatenate([g(n).reshape(-1, P).T for n in ("w1_s", "w2_s", "h1_s", "h2_s", "w3_s")], 1),
    }


def attention_layout(inp):
    g = lambda n: inp["L1_attn_" + n]
    w_in, b_in = g("w_in"), g("b_in")
    HEADS, HD, GH, ROWS = 16, 8, 4, 32
    GROUPS = HEADS // GH
    wqk = np.zeros((P, 2, GROUPS, GH, ROWS), np.float32)
    bqk, low = np.zeros((2, GROUPS, GH, ROWS), np.float32), np.zeros((2, GROUPS, GH, ROWS), np.float32)
    scale = np.ones((2, GROUPS, GH, ROWS), np.float32)
    for kind in range(2):
        w = w_in[kind * P:(kind + 1) * P].T.reshape(P, GROUPS, GH, HD)
        b = b_in[kind * P:(kind + 1) * P].reshape(GROUPS, GH, HD)
        for part in range(3):
            wqk[:, kind, :, :, part * HD:(part + 1) * HD] = w
            bqk[kind, :, :, part * HD:(part + 1) * HD] = b
    low[0, :, :, HD:2 * HD] = -1
    low[1, :, :, 2 * HD:3 * HD] = -1
    bqk[1, :, :, 3 * HD:3 * HD + 2] = 1
    scale[0] = np.float32(1.0 / np.sqrt(HD))
    wv, bv = np.zeros((P, HEADS, HD + 1), np.float32), np.ones((HEADS, HD + 1), np.float32)
    wv[:, :, :HD] = w_in[2 * P:].T.reshape(P, HEADS, HD)
    bv[:, :HD] = b_in[2 * P:].reshape(HEADS, HD)
    cols = lambda a: a.reshape(2 * GROUPS, P).T
    return {
        "w_qk": wqk.reshape(P, 2 * GROUPS, P), "b_qk": cols(bqk), "scale": cols(scale), "low": cols(low),
        "w_v": wv.reshape(P, -1), "b_v": np.broadcast_to(bv.reshape(1, -1), (P, HEADS * (HD + 1))),
        "w_out": g("w_out").T, "b_out": np.broadcast_to(g("b_out"), (P, P)),
        "mask": np.triu(np.full((P, P), -1e30, np.float32), 1),
    }


def kernel(**inputs):
    import concourse.bacc as bacc
    from concourse.bass_utils import run_bass_kernel_spmd

    inp = {k: np.asarray(v) for k, v in inputs.items()}
    nc = bacc.Bacc("TRN2", target_bir_lowering=False, num_devices=1)
    arrays = {}

    def tensor(name, a):
        arrays[name] = np.ascontiguousarray(a)
        return nc.dram_tensor(name, a.shape, mybir.dt.from_np(a.dtype), kind="ExternalInput").ap()

    hidden = tensor("hidden", inp["L0_attn_hidden_states"])
    identity = tensor("identity", np.eye(P, dtype=np.float32))
    groups = [{k: tensor(f"{tag}_{k}", a) for k, a in layout(inp).items()}
              for tag, layout in (("moe", moe_layout), ("mamba", mamba_layout),
                                  ("ternary", ternary_layout), ("attention", attention_layout))]
    out = nc.dram_tensor("out", (NBATCH, SEQ, P), F32, kind="ExternalOutput").ap()
    macaron_program(nc, hidden, identity, out, *groups)
    return run_bass_kernel_spmd(nc, [arrays], core_ids=[0]).results[0]["out"]
```

```python
from contextlib import ExitStack

import numpy as np

import concourse.bass as bass
from concourse import mybir

F32 = mybir.dt.float32
F32R = mybir.dt.float32r
ACT = mybir.ActivationFunctionType
ALU = mybir.AluOpType
AX = mybir.AxisListType.X

P = 128
NBATCH, SEQ = 4, 1024
TOKENS = NBATCH * SEQ
TILES = TOKENS // P
BLK = 512
NBLK = TOKENS // BLK
TPB = BLK // P
EPS = 1e-5


def wait(eng, sem, value):
    if not isinstance(value, int) or value > 0:
        eng.wait_ge(sem, value)


class Chain:

    def __init__(self, eng, sem, base=0):
        self.eng, self.sem, self.base, self.n = eng, sem, base, 0

    def step(self, ins):
        self.n += 1
        ins.then_inc(self.sem, 1)
        return ins

    def join(self):
        wait(self.eng, self.sem, self.base + self.n)


class Phase:

    def __init__(self, nc, ctx, tag):
        self.nc, self.ctx, self.tag, self.sems = nc, ctx, tag, []

    def sb(self, name, shape, dt=F32):
        return self.ctx.enter_context(self.nc.sbuf_tensor(f"{self.tag}_{name}", shape, dt))

    def ps(self, name, shape, dt=F32):
        return self.ctx.enter_context(self.nc.psum_tensor(f"{self.tag}_{name}", shape, dt))

    def sem(self, name):
        s = self.ctx.enter_context(self.nc.semaphore(f"{self.tag}_{name}"))
        self.sems.append(s)
        return s

    def clear(self):
        with self.nc.Block() as block:
            @block.gpsimd
            def _(pool):
                for s in self.sems:
                    pool.sem_clear(s)


def norm_stats(nc, dve, chain, x_tile, stats, mv, spare):
    n = mv.shape[1]
    for t in range(n):
        last = dve.bn_stats(stats[:, t, :], x_tile(t))
    chain.step(last)
    chain.join()
    dve.tensor_copy(spare[:], stats[:, 0, 0:1])
    for t in range(n):
        last = dve.bn_aggr(mv[:, t, :], stats[:, t, :])
    return last


def moe_ffn(nc, tag, x, ident, w):
    E = 8
    JOBS = E + 1
    KC = 4
    NUP = JOBS * KC
    with ExitStack() as ctx:
        ph = Phase(nc, ctx, tag)
        sb, sem = ph.sb, ph.sem
        w1h, w1l = sb("w1h", [P, JOBS, 512], F32R), sb("w1l", [P, JOBS, 512], F32R)
        w2h, w2l = sb("w2h", [P, JOBS, 512], F32R), sb("w2l", [P, JOBS, 512], F32R)
        NST = 4
        wst = sb("wst", [P, NST, 512])
        wr1s = sb("wr1s", [P, P])
        wr1h, wr1l = sb("wr1h", [P, P], F32R), sb("wr1l", [P, P], F32R)
        wr2 = sb("wr2", [P, E])
        br1 = sb("br1", [P, 1])
        b1 = sb("b1", [P, JOBS, KC])
        bs2 = sb("bs2", [P, 1])
        be2s = sb("be2s", [2 * E, P])
        be2h, be2l = sb("be2h", [2 * E, P], F32R), sb("be2l", [2 * E, P], F32R)
        sels = sb("sels", [2 * E, E, P])
        sel = sb("sel", [2 * E, E, P], F32R)
        rank = sb("rank", [P, TPB, E])
        ebase, ebase2, mhalf = sb("ebase", [P, TPB, E]), sb("ebase2", [P, TPB]), sb("mhalf", [P, TPB])

        stats, mv = sb("stats", [P, TPB, 6]), sb("mv", [P, TPB, 2])
        veps, rstd = sb("veps", [P, TPB]), sb("rstd", [P, TPB])
        eps, spare = sb("eps", [P, TPB]), sb("spare", [P, 1])
        xn = sb("xn", [P, TPB, P])
        xh, xl = sb("xh", [P, 2, BLK], F32R), sb("xl", [P, 2, BLK], F32R)
        r1 = sb("r1", [P, BLK])
        NRAW = 4
        raw = sb("raw", [P, NRAW, BLK])
        hh, hl = sb("hh", [P, 2, KC, BLK], F32R), sb("hl", [P, 2, KC, BLK], F32R)
        wts = sb("wts", [2 * E, BLK], F32R)
        wbc = sb("wbc", [P, 2, BLK])
        prod = sb("prod", [P, 2, BLK])
        acc, accf = sb("acc", [P, BLK]), sb("accf", [P, BLK])
        g8 = lambda n: sb(n, [P, TPB, E])
        g1 = lambda n: sb(n, [P, TPB])
        lg, sh, ex, gt, eq, cc, oh1, gm, oh2, wsum, wtmp, wall = map(g8, (
            "lg", "sh", "ex", "gt", "eq", "cc", "oh1", "gm", "oh2", "wsum", "wtmp", "wall"))
        mx, sm, rs, top1, cm, top2, dd, tt, t1, wa, wb = map(g1, (
            "mx", "sm", "rs", "top1", "cm", "top2", "dd", "tt", "t1", "wa", "wb"))
        w16 = sb("w16", [P, TPB, 2 * E])

        U = ph.ps("U", [P, 4, BLK])
        Y = ph.ps("Y", [P, 2, BLK])
        R = ph.ps("R", [P, BLK])
        T = ph.ps("T", [P, BLK])

        s_small = sem("small")
        s_wst = [sem(f"wst{i}") for i in range(NST)]
        s_wsp = sem("wsp")
        s_wsc = sem("wsc")
        s_cst = sem("cst")
        s_pre = sem("pre")
        s_mv = sem("mv")
        s_ve = sem("ve")
        s_rstd = sem("rstd")
        s_xn = sem("xn")
        s_xT = sem("xT")
        s_xh, s_xl = sem("xh"), sem("xl")
        s_r1p, s_r1 = sem("r1p"), sem("r1")
        s_lg = sem("lg")
        s_gch = sem("gch")
        s_sh, s_ex = sem("sh"), sem("ex")
        s_dd, s_tt = sem("dd"), sem("tt")
        s_w = sem("w")
        s_wT, s_wTs = sem("wT"), sem("wTs")
        s_bc, s_wbc = sem("bc"), sem("wbc")
        s_up = sem("up")
        s_raw, s_hh = sem("raw"), sem("hh")
        s_hl = sem("hl")
        s_dn = sem("dn")
        s_yc = sem("yc")
        s_acc = sem("acc")
        s_aT, s_x = sem("aT"), sem("x")

        pieces = [(kind, j) for j in range(JOBS) for kind in (0, 1)]

        with nc.Block() as block:
            @block.sync
            def _(sp):
                for dst, src in ((wr1s[:], w["wr1"]), (wr2[:], w["wr2"]), (br1[:], w["br1"]),
                                 (b1[:], w["b1"]), (bs2[:], w["bs2"]), (be2s[:], w["be2"]),
                                 (sels[:], w["route_sel"]), (rank[:], w["rank"])):
                    sp.dma_start(dst, src).then_inc(s_small, 16)
                for n, (kind, j) in enumerate(pieces):
                    if n >= NST:
                        sp.wait_ge(s_wsp, n - NST + 1)
                    src = (w["w1"], w["w2"])[kind][j]
                    sp.dma_start(wst[:, n % NST, :], src).then_inc(s_wst[n % NST], 16)

            @block.tensor
            def _(pe):
                def up(b, par, j):
                    for k in range(KC):
                        n = NUP * b + KC * j + k
                        if k < KC - 1:
                            wait(pe, s_hh, 3 * JOBS * b + 3 * j + k + 1 - 3)
                        else:
                            wait(pe, s_raw, n - 3)
                        c = slice(k * P, (k + 1) * P)
                        pe.matmul(U[:, k, :], w1h[:, j, c], xh[:, par, :], start=True, stop=False)
                        pe.matmul(U[:, k, :], w1l[:, j, c], xh[:, par, :], start=False, stop=False)
                        pe.matmul(U[:, k, :], w1h[:, j, c], xl[:, par, :], start=False, stop=True)\
                          .then_inc(s_up, 1)

                def down(b, par, j):
                    q = (par + j) % 2
                    wait(pe, s_yc, JOBS * b + j - 1)
                    for k in range(KC):
                        wait(pe, s_hl, NUP * b + KC * j + k + 1)
                        c = slice(k * P, (k + 1) * P)
                        pe.matmul(Y[:, q, :], w2h[:, j, c], hh[:, q, k, :], start=(k == 0), stop=False)
                        pe.matmul(Y[:, q, :], w2l[:, j, c], hh[:, q, k, :], start=False, stop=False)
                        last = k == KC - 1 and j < E
                        mm = pe.matmul(Y[:, q, :], w2h[:, j, c], hl[:, q, k, :], start=False, stop=last)
                    if j == E:
                        pe.matmul(Y[:, q, :], be2h[:], wts[:], start=False, stop=False)
                        mm = pe.matmul(Y[:, q, :], be2l[:], wts[:], start=False, stop=True)
                    mm.then_inc(s_dn, 1)

                def norm_T(b):
                    wait(pe, s_xn, b + 1)
                    for t in range(TPB):
                        mm = pe.transpose(T[:, t * P:(t + 1) * P], xn[:, t, :], ident[:])
                    mm.then_inc(s_xT, 1)

                def sum_T(b):
                    wait(pe, s_yc, JOBS * (b + 1))
                    for t in range(TPB):
                        mm = pe.transpose(T[:, t * P:(t + 1) * P], accf[:, t * P:(t + 1) * P], ident[:])
                    mm.then_inc(s_aT, 1)

                def bcast(b, e):
                    wait(pe, s_wbc, E * b + e)
                    pe.matmul(R[:], sel[:, e, :], wts[:], start=True, stop=True).then_inc(s_bc, 1)

                def router(b, par):
                    wait(pe, s_xh, b + 1)
                    wait(pe, s_xl, b + 1)
                    wait(pe, s_wbc, E * b - 6)
                    pe.matmul(R[:], wr1h[:], xh[:, par, :], start=True, stop=False)
                    pe.matmul(R[:], wr1l[:], xh[:, par, :], start=False, stop=False)
                    pe.matmul(R[:], wr1h[:], xl[:, par, :], start=False, stop=True).then_inc(s_r1p, 1)

                def logits(b):
                    wait(pe, s_r1, b + 1)
                    for t in range(TPB):
                        mm = pe.matmul(R[:, t * E:(t + 1) * E], r1[:, t * P:(t + 1) * P], wr2[:],
                                       start=True, stop=True)
                    mm.then_inc(s_lg, 1)

                def run_block(b, par, first=False):
                    if first:
                        pe.wait_ge(s_wsp, 1)
                    up(b, par, 0)
                    if first:
                        pe.wait_ge(s_wsp, len(pieces))
                    up(b, par, 1)
                    down(b, par, 0)
                    if not first:
                        sum_T(b - 1)
                    up(b, par, 2)
                    wait(pe, s_w, b + 1)
                    wait(pe, s_x, b)
                    for t in range(TPB):
                        mm = pe.transpose(T[0:2 * E, t * P:(t + 1) * P], w16[:, t, :], ident[:])
                    mm.then_inc(s_wT, 1)
                    wait(pe, s_wTs, b + 1)
                    bcast(b, 0)
                    norm_T(b + 1)
                    down(b, par, 1)
                    for j in range(3, JOBS):
                        if j == 4:
                            router(b + 1, 1 - par)
                        up(b, par, j)
                        if j == 4:
                            logits(b + 1)
                            down(b, par, j - 1)
                            wait(pe, s_sh, b + 2)
                        bcast(b, j - 2)
                        if j != 4:
                            down(b, par, j - 1)
                    bcast(b, E - 1)
                    down(b, par, E)

                pe.wait_ge(s_pre, 5)
                norm_T(0)
                router(0, 0)
                logits(0)
                run_block(0, 0, first=True)
                run_block(1, 1)
                with pe.Fori(1, NBLK // 2) as i:
                    run_block(i * 2, 0)
                    run_block(i * 2 + 1, 1)
                pe.wait_ge(s_xh, NBLK + 1)
                pe.wait_ge(s_xl, NBLK + 1)
                sum_T(NBLK - 1)

            @block.scalar
            def _(act):
                def split_x(b, par):
                    wait(act, s_xT, b + 1)
                    wait(act, s_up, NUP * (b - 1))
                    act.activation(xh[:, par, :], T[:], ACT.Copy).then_inc(s_xh, 1)

                def bcast(b, e):
                    wait(act, s_bc, E * b + e + 1)
                    wait(act, s_yc, JOBS * b + e - 1 if e >= 2 else JOBS * b)
                    act.activation(wbc[:, e % 2, :], R[:], ACT.Copy).then_inc(s_wbc, 1)

                def router(b):
                    wait(act, s_r1p, b + 1)
                    wait(act, s_lg, b)
                    act.activation(r1[:], R[:], ACT.Relu, bias=br1[:]).then_inc(s_r1, 1)

                def run_block(b, par):
                    for j in range(JOBS):
                        q = (par + j) % 2
                        for k in range(KC):
                            n = NUP * b + KC * j + k
                            wait(act, s_up, n + 1)
                            wait(act, s_hl, n - 3)
                            act.activation(raw[:, k, :], U[:, k, :], ACT.Silu, bias=b1[:, j, k:k + 1])\
                               .then_inc(s_raw, 1)
                            if k < KC - 1:
                                if k == 0:
                                    wait(act, s_dn, JOBS * b + j - 1)
                                act.activation(hh[:, q, k, :], U[:, k, :], ACT.Silu,
                                               bias=b1[:, j, k:k + 1]).then_inc(s_hh, 1)
                        if j == 2:
                            wait(act, s_wT, b + 1)
                            wait(act, s_dn, JOBS * b)
                            act.activation(wts[:], T[0:2 * E, :], ACT.Copy).then_inc(s_wTs, 1)
                        if j >= 2:
                            bcast(b, j - 2)
                        if j == 2:
                            split_x(b + 1, 1 - par)
                        if j == 3:
                            router(b + 1)
                    bcast(b, E - 1)

                act.wait_ge(s_pre, 5)
                split_x(0, 0)
                router(0)
                for n, (kind, j) in enumerate(pieces):
                    act.wait_ge(s_wst[n % NST], 16 * (n // NST + 1))
                    act.activation((w1h, w2h)[kind][:, j, :], wst[:, n % NST, :], ACT.Copy).then_inc(s_wsc, 1)
                run_block(0, 0)
                run_block(1, 1)
                with act.Fori(1, NBLK // 2) as i:
                    run_block(i * 2, 0)
                    run_block(i * 2 + 1, 1)

            @block.vector
            def _(dve):
                def bc(a):
                    return a[:].rearrange("p (t o) -> p t o", o=1).broadcast_to([P, TPB, E])

                def norm(b, ch):
                    last = norm_stats(nc, dve, ch, lambda t: x[:, bass.ds((b * TPB + t) * P, P)], stats, mv, spare)
                    last.then_inc(s_mv, 1)

                def normalize(b):
                    wait(dve, s_rstd, b + 1)
                    wait(dve, s_xT, b)
                    for t in range(TPB):
                        last = dve.tensor_scalar(xn[:, t, :], x[:, bass.ds((b * TPB + t) * P, P)],
                                                 mv[:, t, 0:1], rstd[:, t:t + 1], ALU.subtract, ALU.mult)
                    last.then_inc(s_xn, 1)

                def split_x(b, par):
                    wait(dve, s_xh, b + 1)
                    dve.tensor_tensor(xl[:, par, :], T[:], xh[:, par, :].bitcast(F32), ALU.subtract)\
                       .then_inc(s_xl, 1)

                def gate(b, ch, n):
                    def first_of_equals(of, top, hot, m):
                        if m == 0:
                            return dve.tensor_reduce(top[:], of[:], AX, ALU.max)
                        if m == 1:
                            return dve.tensor_tensor(eq[:], of[:], bc(top), ALU.is_equal)
                        if m == 2:
                            return dve.tensor_tensor(cc[:], eq[:], rank[:], ALU.mult)
                        if m == 3:
                            return dve.tensor_reduce(cm[:], cc[:], AX, ALU.max)
                        return dve.tensor_tensor(hot[:], cc[:], bc(cm), ALU.is_equal)

                    if n == 0:
                        wait(dve, s_lg, b + 1)
                        ins = dve.tensor_copy(lg[:].rearrange("p t e -> p (t e)"), R[:, 0:TPB * E])
                        ch.step(ins)
                        return
                    ch.join()
                    if n == 1:
                        ins = dve.tensor_reduce(mx[:], lg[:], AX, ALU.max)
                    if n == 2:
                        dve.tensor_tensor(sh[:], lg[:], bc(mx), ALU.subtract).then_inc(s_sh, 1)
                        return
                    if n == 3:
                        wait(dve, s_ex, b + 1)
                        ins = dve.tensor_reduce(sm[:], ex[:], AX, ALU.add)
                    if n == 4:
                        ins = dve.reciprocal(rs[:], sm[:])
                    if n == 5:
                        ins = dve.tensor_tensor(gt[:], ex[:], bc(rs), ALU.mult)
                    if 6 <= n <= 10:
                        ins = first_of_equals(gt, top1, oh1, n - 6)
                    if n == 11:
                        ins = dve.scalar_tensor_tensor(gm[:], oh1[:], -2.0, gt[:], ALU.mult, ALU.add)
                    if 12 <= n <= 16:
                        ins = first_of_equals(gm, top2, oh2, n - 12)
                    if n == 17:
                        dve.tensor_tensor(dd[:], top2[:], top1[:], ALU.subtract).then_inc(s_dd, 1)
                        return
                    if n == 18:
                        wait(dve, s_tt, b + 1)
                        ins = dve.tensor_scalar(t1[:], tt[:], 1.0, None, ALU.add)
                    if n == 19:
                        ins = dve.reciprocal(wa[:], t1[:])
                    if n == 20:
                        ch.step(dve.tensor_tensor(wb[:], tt[:], wa[:], ALU.mult))
                        ins = dve.tensor_tensor(wtmp[:], oh1[:], bc(wa), ALU.mult)
                    if n == 21:
                        ins = dve.tensor_tensor(wsum[:], oh2[:], bc(wb), ALU.mult)
                    if n == 22:
                        ins = dve.tensor_tensor(wall[:], wsum[:], wtmp[:], ALU.add)
                    if n == 23:
                        wait(dve, s_wT, b)
                        ins = dve.tensor_copy(w16[:, :, 0:E].bitcast(F32R), wall[:])
                    if n == 24:
                        dve.tensor_tensor(w16[:, :, E:2 * E], wall[:], w16[:, :, 0:E], ALU.subtract)\
                           .then_inc(s_w, 1)
                        return
                    ch.step(ins)

                def update(b):
                    wait(dve, s_aT, b + 1)
                    xb = x[:, bass.ds(b * BLK, BLK)]
                    dve.scalar_tensor_tensor(xb, T[:], 0.5, xb, ALU.mult, ALU.add).then_inc(s_x, 1)

                def take(b, par, e):
                    q = (par + e) % 2
                    wait(dve, s_dn, JOBS * b + e + 1)
                    wait(dve, s_wbc, E * b + e + 1)
                    wait(dve, s_acc, 7 * b + (max(1, e - 2) if e >= 2 else 0))
                    dve.tensor_tensor(prod[:, e % 2, :], Y[:, q, :], wbc[:, e % 2, :], ALU.mult)\
                       .then_inc(s_yc, 1)

                def total(b, par):
                    wait(dve, s_dn, JOBS * (b + 1))
                    wait(dve, s_acc, 7 * (b + 1))
                    dve.scalar_tensor_tensor(accf[:], Y[:, (par + E) % 2, :], bs2[:], acc[:],
                                             ALU.add, ALU.add).then_inc(s_yc, 1)

                def run_block(b, par, first=False):
                    ch = Chain(dve, s_gch, GATED + CHAIN * b)
                    for j in range(JOBS):
                        q = (par + j) % 2
                        for k in range(KC):
                            n = NUP * b + KC * j + k
                            if k < KC - 1:
                                wait(dve, s_hh, 3 * JOBS * b + 3 * j + k + 1)
                            else:
                                wait(dve, s_raw, n + 1)
                                ch.step(dve.tensor_copy(hh[:, q, k, :], raw[:, k, :]))
                                ch.join()
                            if k == 0:
                                wait(dve, s_dn, JOBS * b + j - 1)
                            dve.tensor_tensor(hl[:, q, k, :], raw[:, k, :], hh[:, q, k, :].bitcast(F32),
                                              ALU.subtract).then_inc(s_hl, 1)
                            if j == 4 and k < 3:
                                gate(b + 1, ch, k)
                            if j >= 6:
                                gate(b + 1, ch, 3 + KC * (j - 6) + k)
                            for step in GATE.get((j, k), ()):
                                gate(b, ch, step)
                            if (j, k) == (0, 1) and not first:
                                total(b - 1, 1 - par)
                            if (j, k) == (2, 0) and not first:
                                update(b - 1)
                        if j == 0:
                            norm(b + 1, ch)
                        if j == 1:
                            normalize(b + 1)
                        if j == 2:
                            split_x(b + 1, 1 - par)
                        if j >= 2:
                            take(b, par, j - 2)
                    take(b, par, E - 1)
                    assert ch.n == CHAIN, ch.n

                GATE = {(0, 0): (15,), (0, 1): (16,), (0, 2): (17,), (1, 0): (18, 19), (1, 1): (20, 21),
                        (1, 2): (22, 23), (1, 3): (24,)}
                CHAIN, GATED = JOBS + 1 + 23, 15
                ch = Chain(dve, s_gch)
                norm(0, ch)
                dve.wait_ge(s_small, 16 * 8)
                dve.tensor_copy(wr1h[:], wr1s[:]).then_inc(s_pre, 1)
                dve.tensor_copy(be2h[:], be2s[:]).then_inc(s_pre, 1)
                dve.tensor_copy(sel[:], sels[:]).then_inc(s_pre, 1)
                dve.wait_ge(s_pre, 2)
                dve.tensor_tensor(wr1l[:], wr1s[:], wr1h[:].bitcast(F32), ALU.subtract).then_inc(s_pre, 1)
                dve.tensor_tensor(be2l[:], be2s[:], be2h[:].bitcast(F32), ALU.subtract).then_inc(s_pre, 1)
                normalize(0)
                split_x(0, 0)
                for n, (kind, j) in enumerate(pieces):
                    dve.wait_ge(s_wsc, n + 1)
                    dve.tensor_tensor((w1l, w2l)[kind][:, j, :], wst[:, n % NST, :],
                                      (w1h, w2h)[kind][:, j, :].bitcast(F32), ALU.subtract).then_inc(s_wsp, 1)
                for n in range(15):
                    gate(0, ch, n)
                assert ch.n == GATED
                run_block(0, 0, first=True)
                run_block(1, 1)
                with dve.Fori(1, NBLK // 2) as i:
                    run_block(i * 2, 0)
                    run_block(i * 2 + 1, 1)
                total(NBLK - 1, 1)
                update(NBLK - 1)

            @block.gpsimd
            def _(pool):
                def rstd_of(b):
                    wait(pool, s_mv, b + 1)
                    pool.tensor_tensor(veps[:], mv[:, :, 1], eps[:], ALU.add).then_inc(s_ve, 1)
                    wait(pool, s_ve, b + 1)
                    wait(pool, s_xn, b)
                    pool.tensor_tensor(rstd[:], veps[:], mhalf[:], ALU.pow).then_inc(s_rstd, 1)

                def exps(b):
                    wait(pool, s_sh, b + 1)
                    pool.tensor_tensor(ex[:], ebase[:], sh[:], ALU.pow).then_inc(s_ex, 1)

                def exp_second(b):
                    wait(pool, s_dd, b + 1)
                    pool.tensor_tensor(tt[:], ebase2[:], dd[:], ALU.pow).then_inc(s_tt, 1)

                def run_block(b, par):
                    exp_second(b)
                    rstd_of(b + 1)
                    for e in range(1, E):
                        if e == 3:
                            exps(b + 1)
                        wait(pool, s_yc, JOBS * b + e + 1)
                        if e > 1:
                            wait(pool, s_acc, 7 * b + e - 1)
                        src = prod[:, 0, :] if e == 1 else acc[:]
                        pool.tensor_tensor(acc[:], src, prod[:, e % 2, :], ALU.add).then_inc(s_acc, 1)

                pool.memset(ebase[:], float(np.exp(1.0)))
                pool.memset(ebase2[:], float(np.exp(0.5)))
                pool.memset(mhalf[:], -0.5).then_inc(s_cst, 1)
                pool.memset(eps[:], EPS).then_inc(s_cst, 1)
                pool.wait_ge(s_cst, 2)
                rstd_of(0)
                exps(0)
                run_block(0, 0)
                run_block(1, 1)
                with pool.Fori(1, NBLK // 2) as i:
                    run_block(i * 2, 0)
                    run_block(i * 2 + 1, 1)
        ph.clear()


def ternary_ffn(nc, tag, x, ident, w):
    KC = 4
    NPAIR = NBLK // 2
    NHID = 6 * KC
    NPROD = 8 * KC
    with ExitStack() as ctx:
        ph = Phase(nc, ctx, tag)
        sb, sem = ph.sb, ph.sem
        NW = 2 + KC + KC + 1
        wh, wl = sb("wh", [P, NW, 512], F32R), sb("wl", [P, NW, 512], F32R)
        wst = sb("wst", [P, 4, 512])
        scal = sb("scal", [P, 4 * KC + 1])
        mhalf = sb("mhalf", [P, TPB])
        stats, mv = sb("stats", [P, TPB, 6]), sb("mv", [P, TPB, 2])
        veps, rstd = sb("veps", [P, TPB]), sb("rstd", [P, TPB])
        eps, spare = sb("eps", [P, TPB]), sb("spare", [P, 1])
        xn = sb("xn", [P, TPB, P])
        xh, xl = sb("xh", [P, 2, BLK], F32R), sb("xl", [P, 2, BLK], F32R)
        raw, hf = sb("raw", [P, KC, BLK]), sb("hf", [P, KC, BLK])
        hh, hl = sb("hh", [P, 2, 2, KC, BLK], F32R), sb("hl", [P, 2, 2, KC, BLK], F32R)
        outT = sb("outT", [P, 2, BLK])

        U = ph.ps("U", [P, 4, BLK])
        Y = ph.ps("Y", [P, 2, BLK])
        T = ph.ps("T", [P, BLK])

        s_small = sem("small")
        s_wst = [sem(f"wst{i}") for i in range(4)]
        s_wsc, s_wsp = sem("wsc"), sem("wsp")
        s_cst = sem("cst")
        s_gch = sem("gch")
        s_mv, s_ve, s_rstd, s_xn = sem("mv"), sem("ve"), sem("rstd"), sem("xn")
        s_xT, s_xh, s_xl = sem("xT"), sem("xh"), sem("xl")
        s_up = sem("up")
        s_ua, s_ud = sem("ua"), sem("ud")
        s_raw = sem("raw")
        s_hh, s_hl = sem("hh"), sem("hl")
        s_y, s_yc = sem("y"), sem("yc")
        s_aT, s_x = sem("aT"), sem("x")

        order = [(s, a) for s in range(3) for a in range(2)]
        readers = []
        for s, a in order:
            for k in range(KC):
                readers += ["act", "dve"] if s == 0 else ["act"]
        first_prod = {}
        n = 0
        for s, a in order:
            first_prod[s, a] = n
            n += 2 * KC if s == 0 else KC
        ACT_READS, DVE_READS = readers.count("act"), readers.count("dve")

        def hid(s, a, k):
            return (2 * s + a) * KC + k

        def bank_free(eng, i, n):
            m = n - 4
            if m < 0:
                i, m = i - 1, m + NPROD
            who = readers[m]
            count = readers[:m + 1].count(who)
            if who == "act":
                wait(eng, s_ua, i * ACT_READS + count)
            else:
                wait(eng, s_ud, i * DVE_READS + count)

        with nc.Block() as block:
            @block.sync
            def _(sp):
                sp.dma_start(scal[:], w["scales"]).then_inc(s_small, 16)
                for n in range(NW):
                    if n >= 4:
                        sp.wait_ge(s_wsp, n - 3)
                    sp.dma_start(wst[:, n % 4, :], w["w"][n]).then_inc(s_wst[n % 4], 16)

            @block.tensor
            def _(pe):
                def passes(out, piece, c, a, rhs_h, rhs_l, start, stop):
                    c = slice(c * P, (c + 1) * P)
                    pe.matmul(out, wh[:, piece, c], rhs_h, start=start, stop=False)
                    pe.matmul(out, wl[:, piece, c], rhs_h, start=False, stop=False)
                    return pe.matmul(out, wh[:, piece, c], rhs_l, start=False, stop=stop)

                def stage(i, s, a):
                    if s == 0:
                        wait(pe, s_xh, 2 * i + a + 1)
                        wait(pe, s_xl, 2 * i + a + 1)
                    for k in range(KC):
                        if s == 0:
                            for v in range(2):
                                n = first_prod[s, a] + 2 * k + v
                                bank_free(pe, i, n)
                                passes(U[:, n % 4, :], v, k, a, xh[:, a, :], xl[:, a, :], True, True)\
                                    .then_inc(s_up, 1)
                        else:
                            n = first_prod[s, a] + k
                            bank_free(pe, i, n)
                            src = (s + 1) % 2
                            for c in range(KC):
                                wait(pe, s_hl, i * NHID + hid(s - 1, a, c) + 1)
                                mm = passes(U[:, n % 4, :], 2 + KC * (s - 1) + c, k, a, hh[:, a, src, c, :],
                                            hl[:, a, src, c, :], c == 0, c == KC - 1)
                            mm.then_inc(s_up, 1)

                def output(i, a):
                    wait(pe, s_yc, 2 * (i - 1) + a + 1)
                    for c in range(KC):
                        wait(pe, s_hl, i * NHID + hid(2, a, c) + 1)
                        mm = passes(Y[:, a, :], NW - 1, c, a, hh[:, a, 0, c, :], hl[:, a, 0, c, :],
                                    c == 0, c == KC - 1)
                    mm.then_inc(s_y, 1)

                def norm_T(i, a):
                    wait(pe, s_xn, 2 * i + a + 1)
                    if a == 0:
                        wait(pe, s_x, 2 * (i - 1))
                    else:
                        wait(pe, s_xl, 2 * i + 1)
                    for t in range(TPB):
                        mm = pe.transpose(T[:, t * P:(t + 1) * P], xn[:, t, :], ident[:])
                    mm.then_inc(s_xT, 1)

                def sum_T(i, a):
                    wait(pe, s_yc, 2 * i + a + 1)
                    if a == 0:
                        wait(pe, s_xl, 2 * (i + 1) + 2)
                    else:
                        wait(pe, s_x, 2 * i + 1)
                    for t in range(TPB):
                        mm = pe.transpose(T[:, t * P:(t + 1) * P], outT[:, a, t * P:(t + 1) * P], ident[:])
                    mm.then_inc(s_aT, 1)

                def pair(i, first=False):
                    for a in range(2):
                        if first and a == 0:
                            pe.wait_ge(s_wsp, 2)
                        stage(i, 0, a)
                        if not first:
                            sum_T(i - 1, a)
                    if first:
                        pe.wait_ge(s_wsp, NW)
                    for a in range(2):
                        stage(i, 1, a)
                        norm_T(i + 1, a)
                    stage(i, 2, 0)
                    stage(i, 2, 1)
                    output(i, 0)
                    output(i, 1)

                norm_T(0, 0)
                norm_T(0, 1)
                pair(0, first=True)
                with pe.Fori(1, NPAIR) as i:
                    pair(i)
                sum_T(NPAIR - 1, 0)
                sum_T(NPAIR - 1, 1)

            @block.scalar
            def _(act):
                def split_x(i, a):
                    wait(act, s_xT, 2 * i + a + 1)
                    wait(act, s_up, (i - 1) * NPROD + first_prod[0, a] + 2 * KC)
                    act.activation(xh[:, a, :], T[:], ACT.Copy).then_inc(s_xh, 1)

                def high(i, a, k):
                    wait(act, s_ud, i * DVE_READS + KC * a + k + 1)
                    act.activation(hh[:, a, 0, k, :], hf[:, k, :], ACT.Copy).then_inc(s_hh, 1)

                def stage(i, s, a):
                    for k in range(KC):
                        h = hid(s, a, k)
                        n = first_prod[s, a] + (2 * k if s == 0 else k)
                        sc = scal[:, (0, 2 * KC, 3 * KC)[s] + k:(0, 2 * KC, 3 * KC)[s] + k + 1]
                        wait(act, s_up, i * NPROD + n + 1)
                        wait(act, s_hl, i * NHID + h - 3)
                        if s == 0:
                            ins = act.activation(raw[:, k, :], U[:, n % 4, :], ACT.Silu, scale=sc)
                            ins.then_inc(s_ua, 1)
                            if k:
                                high(i, a, k - 1)
                        else:
                            act.activation(raw[:, k, :], U[:, n % 4, :], ACT.Gelu, scale=sc).then_inc(s_raw, 1)
                            act.activation(hh[:, a, s % 2, k, :], U[:, n % 4, :], ACT.Gelu, scale=sc)\
                               .then_inc(s_ua, 1)
                    if s == 0:
                        high(i, a, KC - 1)

                def output(i, a):
                    wait(act, s_y, 2 * i + a + 1)
                    wait(act, s_aT, 2 * (i - 1) + a + 1)
                    act.activation(outT[:, a, :], Y[:, a, :], ACT.Copy, scale=scal[:, 4 * KC:4 * KC + 1])\
                       .then_inc(s_yc, 1)

                def pair(i):
                    for a in range(2):
                        stage(i, 0, a)
                    for a in range(2):
                        stage(i, 1, a)
                        split_x(i + 1, a)
                    stage(i, 2, 0)
                    stage(i, 2, 1)
                    output(i, 0)
                    output(i, 1)

                split_x(0, 0)
                split_x(0, 1)
                for n in range(NW):
                    act.wait_ge(s_wst[n % 4], 16 * (n // 4 + 1))
                    act.activation(wh[:, n, :], wst[:, n % 4, :], ACT.Copy).then_inc(s_wsc, 1)
                act.wait_ge(s_small, 16)
                pair(0)
                with act.Fori(1, NPAIR) as i:
                    pair(i)

            @block.vector
            def _(dve):
                def norm(i, a, ch):
                    b = 2 * i + a
                    norm_stats(nc, dve, ch, lambda t: x[:, bass.ds((b * TPB + t) * P, P)], stats, mv, spare)\
                        .then_inc(s_mv, 1)
                    wait(dve, s_rstd, b + 1)
                    wait(dve, s_xT, b)
                    for t in range(TPB):
                        last = dve.tensor_scalar(xn[:, t, :], x[:, bass.ds((b * TPB + t) * P, P)],
                                                 mv[:, t, 0:1], rstd[:, t:t + 1], ALU.subtract, ALU.mult)
                    last.then_inc(s_xn, 1)

                def split_x(i, a):
                    wait(dve, s_xh, 2 * i + a + 1)
                    dve.tensor_tensor(xl[:, a, :], T[:], xh[:, a, :].bitcast(F32), ALU.subtract)\
                       .then_inc(s_xl, 1)

                def stage(i, s, a):
                    for k in range(KC):
                        h = hid(s, a, k)
                        if s == 0:
                            n = first_prod[s, a] + 2 * k
                            wait(dve, s_ua, i * ACT_READS + KC * a + k + 1)
                            wait(dve, s_up, i * NPROD + n + 2)
                            wait(dve, s_hl, i * NHID + h - 3)
                            dve.scalar_tensor_tensor(hf[:, k, :], U[:, (n + 1) % 4, :],
                                                     scal[:, KC + k:KC + k + 1], raw[:, k, :],
                                                     ALU.mult, ALU.mult).then_inc(s_ud, 1)
                            if k:
                                low(i, s, a, k - 1)
                        else:
                            low(i, s, a, k)
                    if s == 0:
                        low(i, s, a, KC - 1)

                def low(i, s, a, k):
                    if s == 0:
                        wait(dve, s_hh, i * 2 * KC + KC * a + k + 1)
                    else:
                        wait(dve, s_ua, i * ACT_READS + 2 * KC + (2 * (s - 1) + a) * KC + k + 1)
                    src = hf if s == 0 else raw
                    dve.tensor_tensor(hl[:, a, s % 2, k, :], src[:, k, :], hh[:, a, s % 2, k, :].bitcast(F32),
                                      ALU.subtract).then_inc(s_hl, 1)

                def update(i, a):
                    wait(dve, s_aT, 2 * i + a + 1)
                    xb = x[:, bass.ds((2 * i + a) * BLK, BLK)]
                    dve.scalar_tensor_tensor(xb, T[:], 0.5, xb, ALU.mult, ALU.add).then_inc(s_x, 1)

                def pair(i, first=False):
                    ch = Chain(dve, s_gch, 2 + 2 * i)
                    for a in range(2):
                        stage(i, 0, a)
                        if not first:
                            update(i - 1, a)
                    for a in range(2):
                        norm(i + 1, a, ch)
                        stage(i, 1, a)
                        split_x(i + 1, a)
                    stage(i, 2, 0)
                    stage(i, 2, 1)

                ch = Chain(dve, s_gch)
                norm(0, 0, ch)
                split_x(0, 0)
                norm(0, 1, ch)
                split_x(0, 1)
                for n in range(NW):
                    dve.wait_ge(s_wsc, n + 1)
                    dve.tensor_tensor(wl[:, n, :], wst[:, n % 4, :], wh[:, n, :].bitcast(F32), ALU.subtract)\
                       .then_inc(s_wsp, 1)
                dve.wait_ge(s_small, 16)
                pair(0, first=True)
                with dve.Fori(1, NPAIR) as i:
                    pair(i)
                update(NPAIR - 1, 0)
                update(NPAIR - 1, 1)

            @block.gpsimd
            def _(pool):
                def rstd_of(b):
                    wait(pool, s_mv, b + 1)
                    pool.tensor_tensor(veps[:], mv[:, :, 1], eps[:], ALU.add).then_inc(s_ve, 1)
                    wait(pool, s_ve, b + 1)
                    wait(pool, s_xn, b)
                    pool.tensor_tensor(rstd[:], veps[:], mhalf[:], ALU.pow).then_inc(s_rstd, 1)

                pool.memset(mhalf[:], -0.5).then_inc(s_cst, 1)
                pool.memset(eps[:], EPS).then_inc(s_cst, 1)
                pool.wait_ge(s_cst, 2)
                rstd_of(0)
                rstd_of(1)
                with pool.Fori(1, NPAIR + 1) as i:
                    rstd_of(2 * i)
                    rstd_of(2 * i + 1)
        ph.clear()
def mamba(nc, tag, x, ident, w):
    NS = 16
    DBC = 2 * 2 * NS
    DBL = DBC + 8
    HALF = 2
    NCH = SEQ // BLK
    TPS = SEQ // P
    PADW = 3
    PAIRS = 2 * NS * NCH
    UNITS = PAIRS * HALF
    PRE = 2 + 8
    with ExitStack() as ctx:
        ph = Phase(nc, ctx, tag)
        sb, sem = ph.sb, ph.sem
        wi = sb("wi", [P, 512])
        wih, wil = sb("wih", [P, 512], F32R), sb("wil", [P, 512], F32R)
        convw = sb("convw", [P, 2, HALF, 4])
        vecs = sb("vecs", [P, 3, 2, HALF])
        xpw = sb("xpw", [P, 2, HALF, DBL])
        dtw = sb("dtw", [DBL, 2, HALF, P])
        alog, aneg = sb("alog", [P, 2, HALF, NS]), sb("aneg", [P, 2, HALF, NS])
        wo = sb("wo", [P, HALF, P])
        sels = sb("sels", [DBC, 4, P])
        sel = sb("sel", [DBC, 2 * NS, P], F32R)
        mhalf, one = sb("mhalf", [P, TILES]), sb("one", [P, 1])
        stats, mv = sb("stats", [P, TILES, 6]), sb("mv", [P, TILES, 2])
        veps, rstd = sb("veps", [P, TILES]), sb("rstd", [P, TILES])
        xn = sb("xn", [P, TPS, P])
        xh, xl = sb("xh", [P, SEQ], F32R), sb("xl", [P, SEQ], F32R)
        xpad = sb("xpad", [P, HALF, SEQ + 2 * PADW])
        zs = sb("zs", [P, HALF, SEQ])
        xs = sb("xs", [P, 2, HALF, SEQ])
        dbl = sb("dbl", [DBL, 2, SEQ])
        bcs = sb("bcs", [DBC, 2, SEQ], F32R)
        dt, u = sb("dt", [P, 2, HALF, SEQ]), sb("u", [P, 2, HALF, SEQ])
        RING = 4
        dA, bx = sb("dA", [P, RING, BLK]), sb("bx", [P, RING, BLK])
        H, hc = sb("H", [P, RING, BLK]), sb("hc", [P, RING, BLK])
        cb = sb("cb", [P, RING, BLK])
        two = lambda t: t[:].rearrange("p (a b) c -> p a (b c)", a=2)
        ab, ee = two(dA)[:, 0, :], two(dA)[:, 1, :]
        ln, uu = two(bx)[:, 0, :], two(bx)[:, 1, :]
        rl, cv = two(H), two(hc)
        ys = sb("ys", [P, HALF, NCH, BLK])

        Y = ph.ps("Y", [P, 4, BLK])
        Bp = ph.ps("Bp", [P, 2, BLK])
        Cp = ph.ps("Cp", [P, BLK])
        O = ph.ps("O", [P, BLK])

        s_ld, s_sel = sem("ld"), sem("sel")
        s_cst, s_aexp, s_pre = sem("cst"), sem("aexp"), sem("pre")
        s_mv, s_ve, s_rstd = sem("mv"), sem("ve"), sem("rstd")
        s_gch = sem("gch")
        s_xn, s_pp = sem("xn"), sem("pp")
        s_xh, s_xl = sem("xh"), sem("xl")
        s_ip = sem("ip")
        s_cv, s_xs = sem("cv"), sem("xs")
        s_dbl, s_bcs = sem("dbl"), sem("bcs")
        s_ab, s_rl, s_ee, s_ln = sem("ab"), sem("rl"), sem("ee"), sem("ln")
        s_dt = sem("dt")
        s_B, s_C, s_cb = sem("B"), sem("C"), sem("cb")
        s_dA, s_bx, s_scan = sem("dA"), sem("bx"), sem("scan")
        s_hc, s_y = sem("hc"), sem("y")
        s_g = sem("g")
        s_o, s_x = sem("o"), sem("x")

        LOADS = ((wi[:], w["in_proj"]), (convw[:], w["conv_w"]), (vecs[:], w["vecs"]),
                 (xpw[:], w["x_proj"]), (dtw[:], w["dt_proj"]), (alog[:], w["A_log"]),
                 (wo[:], w["out_proj"]))
        NSEL = 2 * NS // 4
        units = []
        for d in range(2):
            for n in range(NS):
                for c in (range(NCH) if d == 0 else range(NCH - 1, -1, -1)):
                    for h in range(HALF):
                        units.append((d, n, c, h))

        def chunk(c):
            return slice(c * BLK, (c + 1) * BLK)

        with nc.Block() as block:
            @block.sync
            def _(sp):
                for dst, src in LOADS:
                    sp.dma_start(dst, src).then_inc(s_ld, 16)
                for k in range(NSEL):
                    if k:
                        sp.wait_ge(s_pre, k)
                    sp.dma_start(sels[:], w["bc_sel"][:, 4 * k:4 * k + 4, :]).then_inc(s_sel, 16)

            @block.tensor
            def _(pe):
                def xproj(i, d):
                    for c in range(NCH):
                        n = PRE + 6 * d + c
                        if c == 0:
                            wait(pe, s_xs, 4 * i + 2 * d + 2)
                            if d:
                                wait(pe, s_rl, 4 * i + 1)
                        for h in range(HALF):
                            mm = pe.matmul(Y[0:DBL, n % 4, :], xpw[:, d, h, :], xs[:, d, h, chunk(c)],
                                           start=h == 0, stop=h == 1)
                        mm.then_inc(s_pp, 1)

                def dtproj(i, d):
                    for h in range(HALF):
                        for c in range(NCH):
                            n = PRE + 6 * d + 2 + 2 * h + c
                            if c == 0:
                                wait(pe, s_dbl, 4 * i + 2 * d + 2)
                                if (d, h) == (1, 0):
                                    wait(pe, s_rl, 4 * i + 2)
                            pe.matmul(Y[:, n % 4, :], dtw[:, d, h, :], dbl[:, d, chunk(c)],
                                      start=True, stop=True).then_inc(s_pp, 1)

                def rows(i, q):
                    d, n, c, _ = units[2 * q]
                    Q = i * PAIRS + q
                    wait(pe, s_bx, 2 * (Q - 1))
                    pe.matmul(Bp[:, q % 2, :], sel[:, n, :], bcs[:, d, chunk(c)], start=True, stop=True)\
                      .then_inc(s_B, 1)
                    wait(pe, s_cb, Q)
                    pe.matmul(Cp[:], sel[:, NS + n, :], bcs[:, d, chunk(c)], start=True, stop=True)\
                      .then_inc(s_C, 1)

                def batch(i):
                    wait(pe, s_xn, i + 1)
                    for c in range(NCH):
                        for t in range(TPB):
                            mm = pe.transpose(Y[:, c, t * P:(t + 1) * P], xn[:, TPB * c + t, :], ident[:])
                        mm.then_inc(s_pp, 1)
                    for m in range(4):
                        for c in range(NCH):
                            n = 2 + 2 * m + c
                            wait(pe, s_xl, 2 * i + 2)
                            if n >= 6:
                                wait(pe, s_ip, 8 * i + n - 5)
                            f = slice(m * P, (m + 1) * P)
                            pe.matmul(Y[:, n % 4, :], wih[:, f], xh[:, chunk(c)], start=True, stop=False)
                            pe.matmul(Y[:, n % 4, :], wil[:, f], xh[:, chunk(c)], start=False, stop=False)
                            pe.matmul(Y[:, n % 4, :], wih[:, f], xl[:, chunk(c)], start=False, stop=True)\
                              .then_inc(s_pp, 1)
                    wait(pe, s_ip, 8 * i + 8)
                    for d in range(2):
                        xproj(i, d)
                        dtproj(i, d)
                    wait(pe, s_bcs, 2 * i + 2)
                    rows(i, 0)
                    rows(i, 1)
                    for q in range(PAIRS):
                        if q + 2 < PAIRS:
                            rows(i, q + 2)
                        for h in range(HALF):
                            g = 2 * q + h
                            d, n, c, _ = units[g]
                            wait(pe, s_hc, i * UNITS + g + 1)
                            pe.matmul(Y[:, 2 * c + h, :], ident[:], hc[:, g % RING, :],
                                      start=d == 0 and n == 0, stop=d == 1 and n == NS - 1).then_inc(s_y, 1)
                    for c in range(NCH):
                        if c:
                            wait(pe, s_x, NCH * i + c)
                        wait(pe, s_g, 4 * i + 2 * c + 2)
                        for t in range(TPB):
                            for h in range(HALF):
                                mm = pe.matmul(O[:, t * P:(t + 1) * P], ys[:, h, c, t * P:(t + 1) * P],
                                               wo[:, h, :], start=h == 0, stop=h == 1)
                        mm.then_inc(s_o, 1)

                pe.wait_ge(s_pre, NSEL + 2)
                batch(0)
                with pe.Fori(1, NBATCH) as i:
                    batch(i)

            @block.scalar
            def _(act):
                nc.scalar.preload_act_table_set("natural_log_exp_and_others")
                act.wait_ge(s_ld, 16 * len(LOADS))
                act.activation(aneg[:], alog[:], ACT.Exp).then_inc(s_aexp, 1)
                act.activation(wih[:], wi[:], ACT.Copy).then_inc(s_aexp, 1)
                act.wait_ge(s_cst, 3)

                def batch(i):
                    base = 22 * i
                    nc.scalar.preload_act_table_set("silu_and_others")
                    for c in range(NCH):
                        wait(act, s_pp, base + c + 1)
                        act.activation(xh[:, chunk(c)], Y[:, c, :], ACT.Copy).then_inc(s_xh, 1)
                    for m in range(4):
                        for c in range(NCH):
                            n = 2 + 2 * m + c
                            wait(act, s_pp, base + n + 1)
                            if m < 2:
                                act.activation(xpad[:, m, PADW + c * BLK:PADW + (c + 1) * BLK], Y[:, n % 4, :],
                                               ACT.Copy).then_inc(s_ip, 1)
                            else:
                                act.activation(zs[:, m - 2, chunk(c)], Y[:, n % 4, :], ACT.Silu)\
                                   .then_inc(s_ip, 1)
                    for k in range(4):
                        d, h = k // 2, k % 2
                        wait(act, s_cv, 4 * i + k + 1)
                        act.activation(xs[:, d, h, :], cv[:, k % 2, :], ACT.Silu, bias=vecs[:, 0, d, h:h + 1])\
                           .then_inc(s_xs, 1)
                    nc.scalar.preload_act_table_set("natural_log_exp_and_others")
                    for d in range(2):
                        for c in range(NCH):
                            n = PRE + 6 * d + c
                            wait(act, s_pp, base + n + 1)
                            act.activation(dbl[:, d, chunk(c)], Y[0:DBL, n % 4, :], ACT.Copy).then_inc(s_dbl, 1)
                        for h in range(HALF):
                            k = 2 * d + h
                            n = PRE + 6 * d + 2 + 2 * h
                            src = Y[:, n % 4:n % 4 + 2, :].rearrange("p a b -> p (a b)")
                            b = vecs[:, 1, d, h:h + 1]
                            wait(act, s_pp, base + n + 2)
                            wait(act, s_ee, 4 * i + k)
                            act.activation(ab, src, ACT.Abs, bias=b).then_inc(s_ab, 1)
                            wait(act, s_dt, 4 * i + k - 1)
                            act.activation(rl[:, k % 2, :], src, ACT.Relu, bias=b).then_inc(s_rl, 1)
                            wait(act, s_ab, 4 * i + k + 1)
                            wait(act, s_dt, 4 * i + k)
                            act.activation(ee, ab, ACT.Exp, scale=-1.0).then_inc(s_ee, 1)
                            wait(act, s_ee, 4 * i + k + 1)
                            act.activation(ln, ee, ACT.Ln, bias=one[:]).then_inc(s_ln, 1)
                    for g in range(UNITS):
                        d, n, c, h = units[g]
                        G, Q = i * UNITS + g, i * PAIRS + g // 2
                        if h == 0:
                            wait(act, s_C, Q + 1)
                            wait(act, s_hc, 2 * (Q - RING) + 2)
                            act.activation(cb[:, (g // 2) % RING, :], Cp[:], ACT.Copy).then_inc(s_cb, 1)
                        if g == 0:
                            wait(act, s_dt, 4 * i + 4)
                        wait(act, s_scan, G - RING + 1)
                        act.activation(dA[:, g % RING, :], dt[:, d, h, chunk(c)], ACT.Exp,
                                       scale=aneg[:, d, h, n:n + 1]).then_inc(s_dA, 1)

                batch(0)
                with act.Fori(1, NBATCH) as i:
                    batch(i)

            @block.vector
            def _(dve):
                dve.wait_ge(s_cst, 3)
                ch = Chain(dve, s_gch)
                for t in range(TILES):
                    last = dve.bn_stats(stats[:, t, :], x[:, t * P:(t + 1) * P])
                ch.step(last)
                ch.join()
                for t in range(TILES):
                    last = dve.bn_aggr(mv[:, t, :], stats[:, t, :])
                last.then_inc(s_mv, 1)
                dve.wait_ge(s_aexp, 2)
                for k in range(NSEL):
                    dve.wait_ge(s_sel, 16 * (k + 1))
                    dve.tensor_copy(sel[:, 4 * k:4 * k + 4, :], sels[:]).then_inc(s_pre, 1)
                dve.tensor_scalar(aneg[:], aneg[:], -1.0, None, ALU.mult).then_inc(s_pre, 1)
                dve.tensor_tensor(wil[:], wi[:], wih[:].bitcast(F32), ALU.subtract).then_inc(s_pre, 1)
                dve.wait_ge(s_rstd, 1)

                CONV, SPLIT, SOFT, GATE = 3, 1, 4, 2
                PER = 4 * CONV + 2 * SPLIT + 4 * SOFT + 4 * GATE

                def batch(i):
                    ch = Chain(dve, s_gch, 1 + PER * i)
                    for t in range(TPS):
                        last = dve.tensor_scalar(xn[:, t, :], x[:, bass.ds((i * TPS + t) * P, P)],
                                                 mv[:, bass.ds(i * TPS + t, 1), 0:1].rearrange("p a b -> p (a b)"),
                                                 rstd[:, bass.ds(i * TPS + t, 1)], ALU.subtract, ALU.mult)
                    last.then_inc(s_xn, 1)
                    for c in range(NCH):
                        wait(dve, s_xh, 2 * i + c + 1)
                        dve.tensor_tensor(xl[:, chunk(c)], Y[:, c, :], xh[:, chunk(c)].bitcast(F32),
                                          ALU.subtract).then_inc(s_xl, 1)
                    for k in range(4):
                        d, h = k // 2, k % 2
                        wait(dve, s_ip, 8 * i + 2 * h + 2)
                        wait(dve, s_xs, 4 * i + k - 1)
                        for s in range(4):
                            off = PADW - s if d == 0 else PADW + s
                            src = xpad[:, h, off:off + SEQ]
                            tap = convw[:, d, h, 3 - s:4 - s]
                            if s == 0:
                                ins = dve.tensor_scalar(cv[:, k % 2, :], src, tap, None, ALU.mult)
                            else:
                                ins = dve.scalar_tensor_tensor(cv[:, k % 2, :], src, tap, cv[:, k % 2, :],
                                                               ALU.mult, ALU.add)
                            if s < 3:
                                ch.step(ins)
                                ch.join()
                            else:
                                ins.then_inc(s_cv, 1)
                    for d in range(2):
                        wait(dve, s_dbl, 4 * i + 2 * d + 2)
                        ch.step(dve.tensor_copy(bcs[:, d, :], dbl[0:DBC, d, :]))
                        ch.join()
                        dve.tensor_tensor(bcs[32:64, d, :], dbl[32:64, d, :],
                                          bcs[32:64, d, :].bitcast(F32), ALU.subtract).then_inc(s_bcs, 1)
                        for h in range(HALF):
                            k = 2 * d + h
                            wait(dve, s_ee, 4 * i + k + 1)
                            ch.step(dve.tensor_scalar(uu, ee, 1.0, None, ALU.add))
                            ch.join()
                            ch.step(dve.scalar_tensor_tensor(uu, uu, 1.0, ee, ALU.subtract,
                                                             ALU.subtract))
                            ch.join()
                            wait(dve, s_ln, 4 * i + k + 1)
                            ch.step(dve.tensor_tensor(uu, ln, uu, ALU.subtract))
                            ch.join()
                            ch.step(dve.tensor_tensor(dt[:, d, h, :], uu, rl[:, k % 2, :], ALU.add))
                            ch.join()
                            dve.tensor_tensor(u[:, d, h, :], dt[:, d, h, :], xs[:, d, h, :], ALU.mult)\
                               .then_inc(s_dt, 1)
                    wait(dve, s_dt, 4 * i + 4)
                    for g in range(UNITS):
                        d, n, c, h = units[g]
                        G, Q = i * UNITS + g, i * PAIRS + g // 2
                        wait(dve, s_B, Q + 1)
                        dve.tensor_tensor(bx[:, g % RING, :], u[:, d, h, chunk(c)], Bp[:, (g // 2) % 2, :],
                                          ALU.mult).then_inc(s_bx, 1)
                        if g:
                            scan(i, g - 1)
                    scan(i, UNITS - 1)
                    for k in range(4):
                        c, h = k // 2, k % 2
                        if k == 0:
                            wait(dve, s_y, (i + 1) * UNITS)
                        ch.step(dve.scalar_tensor_tensor(ys[:, h, c, :], xs[:, 0, h, chunk(c)],
                                                         vecs[:, 2, 0, h:h + 1], Y[:, 2 * c + h, :],
                                                         ALU.mult, ALU.add))
                        ch.join()
                        ch.step(dve.scalar_tensor_tensor(ys[:, h, c, :], xs[:, 1, h, chunk(c)],
                                                         vecs[:, 2, 1, h:h + 1], ys[:, h, c, :],
                                                         ALU.mult, ALU.add))
                        ch.join()
                        dve.tensor_tensor(ys[:, h, c, :], ys[:, h, c, :], zs[:, h, chunk(c)], ALU.mult)\
                           .then_inc(s_g, 1)
                    for c in range(NCH):
                        wait(dve, s_o, NCH * i + c + 1)
                        xb = x[:, bass.ds(i * SEQ + c * BLK, BLK)]
                        dve.tensor_tensor(xb, xb, O[:], ALU.add).then_inc(s_x, 1)

                def scan(i, g):
                    d, n, c, h = units[g]
                    G = i * UNITS + g
                    wait(dve, s_dA, G + 1)
                    wait(dve, s_bx, G + 1)
                    wait(dve, s_hc, G - RING + 1)
                    s = g % RING
                    if c == (0 if d == 0 else NCH - 1):
                        init = 0.0
                    else:
                        wait(dve, s_scan, G - 1)
                        prev = (g - 2) % RING
                        init = H[:, prev, BLK - 1:BLK] if d == 0 else H[:, prev, 0:1]
                    if d == 0:
                        dve.tensor_tensor_scan(H[:, s, :], dA[:, s, :], bx[:, s, :], init, ALU.mult, ALU.add)\
                           .then_inc(s_scan, 1)
                    else:
                        dve.tensor_tensor_scan(H[:, s, ::-1], dA[:, s, ::-1], bx[:, s, ::-1], init,
                                               ALU.mult, ALU.add).then_inc(s_scan, 1)

                batch(0)
                with dve.Fori(1, NBATCH) as i:
                    batch(i)

            @block.gpsimd
            def _(pool):
                pool.memset(mhalf[:], -0.5).then_inc(s_cst, 1)
                pool.memset(one[:], 1.0).then_inc(s_cst, 1)
                pool.memset(xpad[:], 0.0).then_inc(s_cst, 1)
                pool.wait_ge(s_cst, 3)
                pool.wait_ge(s_mv, 1)
                pool.tensor_scalar(veps[:], mv[:, :, 1], EPS, None, ALU.add).then_inc(s_ve, 1)
                pool.wait_ge(s_ve, 1)
                pool.tensor_tensor(rstd[:], veps[:], mhalf[:], ALU.pow).then_inc(s_rstd, 1)

                def batch(i):
                    for g in range(UNITS):
                        G, Q = i * UNITS + g, i * PAIRS + g // 2
                        wait(pool, s_scan, G + 1)
                        wait(pool, s_cb, Q + 1)
                        wait(pool, s_y, G - RING + 1)
                        pool.tensor_tensor(hc[:, g % RING, :], H[:, g % RING, :], cb[:, (g // 2) % RING, :],
                                           ALU.mult).then_inc(s_hc, 1)

                batch(0)
                with pool.Fori(1, NBATCH) as i:
                    batch(i)
        ph.clear()
def attention(nc, tag, x, ident, w):
    GROUPS, GH = 4, 4
    HD = 8
    ROWS = P // GH
    NCH, TPS = SEQ // BLK, SEQ // P
    VW = HD + 1
    GV = 2 * GH * VW
    PR = 2 * GH
    SU = [(t, c, j) for t, c in ((3, 0), (2, 0), (0, 0), (1, 0), (4, 0), (5, 0), (5, 1), (6, 0), (4, 1), (6, 1),
                                 (7, 0), (7, 1)) for j in range(GH)]
    STEPS = [(c, kt) for c in range(NCH) for kt in range(TPB * (c + 1))]
    NS, NT = len(SU), len(STEPS)
    SPS = NS // NT
    DIAG = [v for v, (c, kt) in enumerate(STEPS) if kt >= TPB * c]

    def slot_uses(stage, g):
        if stage == "tail":
            return {3: ("norm", -1, 3, 1), 4: ("oT", -1, 0, 0), 5: ("oT", -1, 0, 1),
                    6: ("O", -1, 0, 0), 7: ("O", -1, 0, 1)}
        uses = {}
        if stage == "pre":
            uses.update({-7: ("xT", 0, 0, 0), -6: ("xT", 0, 0, 1), -5: ("Q", 0, 0, 0), -4: ("Q", 0, 0, 1),
                         -3: ("K", 0, 0, 0), -2: ("K", 0, 0, 1), -1: ("V", 0, 0, 0)})
        else:
            uses[1], uses[9] = ("max", 0, g, 1), ("norm", 0, g, 0)
            if g:
                uses[3] = ("norm", 0, g - 1, 1)
            elif stage != "first":
                uses[3] = ("norm", -1, 3, 1)
        if stage != "last" or g + 2 < GROUPS:
            rel, n = (g + 2) // GROUPS, (g + 2) % GROUPS
            uses.update({0: ("Q", rel, n, 0), 2: ("Q", rel, n, 1), 4: ("K", rel, n, 0), 5: ("K", rel, n, 1),
                         6: ("V", rel, n // 2, n % 2)})
        if stage != "last" or g + 1 < GROUPS:
            uses[7] = ("max", (g + 1) // GROUPS, (g + 1) % GROUPS, 0)
        if stage in ("mid", "last"):
            if g == 0:
                uses[8], uses[10], uses[11] = ("oT", -1, 0, 0), ("oT", -1, 0, 1), ("O", -1, 0, 0)
            if g == 1:
                uses[8] = ("O", -1, 0, 1)
        if stage in ("first", "mid") and g == 1:
            uses[10], uses[11] = ("xT", 1, 0, 0), ("xT", 1, 0, 1)
        return uses

    SLOTS = {"pre": [-1], "first": [0, 1, 2, 3], "mid": [0, 1, 2, 3], "last": [0, 1, 2, 3], "tail": [0]}
    LIST = {st: [(g, v, u) for g in gs for v, u in sorted(slot_uses(st, g).items())]
            for st, gs in SLOTS.items()}
    def copies(stage, g, v):
        uses = slot_uses(stage, g)
        use = uses.get(v - 2) if v < 0 else uses.get({9: 0, 10: 2}.get(v))
        return use if use and use[0] == "Q" else None

    WEIGHT = {"M": lambda k: 1, "D": lambda k: k not in ("Q", "K", "oT"), "A": lambda k: k in ("Q", "K", "oT"),
              "C": lambda k: {"norm": 1, "O": 2}.get(k, 0)}

    def total(w, stage, keep=lambda g, v: True):
        return sum(int(WEIGHT[w](u[0])) for g, v, u in LIST[stage] if keep(g, v))

    def base(w, stage, i):
        if stage == "pre":
            return 0
        n = total(w, "pre")
        if stage == "first":
            return n
        n += total(w, "first") + (i - 1) * total(w, "mid")
        return n if stage != "tail" else n - total(w, "mid") + total(w, "last")

    def through(w, stage, i, g, v):
        if g >= SLOTS[stage][0]:
            return base(w, stage, i) + total(w, stage, lambda gg, vv: (gg, vv) <= (g, v))
        prev = {"first": "pre", "mid": "mid", "last": "mid", "tail": "last"}[stage]
        last = SLOTS[prev][-1]
        return base(w, stage, i) - total(w, prev, lambda gg, vv: gg == last and vv > v)

    def steps(stage):
        return range(-7, NT) if stage == "pre" else range(9) if stage == "tail" else range(NT)

    def use_before(stage, g, v, back):
        v -= back
        if v < 0 and stage != "pre":
            g, v = g - 1, v + NT
            if g < SLOTS[stage][0]:
                return None
        use = slot_uses(stage, g).get(v)
        return use and (use, g, v)

    def has_exp(stage):
        return stage not in ("pre", "tail")

    def has_max(stage, g):
        return stage != "tail" and not (stage == "last" and g + 1 == GROUPS)

    def all_slots(slot, eng):
        slot("pre", 0, -1)
        for g in range(GROUPS):
            slot("first", 0, g)
        with eng.Fori(1, NBATCH - 1) as i:
            for g in range(GROUPS):
                slot("mid", i, g)
        for g in range(GROUPS):
            slot("last", NBATCH - 1, g)
        slot("tail", NBATCH, 0)

    with ExitStack() as ctx:
        ph = Phase(nc, ctx, tag)
        sb, sem = ph.sb, ph.sem
        NW = 2 * GROUPS
        wst = sb("wst", [P, NW, P])
        wh, wl = sb("wh", [P, NW, P], F32R), sb("wl", [P, NW, P], F32R)
        wvs = sb("wvs", [P, GROUPS * GH * VW])
        wvh, wvl = sb("wvh", [P, GROUPS * GH * VW], F32R), sb("wvl", [P, GROUPS * GH * VW], F32R)
        vb = sb("vb", [P, GROUPS * GH * VW])
        bias, scale, low = sb("bias", [P, NW]), sb("scale", [P, NW]), sb("low", [P, NW])
        bsc = sb("bsc", [P, NW])
        wo, bo = sb("wo", [P, P]), sb("bo", [P, P])
        mask = sb("mask", [P, P])
        idr, mneg = sb("idr", [P, P], F32R), sb("mneg", [P, P], F32R)
        stk = sb("stk", [P, 2, BLK])
        mhalf, zero = sb("mhalf", [P, TILES]), sb("zero", [P, TPB, GH])
        spare = sb("spare", [P, 4])
        stats, mv = sb("stats", [P, TILES, 6]), sb("mv", [P, TILES, 2])
        veps, rstd = sb("veps", [P, TILES]), sb("rstd", [P, TILES])
        xn = sb("xn", [P, TPS, P])
        xh, xl = sb("xh", [P, SEQ], F32R), sb("xl", [P, SEQ], F32R)
        qf, qh = sb("qf", [P, 2, BLK]), sb("qh", [P, 2, BLK], F32R)
        Q, K = sb("Q", [P, GROUPS * GH, SEQ], F32R), sb("K", [P, GROUPS, SEQ], F32R)
        V = sb("V", [P, TPS, GROUPS * GH, ROWS])
        mx, mx0, mxh = sb("mx", [P, 2, TPS, GH]), sb("mx0", [P, TPS - TPB, GH]), sb("mxh", [P, 2, TPB, GH], F32R)
        mt = sb("mt", [P, NCH, TPB, P])
        pt = sb("pt", [P, PR, BLK])
        ov = sb("ov", [P, NCH, BLK])
        rs = sb("rs", [P, TPB, GH])
        on = sb("on", [P, TPS, P])
        oT = sb("oT", [P, NCH, BLK])
        att, pos = sb("att", [P, BLK]), sb("pos", [P, BLK])

        W = ph.ps("W", [P, 5, BLK])
        PV = ph.ps("PV", [P, NCH, BLK])
        M = ph.ps("M", [P, BLK])

        s_ld, s_cst, s_wh, s_pre = sem("ld"), sem("cst"), sem("wh"), sem("pre")
        s_mv, s_ve, s_rstd = sem("mv"), sem("ve"), sem("rstd")
        s_gch, s_pch = sem("gch"), sem("pch")
        s_xn, s_xh = sem("xn"), sem("xh")
        s_M, s_Md, s_Ma = sem("M"), sem("Md"), sem("Ma")
        s_st, s_q = sem("st"), sem("q")
        s_S, s_max = sem("S"), sem("max")
        s_mx, s_sp = sem("mx"), sem("sp")
        s_T, s_exp, s_pm = sem("T"), sem("exp"), sem("pm")
        s_pv, s_ov = sem("pv"), sem("ov")

        LOADS = ((wst[:], w["w_qk"]), (wvs[:], w["w_v"]), (vb[:], w["b_v"]), (bias[:], w["b_qk"]),
                 (scale[:], w["scale"]), (low[:], w["low"]), (wo[:], w["w_out"]), (bo[:], w["b_out"]),
                 (mask[:], w["mask"]))

        def chunk(c):
            return slice(c * BLK, (c + 1) * BLK)

        def tile(t):
            return slice(t * P, (t + 1) * P)

        def head(j):
            return slice(ROWS * j, ROWS * (j + 1))

        with nc.Block() as block:
            @block.sync
            def _(sp):
                for dst, src in LOADS:
                    sp.dma_start(dst, src).then_inc(s_ld, 16)

            @block.tensor
            def _(pe):
                def passes(out, ah, al, bh, bl):
                    pe.matmul(out, ah, bh, start=True, stop=False)
                    pe.matmul(out, al, bh, start=False, stop=False)
                    return pe.matmul(out, ah, bl, start=False, stop=True)

                def max_unit(G, g, s):
                    t, c, j = SU[s]
                    n = G * NS + s
                    cols = min(BLK, (t + 1) * P - c * BLK)
                    diag = c == t // TPB
                    wait(pe, s_max, n - 1)
                    out = W[:, s % 2, 0:cols]
                    mm = pe.matmul(out, Q[:, g * GH + j, tile(t)], K[:, g, c * BLK:c * BLK + cols],
                                   start=True, stop=not diag)
                    if diag:
                        mm = pe.matmul(W[:, s % 2, cols - P:cols], idr[:], mneg[:], start=False, stop=True)
                    mm.then_inc(s_S, 1)

                def exp_unit(stage, i, g, v, j):
                    c, kt = STEPS[v]
                    r = max(0, kt - TPB * c)
                    if kt == 0 and j == 0:
                        wait(pe, s_Md, through("D", stage, i, g, 1) if c else through("D", stage, i, g - 1, 7))
                    u = v * GH + j
                    n = (i * GROUPS + g) * NT * GH + u
                    wait(pe, s_exp, n - 2)
                    pe.matmul(W[:, 2 + u % 3, 0:BLK - r * P], K[:, g, tile(kt)],
                              Q[:, g * GH + j, c * BLK + r * P:(c + 1) * BLK],
                              start=True, stop=True).then_inc(s_T, 1)

                def value_step(G, g, v):
                    c, kt = STEPS[v]
                    r = max(0, kt - TPB * c)
                    if kt == 0:
                        wait(pe, s_ov, 2 * (G - 1) + c + 1)
                    for j in range(GH):
                        u = v * GH + j
                        n = G * NT * GH + u
                        if v in DIAG:
                            wait(pe, s_pm, G * len(DIAG) + DIAG.index(v) + 1)
                        else:
                            wait(pe, s_exp, n + 1)
                        pe.matmul(PV[head(j), c, r * P:], V[:, kt, g * GH + j, :], pt[:, u % PR, 0:BLK - r * P],
                                  start=kt == 0, stop=kt == TPB * (c + 1) - 1).then_inc(s_pv, 1)

                def m_use(stage, i, g, v, use):
                    kind, rel, n, c = use
                    G = (i + rel) * GROUPS + n
                    wait(pe, s_Md, through("D", stage, i, g, v - 1))
                    wait(pe, s_Ma, through("A", stage, i, g, v - 1))
                    if kind in ("max", "norm", "xT", "oT"):
                        if kind == "max":
                            wait(pe, s_sp, 2 * G + c + 1)
                            src = [mt[:, c, t, :] for t in range(TPB)]
                        elif kind == "norm":
                            wait(pe, s_ov, 2 * G + c + 1)
                            src = [ov[:, c, tile(t)] for t in range(TPB)]
                        elif kind == "xT":
                            wait(pe, s_xn, i + rel + 1)
                            src = [xn[:, TPB * c + t, :] for t in range(TPB)]
                        else:
                            src = [on[:, TPB * c + t, :] for t in range(TPB)]
                        for t in range(TPB):
                            mm = pe.transpose(M[:, tile(t)], src[t], ident[:])
                    elif kind in ("Q", "K"):
                        k = n if kind == "Q" else GROUPS + n
                        mm = passes(M[:], wh[:, k, :], wl[:, k, :], xh[:, chunk(c)], xl[:, chunk(c)])
                    elif kind == "V":
                        f = slice(n * GV, (n + 1) * GV)
                        for t in range(TPB):
                            tt = tile(TPB * c + t)
                            mm = passes(M[:, t * GV:(t + 1) * GV], xh[:, tt], xl[:, tt],
                                        wvh[:, f], wvl[:, f])
                    else:
                        for t in range(TPB):
                            mm = pe.matmul(M[:, tile(t)], oT[:, c, tile(t)], wo[:], start=True, stop=True)
                    mm.then_inc(s_M, 1)

                def slot(stage, i, g):
                    G = i * GROUPS + g
                    uses = slot_uses(stage, g)
                    for v in steps(stage):
                        for j in range(GH):
                            if has_exp(stage):
                                exp_unit(stage, i, g, v, j)
                            if has_max(stage, g) and v >= 0:
                                if v == 0 and j == 0:
                                    wait(pe, s_q, 2 * G + 4)
                                    wait(pe, s_st, 4 * G + 8)
                                max_unit(G + 1, (g + 1) % GROUPS, SPS * v + j)
                            if j == 1 and v > 0 and has_exp(stage):
                                value_step(G, g, v - 1)
                            if j == 1 and v == 0 and stage != "pre" and (stage, g) != ("first", 0):
                                value_step(G - 1, (g - 1) % GROUPS, NT - 1)
                        if v in uses:
                            m_use(stage, i, g, v, uses[v])

                pe.wait_ge(s_pre, 3)
                all_slots(slot, pe)

            @block.scalar
            def _(act):
                act.wait_ge(s_ld, 16 * len(LOADS))
                act.activation(wh[:], wst[:], ACT.Copy).then_inc(s_wh, 1)
                act.activation(wvh[:], wvs[:], ACT.Copy).then_inc(s_wh, 1)
                act.wait_ge(s_pre, 4)

                def exp_unit(i, g, v, j):
                    c, kt = STEPS[v]
                    r = max(0, kt - TPB * c)
                    u = v * GH + j
                    n = (i * GROUPS + g) * NT * GH + u
                    wait(act, s_T, n + 1)
                    wait(act, s_pv, n - PR + 1)
                    act.activation(pt[:, u % PR, 0:BLK - r * P], W[:, 2 + u % 3, 0:BLK - r * P],
                                   ACT.Exp).then_inc(s_exp, 1)

                def take_out(stage, i, g, c):
                    G = i * GROUPS + g - c
                    wait(act, s_pv, (G * NT + (TPB if c == 0 else NT)) * GH)
                    if not (isinstance(G, int) and G == 0):
                        wait(act, s_M, through("M", stage, i, g - 1, 9 if c == 0 else 3))
                    act.activation(ov[:, c, :], PV[:, c, :], ACT.Copy).then_inc(s_ov, 1)

                def m_read(stage, i, g, v, use, j):
                    kind, rel, n, c = use
                    if kind in ("Q", "K") and j < 2:
                        G = (i + rel) * GROUPS + n
                        m, k = (c, n) if kind == "Q" else (2 + c, GROUPS + n)
                        if j == 0:
                            wait(act, s_M, through("M", stage, i, g, v))
                            wait(act, s_st, 4 * G + m - 1)
                            act.activation(qf[:, m % 2, :], M[:], ACT.Identity,
                                           bias=bsc[:, k:k + 1], scale=scale[:, k:k + 1])
                        else:
                            act.activation(qh[:, m % 2, :], M[:], ACT.Identity,
                                           bias=bsc[:, k:k + 1], scale=scale[:, k:k + 1]).then_inc(s_Ma, 1)
                    if kind in ("xT", "oT") and j == 0:
                        wait(act, s_M, through("M", stage, i, g, v))
                        if kind == "xT":
                            act.activation(xh[:, chunk(c)], M[:], ACT.Copy).then_inc(s_xh, 1)
                        else:
                            act.activation(oT[:, c, :], M[:], ACT.Copy).then_inc(s_Ma, 1)

                def queries(i, use, j):
                    kind, rel, n, c = use
                    G = (i + rel) * GROUPS + n
                    if j == 0:
                        wait(act, s_st, 4 * G + c + 1)
                    last = act.activation(Q[head(j), n * GH + j, chunk(c)], stk[head(j), c, :], ACT.Copy)
                    if j == GH - 1:
                        last.then_inc(s_q, 1)

                def slot(stage, i, g):
                    for v in steps(stage):
                        for j in range(GH):
                            if has_exp(stage):
                                exp_unit(i, g, v, j)
                            before = use_before(stage, g, v, 1)
                            if before:
                                m_read(stage, i, before[1], before[2], before[0], j)
                            copied = copies(stage, g, v)
                            if copied:
                                queries(i, copied, j)
                        if v == 5 and has_exp(stage):
                            take_out(stage, i, g, 0)
                        if v == 1 and stage != "pre" and (stage, g) != ("first", 0):
                            take_out(stage, i, g, 1)

                all_slots(slot, act)

            @block.vector
            def _(dve):
                dve.wait_ge(s_ld, 16 * len(LOADS))
                ch = Chain(dve, s_gch)
                for t in range(TILES):
                    last = dve.bn_stats(stats[:, t, :], x[:, tile(t)])
                ch.step(last)
                ch.join()
                for t in range(TILES):
                    last = dve.bn_aggr(mv[:, t, :], stats[:, t, :])
                last.then_inc(s_mv, 1)
                dve.tensor_tensor(bsc[:], bias[:], scale[:], ALU.mult)
                dve.tensor_copy(idr[:], ident[:])
                dve.tensor_copy(mneg[:], mask[:]).then_inc(s_pre, 1)
                dve.wait_ge(s_wh, 2)
                dve.tensor_tensor(wl[:], wst[:], wh[:].bitcast(F32), ALU.subtract).then_inc(s_pre, 1)
                dve.tensor_tensor(wvl[:], wvs[:], wvh[:].bitcast(F32), ALU.subtract).then_inc(s_pre, 1)
                dve.memset(Q[:].bitcast(F32), 0.0).then_inc(s_pre, 1)
                dve.wait_ge(s_cst, 4)
                dve.wait_ge(s_rstd, 1)
                def max_unit(G, g, s):
                    t, c, j = SU[s]
                    n = G * NS + s
                    wait(dve, s_S, n + 1)
                    if s == 0:
                        wait(dve, s_sp, 2 * (G - 1))
                    last = c == t // TPB
                    dst = mx[:, g % 2, t, j:j + 1] if last else mx0[:, t - TPB, j:j + 1]
                    dve.tensor_reduce(dst, W[:, s % 2, 0:min(BLK, (t + 1) * P - c * BLK)], AX, ALU.max)\
                       .then_inc(s_max, 1)

                def both_chunks(G, g, t):
                    n = max(s for s in range(NS) if SU[s][0] == t)
                    wait(dve, s_max, G * NS + n + 1)
                    dve.tensor_tensor(mx[:, g % 2, t, :], mx[:, g % 2, t, :], mx0[:, t - TPB, :], ALU.max)\
                       .then_inc(s_mx, 1)

                def m_read(stage, i, g, v, use, ch, j):
                    kind, rel, n, c = use
                    if kind in ("Q", "K", "oT"):
                        return
                    last = None
                    if j == 0:
                        wait(dve, s_M, through("M", stage, i, g, v))
                    if kind == "xT" and j == 0:
                        wait(dve, s_xh, 2 * (i + rel) + c + 1)
                        last = dve.tensor_tensor(xl[:, chunk(c)], M[:], xh[:, chunk(c)].bitcast(F32), ALU.subtract)
                    if kind == "max":
                        q = Q[head(j), n * GH + j, chunk(c)]
                        ins = dve.tensor_tensor(q, q.bitcast(F32), M[head(j), :], ALU.add)
                        if j == GH - 1:
                            last = ins
                    if kind == "norm":
                        m4 = M[:].rearrange("p (t j r) -> p t j r", t=TPB, j=GH)
                        if j == 0:
                            ch.step(dve.reciprocal(rs[:], m4[:, :, :, HD]))
                        if j == 1:
                            ch.join()
                            out = on[:, TPB * c:TPB * (c + 1), n * GH * HD:(n + 1) * GH * HD]
                            last = dve.tensor_tensor(out.rearrange("p t (j d) -> p t j d", j=GH),
                                                     m4[:, :, :, 0:HD],
                                                     rs[:].unsqueeze(3).broadcast_to((P, TPB, GH, HD)), ALU.mult)
                    if kind == "V" and j == 0:
                        last = dve.tensor_tensor(V[:, TPB * c:TPB * (c + 1), n * 2 * GH:(n + 1) * 2 * GH, 0:VW],
                                                 M[:, 0:TPB * GV].rearrange("p (t h e) -> p t h e", t=TPB, e=VW),
                                                 vb[:, n * GV:(n + 1) * GV].rearrange("p (h e) -> p h e", e=VW)
                                                 .unsqueeze(1).broadcast_to((P, TPB, 2 * GH, VW)), ALU.add)
                    if kind == "O":
                        xb = x[:, bass.ds((i + rel) * SEQ + c * BLK, BLK)]
                        if j == 0:
                            ch.step(dve.tensor_tensor(att[:].rearrange("p (t f) -> p t f", t=TPB),
                                                      M[:].rearrange("p (t f) -> p t f", t=TPB),
                                                      bo[:].unsqueeze(1).broadcast_to((P, TPB, P)), ALU.add))
                        if j == 1:
                            ch.join()
                            ch.step(dve.scalar_tensor_tensor(pos[:], att[:], 0.0, xb, ALU.max, ALU.add))
                        if j == 2:
                            ch.join()
                            last = dve.scalar_tensor_tensor(xb, att[:], 0.0, pos[:], ALU.min, ALU.add)
                    if last is not None:
                        last.then_inc(s_Md, 1)

                def stack(stage, i, g, v, use):
                    kind, rel, n, c = use
                    G = (i + rel) * GROUPS + n
                    m, k = (c, n) if kind == "Q" else (2 + c, GROUPS + n)
                    wait(dve, s_Ma, through("A", stage, i, g, v))
                    if kind == "Q":
                        wait(dve, s_q, 2 * (G - 1) + c + 1)
                        out = stk[:, c, :]
                    else:
                        out = K[:, n, chunk(c)]
                    dve.scalar_tensor_tensor(out, qh[:, m % 2, :].bitcast(F32), low[:, k:k + 1],
                                             qf[:, m % 2, :], ALU.mult, ALU.add).then_inc(s_st, 1)

                def normalize(i):
                    for t in range(TPS):
                        last = dve.tensor_scalar(xn[:, t, :], x[:, bass.ds((i * TPS + t) * P, P)],
                                                 mv[:, bass.ds(i * TPS + t, 1), 0:1].rearrange("p a b -> p (a b)"),
                                                 rstd[:, bass.ds(i * TPS + t, 1)], ALU.subtract, ALU.mult)
                    last.then_inc(s_xn, 1)

                def slot(stage, i, g):
                    G = i * GROUPS + g
                    if g == SLOTS[stage][0]:
                        chain[0] = Chain(dve, s_gch, 1 + base("C", stage, i))
                    if stage == "pre":
                        normalize(0)
                    for v in steps(stage):
                        before = use_before(stage, g, v, 1)
                        for j in range(GH):
                            s = SPS * v + j
                            if has_max(stage, g) and v >= 0:
                                max_unit(G + 1, (g + 1) % GROUPS, s)
                                if j == 0 and s and SU[s - 1][1] == 1:
                                    both_chunks(G + 1, (g + 1) % GROUPS, SU[s - 1][0])
                            if before:
                                m_read(stage, i, before[1], before[2], before[0], chain[0], j)
                        if before and before[0][0] in ("Q", "K"):
                            stack(stage, i, before[1], before[2], before[0])
                        if v == 8 and g == 1 and stage in ("first", "mid"):
                            normalize(i + 1)
                    if has_max(stage, g):
                        both_chunks(G + 1, (g + 1) % GROUPS, TPS - 1)

                chain = [None]
                all_slots(slot, dve)

            @block.gpsimd
            def _(pool):
                pool.memset(mhalf[:], -0.5).then_inc(s_cst, 1)
                pool.memset(V[:], 0.0).then_inc(s_cst, 1)
                pool.memset(mt[:], 0.0).then_inc(s_cst, 1)
                pool.memset(zero[:], 0.0).then_inc(s_cst, 1)
                pool.wait_ge(s_cst, 4)
                pool.wait_ge(s_mv, 1)
                pool.tensor_scalar(veps[:], mv[:, :, 1], EPS, None, ALU.add).then_inc(s_ve, 1)
                pool.wait_ge(s_ve, 1)
                pool.tensor_tensor(rstd[:], veps[:], mhalf[:], ALU.pow).then_inc(s_rstd, 1)

                def split_max(stage, i, slot, G, g, c):
                    if c == 0:
                        wait(pool, s_max, G * NS + TPB * GH)
                    else:
                        wait(pool, s_mx, (G + 1) * TPB)
                    if not (isinstance(G, int) and G == 0):
                        wait(pool, s_M, through("M", stage, i, slot - 1, 1 if c else 7))
                    src = mx[:, g % 2, TPB * c:TPB * (c + 1), :]
                    m4 = mt[:, c, :, :].rearrange("p t (j r) -> p t j r", j=GH)
                    pool.tensor_tensor(mxh[:, c, :, :], src, zero[:], ALU.add).then_inc(s_pch, 1)
                    wait(pool, s_pch, 2 * G + c + 1)
                    high = mxh[:, c, :, :].bitcast(F32)
                    pool.tensor_tensor(m4[:, :, :, 3 * HD], zero[:], high, ALU.subtract)
                    pool.tensor_tensor(m4[:, :, :, 3 * HD + 1], high, src, ALU.subtract).then_inc(s_sp, 1)

                def mask_step(i, g, v):
                    wait(pool, s_exp, ((i * GROUPS + g) * NT + v + 1) * GH)
                    pool.tensor_tensor(spare[:, DIAG.index(v) % 4:DIAG.index(v) % 4 + 1], zero[:, 0, 0:1], zero[:, 0, 0:1],
                                       ALU.add)
                    d = pt[:, (v % 2) * GH:(v % 2 + 1) * GH, 0:P]
                    pool.affine_select(out=d, in_=d, compare_op=ALU.is_ge, fill=0.0, base=0,
                                       pattern=[[0, GH], [1, P]], channel_multiplier=-1).then_inc(s_pm, 1)

                def slot(stage, i, g):
                    G = i * GROUPS + g
                    if has_exp(stage):
                        split_max(stage, i, g, G, g, 1)
                        for v in DIAG[:TPB]:
                            mask_step(i, g, v)
                    if has_max(stage, g):
                        split_max(stage, i, g, G + 1, (g + 1) % GROUPS, 0)
                    if has_exp(stage):
                        for v in DIAG[TPB:]:
                            mask_step(i, g, v)

                all_slots(slot, pool)
        ph.clear()
def macaron_program(nc, hidden, identity, out, moe, mam, tern, att):
    PAD = 2 * TPB
    with ExitStack() as ctx:
        x = ctx.enter_context(nc.sbuf_tensor("x", [P, (TILES + PAD) * P], F32))
        ident = ctx.enter_context(nc.sbuf_tensor("ident", [P, P], F32))
        s_load = ctx.enter_context(nc.semaphore("load"))
        s_store = ctx.enter_context(nc.semaphore("store"))
        x_tiles = x[:, 0:TOKENS].rearrange("p (t c) -> p t c", t=TILES)

        with nc.Block() as block:
            @block.sync
            def _(sp):
                sp.dma_start(x_tiles, hidden.rearrange("b (t p) c -> p (b t) c", p=P)).then_inc(s_load, 16)
                sp.dma_start(ident[:], identity).then_inc(s_load, 16)
                sp.wait_ge(s_load, 32)

            @block.gpsimd
            def _(pool):
                pool.memset(x[:, TOKENS:], 0.0)

        moe_ffn(nc, "m0", x, ident, moe)
        mamba(nc, "a0", x, ident, mam)
        moe_ffn(nc, "m1", x, ident, moe)
        ternary_ffn(nc, "t0", x, ident, tern)
        attention(nc, "a1", x, ident, att)
        ternary_ffn(nc, "t1", x, ident, tern)

        with nc.Block() as block:
            @block.sync
            def _(sp):
                sp.dma_start(out.rearrange("b (t p) c -> p (b t) c", p=P), x_tiles).then_inc(s_store, 16)
                sp.wait_ge(s_store, 16)


def stacked(a, parts):
    return a.reshape(parts, P, *a.shape[1:]).swapaxes(0, 1)


def moe_layout(inp):
    g = lambda n: inp["L0_ffn_" + n]
    E, H, HID = g("be2").shape[0], g("Wr1").shape[1], g("Ws1").shape[1]
    wr1, wr2, br1 = np.zeros((P, P), np.float32), np.zeros((P, E), np.float32), np.zeros((P, 1), np.float32)
    wr1[:, :H] = g("Wr1")
    wr2[:H] = g("Wr2")
    wr2[H] = g("br2")
    br1[:H, 0] = g("br1")
    br1[H] = 1
    b1 = np.concatenate([g("be1"), g("bs1")[None]])
    w2 = np.concatenate([g("We2"), g("Ws2")[None]])
    sel = np.zeros((2, E, E, P), np.float32)
    for e in range(E):
        sel[:, e, e] = 1
    return {
        "wr1": wr1, "wr2": wr2, "br1": br1,
        "b1": b1.reshape(E + 1, HID // P, P).transpose(2, 0, 1),
        "bs2": g("bs2").reshape(P, 1),
        "be2": np.concatenate([g("be2"), g("be2")]),
        "w1": np.concatenate([g("We1"), g("Ws1")[None]]),
        "w2": w2.reshape(E + 1, HID // P, P, P).transpose(0, 2, 1, 3).reshape(E + 1, P, HID),
        "route_sel": sel.reshape(2 * E, E, P),
        "rank": np.broadcast_to(E - np.arange(E, dtype=np.float32), (P, TPB, E)),
    }


def mamba_layout(inp):
    g = lambda n: inp["L0_attn_" + n]
    both = lambda n: np.stack([g(n + "f"), g(n + "r")])
    ns, rank = g("A_log_f").shape[1], g("dt_proj_w_f").shape[1]
    dbc = 4 * ns
    b, c = np.arange(rank, rank + ns), np.arange(rank + ns, rank + 2 * ns)
    rows = np.concatenate([b, c, b, c, np.arange(rank)])
    dtw = np.zeros((dbc + rank, 2, 2, P), np.float32)
    dtw[dbc:] = both("dt_proj_w_").transpose(2, 0, 1).reshape(rank, 2, 2, P)
    sel = np.zeros((2, 2 * ns, 2 * ns, P), np.float32)
    for n in range(2 * ns):
        sel[:, n, n] = 1
    halves = lambda a: a.reshape(2, 2, P, -1).transpose(2, 0, 1, 3)
    return {
        "in_proj": g("in_proj_w").T,
        "conv_w": halves(both("conv_w_")),
        "vecs": np.stack([halves(both(n))[..., 0] for n in ("conv_b_", "dt_proj_b_", "D_")], 1),
        "x_proj": both("x_proj_w_")[:, rows].reshape(2, dbc + rank, 2, P).transpose(3, 0, 2, 1),
        "dt_proj": dtw,
        "A_log": halves(both("A_log_")),
        "out_proj": stacked(g("out_proj_w").T, 2),
        "bc_sel": sel.reshape(dbc, 2 * ns, P),
    }


def ternary_layout(inp):
    g = lambda n: inp["L1_ffn_" + n]
    square = lambda n: g(n).T.reshape(4, P, 4 * P)
    w3 = stacked(g("w3_w").T, 4).reshape(1, P, 4 * P)
    return {
        "w": np.concatenate([g("w1_w").T[None], g("w2_w").T[None], square("h1_w"), square("h2_w"), w3]),
        "scales": np.concatenate([g(n).reshape(-1, P).T for n in ("w1_s", "w2_s", "h1_s", "h2_s", "w3_s")], 1),
    }


def attention_layout(inp):
    g = lambda n: inp["L1_attn_" + n]
    w_in, b_in = g("w_in"), g("b_in")
    HEADS, HD, GH, ROWS = 16, 8, 4, 32
    GROUPS = HEADS // GH
    wqk = np.zeros((P, 2, GROUPS, GH, ROWS), np.float32)
    bqk, low = np.zeros((2, GROUPS, GH, ROWS), np.float32), np.zeros((2, GROUPS, GH, ROWS), np.float32)
    scale = np.ones((2, GROUPS, GH, ROWS), np.float32)
    for kind in range(2):
        w = w_in[kind * P:(kind + 1) * P].T.reshape(P, GROUPS, GH, HD)
        b = b_in[kind * P:(kind + 1) * P].reshape(GROUPS, GH, HD)
        for part in range(3):
            wqk[:, kind, :, :, part * HD:(part + 1) * HD] = w
            bqk[kind, :, :, part * HD:(part + 1) * HD] = b
    low[0, :, :, HD:2 * HD] = -1
    low[1, :, :, 2 * HD:3 * HD] = -1
    bqk[1, :, :, 3 * HD:3 * HD + 2] = 1
    scale[0] = np.float32(1.0 / np.sqrt(HD))
    wv, bv = np.zeros((P, HEADS, HD + 1), np.float32), np.ones((HEADS, HD + 1), np.float32)
    wv[:, :, :HD] = w_in[2 * P:].T.reshape(P, HEADS, HD)
    bv[:, :HD] = b_in[2 * P:].reshape(HEADS, HD)
    cols = lambda a: a.reshape(2 * GROUPS, P).T
    return {
        "w_qk": wqk.reshape(P, 2 * GROUPS, P), "b_qk": cols(bqk), "scale": cols(scale), "low": cols(low),
        "w_v": wv.reshape(P, -1), "b_v": np.broadcast_to(bv.reshape(1, -1), (P, HEADS * (HD + 1))),
        "w_out": g("w_out").T, "b_out": np.broadcast_to(g("b_out"), (P, P)),
        "mask": np.triu(np.full((P, P), -1e30, np.float32), 1),
    }


def kernel(**inputs):
    import concourse.bacc as bacc
    from concourse.bass_utils import run_bass_kernel_spmd

    inp = {k: np.asarray(v) for k, v in inputs.items()}
    nc = bacc.Bacc("TRN2", target_bir_lowering=False, num_devices=1)
    arrays = {}

    def tensor(name, a):
        arrays[name] = np.ascontiguousarray(a)
        return nc.dram_tensor(name, a.shape, mybir.dt.from_np(a.dtype), kind="ExternalInput").ap()

    hidden = tensor("hidden", inp["L0_attn_hidden_states"])
    identity = tensor("identity", np.eye(P, dtype=np.float32))
    groups = [{k: tensor(f"{tag}_{k}", a) for k, a in layout(inp).items()}
              for tag, layout in (("moe", moe_layout), ("mamba", mamba_layout),
                                  ("ternary", ternary_layout), ("attention", attention_layout))]
    out = nc.dram_tensor("out", (NBATCH, SEQ, P), F32, kind="ExternalOutput").ap()
    macaron_program(nc, hidden, identity, out, *groups)
    return run_bass_kernel_spmd(nc, [arrays], core_ids=[0]).results[0]["out"]
```

```python
from contextlib import ExitStack

import numpy as np

import concourse.bass as bass
from concourse import mybir

F32 = mybir.dt.float32
F32R = mybir.dt.float32r
ACT = mybir.ActivationFunctionType
ALU = mybir.AluOpType
AX = mybir.AxisListType.X

P = 128
NBATCH, SEQ = 4, 1024
TOKENS = NBATCH * SEQ
TILES = TOKENS // P
BLK = 512
NBLK = TOKENS // BLK
TPB = BLK // P
EPS = 1e-5


def wait(eng, sem, value):
    if not isinstance(value, int) or value > 0:
        eng.wait_ge(sem, value)


class Chain:

    def __init__(self, eng, sem, base=0):
        self.eng, self.sem, self.base, self.n = eng, sem, base, 0

    def step(self, ins):
        self.n += 1
        ins.then_inc(self.sem, 1)
        return ins

    def join(self):
        wait(self.eng, self.sem, self.base + self.n)


class Phase:

    def __init__(self, nc, ctx, tag):
        self.nc, self.ctx, self.tag, self.sems = nc, ctx, tag, []

    def sb(self, name, shape, dt=F32):
        return self.ctx.enter_context(self.nc.sbuf_tensor(f"{self.tag}_{name}", shape, dt))

    def ps(self, name, shape, dt=F32):
        return self.ctx.enter_context(self.nc.psum_tensor(f"{self.tag}_{name}", shape, dt))

    def sem(self, name):
        s = self.ctx.enter_context(self.nc.semaphore(f"{self.tag}_{name}"))
        self.sems.append(s)
        return s

    def clear(self):
        with self.nc.Block() as block:
            @block.gpsimd
            def _(pool):
                for s in self.sems:
                    pool.sem_clear(s)


def norm_stats(nc, dve, chain, x_tile, stats, mv, spare):
    n = mv.shape[1]
    for t in range(n):
        last = dve.bn_stats(stats[:, t, :], x_tile(t))
    chain.step(last)
    chain.join()
    dve.tensor_copy(spare[:], stats[:, 0, 0:1])
    for t in range(n):
        last = dve.bn_aggr(mv[:, t, :], stats[:, t, :])
    return last


def moe_ffn(nc, tag, x, ident, w):
    E = 8
    JOBS = E + 1
    KC = 4
    NUP = JOBS * KC
    with ExitStack() as ctx:
        ph = Phase(nc, ctx, tag)
        sb, sem = ph.sb, ph.sem
        w1h, w1l = sb("w1h", [P, JOBS, 512], F32R), sb("w1l", [P, JOBS, 512], F32R)
        w2h, w2l = sb("w2h", [P, JOBS, 512], F32R), sb("w2l", [P, JOBS, 512], F32R)
        NST = 4
        wst = sb("wst", [P, NST, 512])
        wr1s = sb("wr1s", [P, P])
        wr1h, wr1l = sb("wr1h", [P, P], F32R), sb("wr1l", [P, P], F32R)
        wr2 = sb("wr2", [P, E])
        br1 = sb("br1", [P, 1])
        b1 = sb("b1", [P, JOBS, KC])
        bs2 = sb("bs2", [P, 1])
        be2s = sb("be2s", [2 * E, P])
        be2h, be2l = sb("be2h", [2 * E, P], F32R), sb("be2l", [2 * E, P], F32R)
        sels = sb("sels", [2 * E, E, P])
        sel = sb("sel", [2 * E, E, P], F32R)
        rank = sb("rank", [P, TPB, E])
        ebase, ebase2, mhalf = sb("ebase", [P, TPB, E]), sb("ebase2", [P, TPB]), sb("mhalf", [P, TPB])

        stats, mv = sb("stats", [P, TPB, 6]), sb("mv", [P, TPB, 2])
        veps, rstd = sb("veps", [P, TPB]), sb("rstd", [P, TPB])
        eps, spare = sb("eps", [P, TPB]), sb("spare", [P, 1])
        xn = sb("xn", [P, TPB, P])
        xh, xl = sb("xh", [P, 2, BLK], F32R), sb("xl", [P, 2, BLK], F32R)
        r1 = sb("r1", [P, BLK])
        NRAW = 4
        raw = sb("raw", [P, NRAW, BLK])
        hh, hl = sb("hh", [P, 2, KC, BLK], F32R), sb("hl", [P, 2, KC, BLK], F32R)
        wts = sb("wts", [2 * E, BLK], F32R)
        wbc = sb("wbc", [P, 2, BLK])
        prod = sb("prod", [P, 2, BLK])
        acc, accf = sb("acc", [P, BLK]), sb("accf", [P, BLK])
        g8 = lambda n: sb(n, [P, TPB, E])
        g1 = lambda n: sb(n, [P, TPB])
        lg, sh, ex, gt, eq, cc, oh1, gm, oh2, wsum, wtmp, wall = map(g8, (
            "lg", "sh", "ex", "gt", "eq", "cc", "oh1", "gm", "oh2", "wsum", "wtmp", "wall"))
        mx, sm, rs, top1, cm, top2, dd, tt, t1, wa, wb = map(g1, (
            "mx", "sm", "rs", "top1", "cm", "top2", "dd", "tt", "t1", "wa", "wb"))
        w16 = sb("w16", [P, TPB, 2 * E])

        U = ph.ps("U", [P, 4, BLK])
        Y = ph.ps("Y", [P, 2, BLK])
        R = ph.ps("R", [P, BLK])
        T = ph.ps("T", [P, BLK])

        s_small = sem("small")
        s_wst = [sem(f"wst{i}") for i in range(NST)]
        s_wsp = sem("wsp")
        s_wsc = sem("wsc")
        s_cst = sem("cst")
        s_pre = sem("pre")
        s_mv = sem("mv")
        s_ve = sem("ve")
        s_rstd = sem("rstd")
        s_xn = sem("xn")
        s_xT = sem("xT")
        s_xh, s_xl = sem("xh"), sem("xl")
        s_r1p, s_r1 = sem("r1p"), sem("r1")
        s_lg = sem("lg")
        s_gch = sem("gch")
        s_sh, s_ex = sem("sh"), sem("ex")
        s_dd, s_tt = sem("dd"), sem("tt")
        s_w = sem("w")
        s_wT, s_wTs = sem("wT"), sem("wTs")
        s_bc, s_wbc = sem("bc"), sem("wbc")
        s_up = sem("up")
        s_raw, s_hh = sem("raw"), sem("hh")
        s_hl = sem("hl")
        s_dn = sem("dn")
        s_yc = sem("yc")
        s_acc = sem("acc")
        s_aT, s_x = sem("aT"), sem("x")

        pieces = [(kind, j) for j in range(JOBS) for kind in (0, 1)]
        AHEAD = 4

        with nc.Block() as block:
            @block.sync
            def _(sp):
                for dst, src in ((wr1s[:], w["wr1"]), (wr2[:], w["wr2"]), (br1[:], w["br1"]),
                                 (b1[:], w["b1"]), (bs2[:], w["bs2"]), (be2s[:], w["be2"]),
                                 (sels[:], w["route_sel"]), (rank[:], w["rank"])):
                    sp.dma_start(dst, src).then_inc(s_small, 16)
                for n, (kind, j) in enumerate(pieces):
                    if n >= NST:
                        sp.wait_ge(s_wsp, n - NST + 1)
                    src = (w["w1"], w["w2"])[kind][j]
                    sp.dma_start(wst[:, n % NST, :], src).then_inc(s_wst[n % NST], 16)

            @block.tensor
            def _(pe):
                def up(b, par, j, first=False):
                    if first:
                        pe.wait_ge(s_wsp, 2 * j + 1)
                    for k in range(KC):
                        n = NUP * b + KC * j + k
                        if k < KC - 1:
                            wait(pe, s_hh, 3 * JOBS * b + 3 * j + k + 1 - 3)
                        else:
                            wait(pe, s_raw, n - 3)
                        c = slice(k * P, (k + 1) * P)
                        pe.matmul(U[:, k, :], w1h[:, j, c], xh[:, par, :], start=True, stop=False)
                        pe.matmul(U[:, k, :], w1l[:, j, c], xh[:, par, :], start=False, stop=False)
                        pe.matmul(U[:, k, :], w1h[:, j, c], xl[:, par, :], start=False, stop=True)\
                          .then_inc(s_up, 1)

                def down(b, par, j, first=False):
                    if first:
                        pe.wait_ge(s_wsp, 2 * j + 2)
                    q = (par + j) % 2
                    wait(pe, s_yc, JOBS * b + j - 1)
                    for k in range(KC):
                        pe.wait_ge(s_hl, NUP * b + KC * j + k + 1)
                        c = slice(k * P, (k + 1) * P)
                        pe.matmul(Y[:, q, :], w2h[:, j, c], hh[:, q, k, :], start=(k == 0), stop=False)
                        pe.matmul(Y[:, q, :], w2l[:, j, c], hh[:, q, k, :], start=False, stop=False)
                        last = k == KC - 1 and j < E
                        mm = pe.matmul(Y[:, q, :], w2h[:, j, c], hl[:, q, k, :], start=False, stop=last)
                    if j == E:
                        pe.matmul(Y[:, q, :], be2h[:], wts[:], start=False, stop=False)
                        mm = pe.matmul(Y[:, q, :], be2l[:], wts[:], start=False, stop=True)
                    mm.then_inc(s_dn, 1)

                def norm_T(b):
                    pe.wait_ge(s_xn, b + 1)
                    for t in range(TPB):
                        mm = pe.transpose(T[:, t * P:(t + 1) * P], xn[:, t, :], ident[:])
                    mm.then_inc(s_xT, 1)

                def sum_T(b):
                    pe.wait_ge(s_yc, JOBS * (b + 1))
                    for t in range(TPB):
                        mm = pe.transpose(T[:, t * P:(t + 1) * P], accf[:, t * P:(t + 1) * P], ident[:])
                    mm.then_inc(s_aT, 1)

                def bcast(b, e):
                    wait(pe, s_wbc, E * b + e)
                    pe.matmul(R[:], sel[:, e, :], wts[:], start=True, stop=True).then_inc(s_bc, 1)

                def router(b, par):
                    pe.wait_ge(s_xh, b + 1)
                    pe.wait_ge(s_xl, b + 1)
                    wait(pe, s_wbc, E * b - 6)
                    pe.matmul(R[:], wr1h[:], xh[:, par, :], start=True, stop=False)
                    pe.matmul(R[:], wr1l[:], xh[:, par, :], start=False, stop=False)
                    pe.matmul(R[:], wr1h[:], xl[:, par, :], start=False, stop=True).then_inc(s_r1p, 1)

                def logits(b):
                    pe.wait_ge(s_r1, b + 1)
                    for t in range(TPB):
                        mm = pe.matmul(R[:, t * E:(t + 1) * E], r1[:, t * P:(t + 1) * P], wr2[:],
                                       start=True, stop=True)
                    mm.then_inc(s_lg, 1)

                def run_block(b, par, first=False):
                    up(b, par, 0, first)
                    up(b, par, 1, first)
                    down(b, par, 0, first)
                    if not first:
                        sum_T(b - 1)
                    up(b, par, 2, first)
                    pe.wait_ge(s_w, b + 1)
                    wait(pe, s_x, b)
                    for t in range(TPB):
                        mm = pe.transpose(T[0:2 * E, t * P:(t + 1) * P], w16[:, t, :], ident[:])
                    mm.then_inc(s_wT, 1)
                    pe.wait_ge(s_wTs, b + 1)
                    bcast(b, 0)
                    norm_T(b + 1)
                    down(b, par, 1, first)
                    for j in range(3, JOBS):
                        if j == 4:
                            router(b + 1, 1 - par)
                        up(b, par, j, first)
                        if j == 4:
                            logits(b + 1)
                            down(b, par, j - 1, first)
                            pe.wait_ge(s_sh, b + 2)
                        bcast(b, j - 2)
                        if j != 4:
                            down(b, par, j - 1, first)
                    bcast(b, E - 1)
                    down(b, par, E, first)

                pe.wait_ge(s_pre, 5)
                norm_T(0)
                router(0, 0)
                logits(0)
                run_block(0, 0, first=True)
                run_block(1, 1)
                with pe.Fori(1, NBLK // 2) as i:
                    run_block(i * 2, 0)
                    run_block(i * 2 + 1, 1)
                pe.wait_ge(s_xh, NBLK + 1)
                pe.wait_ge(s_xl, NBLK + 1)
                sum_T(NBLK - 1)

            @block.scalar
            def _(act):
                def split_x(b, par):
                    act.wait_ge(s_xT, b + 1)
                    wait(act, s_up, NUP * (b - 1))
                    act.activation(xh[:, par, :], T[:], ACT.Copy).then_inc(s_xh, 1)

                def bcast(b, e):
                    act.wait_ge(s_bc, E * b + e + 1)
                    wait(act, s_yc, JOBS * b + e - 1 if e >= 2 else JOBS * b)
                    act.activation(wbc[:, e % 2, :], R[:], ACT.Copy).then_inc(s_wbc, 1)

                def router(b):
                    act.wait_ge(s_r1p, b + 1)
                    wait(act, s_lg, b)
                    act.activation(r1[:], R[:], ACT.Relu, bias=br1[:]).then_inc(s_r1, 1)

                def high(n):
                    kind, j = pieces[n]
                    act.wait_ge(s_wst[n % NST], 16 * (n // NST + 1))
                    act.activation((w1h, w2h)[kind][:, j, :], wst[:, n % NST, :], ACT.Copy).then_inc(s_wsc, 1)

                def run_block(b, par, first=False):
                    for j in range(JOBS):
                        q = (par + j) % 2
                        for k in range(KC):
                            n = NUP * b + KC * j + k
                            act.wait_ge(s_up, n + 1)
                            wait(act, s_hl, n - 3)
                            act.activation(raw[:, k, :], U[:, k, :], ACT.Silu, bias=b1[:, j, k:k + 1])\
                               .then_inc(s_raw, 1)
                            if k < KC - 1:
                                if k == 0:
                                    wait(act, s_dn, JOBS * b + j - 1)
                                act.activation(hh[:, q, k, :], U[:, k, :], ACT.Silu,
                                               bias=b1[:, j, k:k + 1]).then_inc(s_hh, 1)
                            if first and k % 2 and 2 * j + k // 2 + AHEAD < len(pieces):
                                high(2 * j + k // 2 + AHEAD)
                        if j == 2:
                            act.wait_ge(s_wT, b + 1)
                            wait(act, s_dn, JOBS * b)
                            act.activation(wts[:], T[0:2 * E, :], ACT.Copy).then_inc(s_wTs, 1)
                        if j >= 2:
                            bcast(b, j - 2)
                        if j == 2:
                            split_x(b + 1, 1 - par)
                        if j == 3:
                            router(b + 1)
                    bcast(b, E - 1)

                act.wait_ge(s_pre, 5)
                split_x(0, 0)
                router(0)
                for n in range(AHEAD):
                    high(n)
                run_block(0, 0, first=True)
                run_block(1, 1)
                with act.Fori(1, NBLK // 2) as i:
                    run_block(i * 2, 0)
                    run_block(i * 2 + 1, 1)

            @block.vector
            def _(dve):
                def bc(a):
                    return a[:].rearrange("p (t o) -> p t o", o=1).broadcast_to([P, TPB, E])

                def norm(b, ch):
                    last = norm_stats(nc, dve, ch, lambda t: x[:, bass.ds((b * TPB + t) * P, P)], stats, mv, spare)
                    last.then_inc(s_mv, 1)

                def normalize(b):
                    dve.wait_ge(s_rstd, b + 1)
                    wait(dve, s_xT, b)
                    for t in range(TPB):
                        last = dve.tensor_scalar(xn[:, t, :], x[:, bass.ds((b * TPB + t) * P, P)],
                                                 mv[:, t, 0:1], rstd[:, t:t + 1], ALU.subtract, ALU.mult)
                    last.then_inc(s_xn, 1)

                def split_x(b, par):
                    dve.wait_ge(s_xh, b + 1)
                    dve.tensor_tensor(xl[:, par, :], T[:], xh[:, par, :].bitcast(F32), ALU.subtract)\
                       .then_inc(s_xl, 1)

                def gate(b, ch, n):
                    def first_of_equals(of, top, hot, m):
                        if m == 0:
                            return dve.tensor_reduce(top[:], of[:], AX, ALU.max)
                        if m == 1:
                            return dve.tensor_tensor(eq[:], of[:], bc(top), ALU.is_equal)
                        if m == 2:
                            return dve.tensor_tensor(cc[:], eq[:], rank[:], ALU.mult)
                        if m == 3:
                            return dve.tensor_reduce(cm[:], cc[:], AX, ALU.max)
                        return dve.tensor_tensor(hot[:], cc[:], bc(cm), ALU.is_equal)

                    if n == 0:
                        dve.wait_ge(s_lg, b + 1)
                        ins = dve.tensor_copy(lg[:].rearrange("p t e -> p (t e)"), R[:, 0:TPB * E])
                        ch.step(ins)
                        return
                    ch.join()
                    if n == 1:
                        ins = dve.tensor_reduce(mx[:], lg[:], AX, ALU.max)
                    if n == 2:
                        dve.tensor_tensor(sh[:], lg[:], bc(mx), ALU.subtract).then_inc(s_sh, 1)
                        return
                    if n == 3:
                        dve.wait_ge(s_ex, b + 1)
                        ins = dve.tensor_reduce(sm[:], ex[:], AX, ALU.add)
                    if n == 4:
                        ins = dve.reciprocal(rs[:], sm[:])
                    if n == 5:
                        ins = dve.tensor_tensor(gt[:], ex[:], bc(rs), ALU.mult)
                    if 6 <= n <= 10:
                        ins = first_of_equals(gt, top1, oh1, n - 6)
                    if n == 11:
                        ins = dve.scalar_tensor_tensor(gm[:], oh1[:], -2.0, gt[:], ALU.mult, ALU.add)
                    if 12 <= n <= 16:
                        ins = first_of_equals(gm, top2, oh2, n - 12)
                    if n == 17:
                        dve.tensor_tensor(dd[:], top2[:], top1[:], ALU.subtract).then_inc(s_dd, 1)
                        return
                    if n == 18:
                        dve.wait_ge(s_tt, b + 1)
                        ins = dve.tensor_scalar(t1[:], tt[:], 1.0, None, ALU.add)
                    if n == 19:
                        ins = dve.reciprocal(wa[:], t1[:])
                    if n == 20:
                        ch.step(dve.tensor_tensor(wb[:], tt[:], wa[:], ALU.mult))
                        ins = dve.tensor_tensor(wtmp[:], oh1[:], bc(wa), ALU.mult)
                    if n == 21:
                        ins = dve.tensor_tensor(wsum[:], oh2[:], bc(wb), ALU.mult)
                    if n == 22:
                        ins = dve.tensor_tensor(wall[:], wsum[:], wtmp[:], ALU.add)
                    if n == 23:
                        wait(dve, s_wT, b)
                        ins = dve.tensor_copy(w16[:, :, 0:E].bitcast(F32R), wall[:])
                    if n == 24:
                        dve.tensor_tensor(w16[:, :, E:2 * E], wall[:], w16[:, :, 0:E], ALU.subtract)\
                           .then_inc(s_w, 1)
                        return
                    ch.step(ins)

                def update(b):
                    dve.wait_ge(s_aT, b + 1)
                    xb = x[:, bass.ds(b * BLK, BLK)]
                    dve.scalar_tensor_tensor(xb, T[:], 0.5, xb, ALU.mult, ALU.add).then_inc(s_x, 1)

                def take(b, par, e):
                    q = (par + e) % 2
                    dve.wait_ge(s_dn, JOBS * b + e + 1)
                    dve.wait_ge(s_wbc, E * b + e + 1)
                    wait(dve, s_acc, 7 * b + (max(1, e - 2) if e >= 2 else 0))
                    dve.tensor_tensor(prod[:, e % 2, :], Y[:, q, :], wbc[:, e % 2, :], ALU.mult)\
                       .then_inc(s_yc, 1)

                def total(b, par):
                    dve.wait_ge(s_dn, JOBS * (b + 1))
                    dve.wait_ge(s_acc, 7 * (b + 1))
                    dve.scalar_tensor_tensor(accf[:], Y[:, (par + E) % 2, :], bs2[:], acc[:],
                                             ALU.add, ALU.add).then_inc(s_yc, 1)

                def low(n):
                    kind, j = pieces[n]
                    dve.wait_ge(s_wsc, n + 1)
                    dve.tensor_tensor((w1l, w2l)[kind][:, j, :], wst[:, n % NST, :],
                                      (w1h, w2h)[kind][:, j, :].bitcast(F32), ALU.subtract).then_inc(s_wsp, 1)

                def run_block(b, par, first=False):
                    ch = Chain(dve, s_gch, GATED + CHAIN * b)
                    for j in range(JOBS):
                        q = (par + j) % 2
                        for k in range(KC):
                            n = NUP * b + KC * j + k
                            if k < KC - 1:
                                dve.wait_ge(s_hh, 3 * JOBS * b + 3 * j + k + 1)
                            else:
                                dve.wait_ge(s_raw, n + 1)
                                ch.step(dve.tensor_copy(hh[:, q, k, :], raw[:, k, :]))
                                ch.join()
                            if k == 0:
                                wait(dve, s_dn, JOBS * b + j - 1)
                            dve.tensor_tensor(hl[:, q, k, :], raw[:, k, :], hh[:, q, k, :].bitcast(F32),
                                              ALU.subtract).then_inc(s_hl, 1)
                            if first and k % 2 and 2 * j + k // 2 + AHEAD < len(pieces):
                                low(2 * j + k // 2 + AHEAD)
                            if j == 4 and k < 3:
                                gate(b + 1, ch, k)
                            if j >= 6:
                                gate(b + 1, ch, 3 + KC * (j - 6) + k)
                            for step in GATE.get((j, k), ()):
                                gate(b, ch, step)
                            if (j, k) == (0, 1) and not first:
                                total(b - 1, 1 - par)
                            if (j, k) == (2, 0) and not first:
                                update(b - 1)
                        if j == 0:
                            norm(b + 1, ch)
                        if j == 1:
                            normalize(b + 1)
                        if j == 2:
                            split_x(b + 1, 1 - par)
                        if j >= 2:
                            take(b, par, j - 2)
                    take(b, par, E - 1)
                    assert ch.n == CHAIN, ch.n

                GATE = {(0, 0): (15,), (0, 1): (16,), (0, 2): (17,), (1, 0): (18, 19), (1, 1): (20, 21),
                        (1, 2): (22, 23), (1, 3): (24,)}
                CHAIN, GATED = JOBS + 1 + 23, 15
                ch = Chain(dve, s_gch)
                norm(0, ch)
                dve.wait_ge(s_small, 16 * 8)
                dve.tensor_copy(wr1h[:], wr1s[:]).then_inc(s_pre, 1)
                dve.tensor_copy(be2h[:], be2s[:]).then_inc(s_pre, 1)
                dve.tensor_copy(sel[:], sels[:]).then_inc(s_pre, 1)
                dve.wait_ge(s_pre, 2)
                dve.tensor_tensor(wr1l[:], wr1s[:], wr1h[:].bitcast(F32), ALU.subtract).then_inc(s_pre, 1)
                dve.tensor_tensor(be2l[:], be2s[:], be2h[:].bitcast(F32), ALU.subtract).then_inc(s_pre, 1)
                normalize(0)
                split_x(0, 0)
                for n in range(AHEAD):
                    low(n)
                for n in range(15):
                    gate(0, ch, n)
                assert ch.n == GATED
                run_block(0, 0, first=True)
                run_block(1, 1)
                with dve.Fori(1, NBLK // 2) as i:
                    run_block(i * 2, 0)
                    run_block(i * 2 + 1, 1)
                total(NBLK - 1, 1)
                update(NBLK - 1)

            @block.gpsimd
            def _(pool):
                def rstd_of(b):
                    pool.wait_ge(s_mv, b + 1)
                    pool.tensor_tensor(veps[:], mv[:, :, 1], eps[:], ALU.add).then_inc(s_ve, 1)
                    pool.wait_ge(s_ve, b + 1)
                    wait(pool, s_xn, b)
                    pool.tensor_tensor(rstd[:], veps[:], mhalf[:], ALU.pow).then_inc(s_rstd, 1)

                def exps(b):
                    pool.wait_ge(s_sh, b + 1)
                    pool.tensor_tensor(ex[:], ebase[:], sh[:], ALU.pow).then_inc(s_ex, 1)

                def exp_second(b):
                    pool.wait_ge(s_dd, b + 1)
                    pool.tensor_tensor(tt[:], ebase2[:], dd[:], ALU.pow).then_inc(s_tt, 1)

                def run_block(b, par):
                    exp_second(b)
                    rstd_of(b + 1)
                    for e in range(1, E):
                        if e == 3:
                            exps(b + 1)
                        pool.wait_ge(s_yc, JOBS * b + e + 1)
                        if e > 1:
                            pool.wait_ge(s_acc, 7 * b + e - 1)
                        src = prod[:, 0, :] if e == 1 else acc[:]
                        pool.tensor_tensor(acc[:], src, prod[:, e % 2, :], ALU.add).then_inc(s_acc, 1)

                pool.memset(ebase[:], float(np.exp(1.0)))
                pool.memset(ebase2[:], float(np.exp(0.5)))
                pool.memset(mhalf[:], -0.5).then_inc(s_cst, 1)
                pool.memset(eps[:], EPS).then_inc(s_cst, 1)
                pool.wait_ge(s_cst, 2)
                rstd_of(0)
                exps(0)
                run_block(0, 0)
                run_block(1, 1)
                with pool.Fori(1, NBLK // 2) as i:
                    run_block(i * 2, 0)
                    run_block(i * 2 + 1, 1)
        ph.clear()


def ternary_ffn(nc, tag, x, ident, w):
    KC = 4
    NPAIR = NBLK // 2
    NHID = 6 * KC
    NPROD = 8 * KC
    with ExitStack() as ctx:
        ph = Phase(nc, ctx, tag)
        sb, sem = ph.sb, ph.sem
        NW = 2 + KC + KC + 1
        wh, wl = sb("wh", [P, NW, 512], F32R), sb("wl", [P, NW, 512], F32R)
        wst = sb("wst", [P, 4, 512])
        scal = sb("scal", [P, 4 * KC + 1])
        mhalf = sb("mhalf", [P, TPB])
        stats, mv = sb("stats", [P, TPB, 6]), sb("mv", [P, TPB, 2])
        veps, rstd = sb("veps", [P, TPB]), sb("rstd", [P, TPB])
        eps, spare = sb("eps", [P, TPB]), sb("spare", [P, 1])
        xn = sb("xn", [P, TPB, P])
        xh, xl = sb("xh", [P, 2, BLK], F32R), sb("xl", [P, 2, BLK], F32R)
        raw, hf = sb("raw", [P, KC, BLK]), sb("hf", [P, KC, BLK])
        hh, hl = sb("hh", [P, 2, 2, KC, BLK], F32R), sb("hl", [P, 2, 2, KC, BLK], F32R)
        outT = sb("outT", [P, 2, BLK])

        U = ph.ps("U", [P, 4, BLK])
        Y = ph.ps("Y", [P, 2, BLK])
        T = ph.ps("T", [P, BLK])

        s_small = sem("small")
        s_wst = [sem(f"wst{i}") for i in range(4)]
        s_wsc, s_wsp = sem("wsc"), sem("wsp")
        s_cst = sem("cst")
        s_gch = sem("gch")
        s_mv, s_ve, s_rstd, s_xn = sem("mv"), sem("ve"), sem("rstd"), sem("xn")
        s_xT, s_xh, s_xl = sem("xT"), sem("xh"), sem("xl")
        s_up = sem("up")
        s_ua, s_ud = sem("ua"), sem("ud")
        s_raw = sem("raw")
        s_hh, s_hl = sem("hh"), sem("hl")
        s_y, s_yc = sem("y"), sem("yc")
        s_aT, s_x = sem("aT"), sem("x")

        order = [(s, a) for s in range(3) for a in range(2)]
        readers = []
        for s, a in order:
            for k in range(KC):
                readers += ["act", "dve"] if s == 0 else ["act"]
        first_prod = {}
        n = 0
        for s, a in order:
            first_prod[s, a] = n
            n += 2 * KC if s == 0 else KC
        ACT_READS, DVE_READS = readers.count("act"), readers.count("dve")

        def hid(s, a, k):
            return (2 * s + a) * KC + k

        def piece(s, a, k):
            return 2 + (2 * s + a) * KC + k

        def bank_free(eng, i, n):
            m = n - 4
            if m < 0:
                i, m = i - 1, m + NPROD
            who = readers[m]
            count = readers[:m + 1].count(who)
            if who == "act":
                wait(eng, s_ua, i * ACT_READS + count)
            else:
                eng.wait_ge(s_ud, i * DVE_READS + count)

        with nc.Block() as block:
            @block.sync
            def _(sp):
                sp.dma_start(scal[:], w["scales"]).then_inc(s_small, 16)
                for n in range(NW):
                    if n >= 4:
                        sp.wait_ge(s_wsp, n - 3)
                    sp.dma_start(wst[:, n % 4, :], w["w"][n]).then_inc(s_wst[n % 4], 16)

            @block.tensor
            def _(pe):
                def passes(out, piece, c, a, rhs_h, rhs_l, start, stop):
                    c = slice(c * P, (c + 1) * P)
                    pe.matmul(out, wh[:, piece, c], rhs_h, start=start, stop=False)
                    pe.matmul(out, wl[:, piece, c], rhs_h, start=False, stop=False)
                    return pe.matmul(out, wh[:, piece, c], rhs_l, start=False, stop=stop)

                def stage(i, s, a, first=False):
                    if s == 0:
                        pe.wait_ge(s_xh, 2 * i + a + 1)
                        pe.wait_ge(s_xl, 2 * i + a + 1)
                    for k in range(KC):
                        if s == 0:
                            for v in range(2):
                                n = first_prod[s, a] + 2 * k + v
                                bank_free(pe, i, n)
                                passes(U[:, n % 4, :], v, k, a, xh[:, a, :], xl[:, a, :], True, True)\
                                    .then_inc(s_up, 1)
                        else:
                            n = first_prod[s, a] + k
                            bank_free(pe, i, n)
                            src = (s + 1) % 2
                            for c in range(KC):
                                if first and k == 0:
                                    pe.wait_ge(s_wsp, 2 + KC * (s - 1) + c + 1)
                                pe.wait_ge(s_hl, i * NHID + hid(s - 1, a, c) + 1)
                                mm = passes(U[:, n % 4, :], 2 + KC * (s - 1) + c, k, a, hh[:, a, src, c, :],
                                            hl[:, a, src, c, :], c == 0, c == KC - 1)
                            mm.then_inc(s_up, 1)

                def output(i, a):
                    wait(pe, s_yc, 2 * (i - 1) + a + 1)
                    for c in range(KC):
                        pe.wait_ge(s_hl, i * NHID + hid(2, a, c) + 1)
                        mm = passes(Y[:, a, :], NW - 1, c, a, hh[:, a, 0, c, :], hl[:, a, 0, c, :],
                                    c == 0, c == KC - 1)
                    mm.then_inc(s_y, 1)

                def norm_T(i, a):
                    pe.wait_ge(s_xn, 2 * i + a + 1)
                    if a == 0:
                        wait(pe, s_x, 2 * (i - 1))
                    else:
                        pe.wait_ge(s_xl, 2 * i + 1)
                    for t in range(TPB):
                        mm = pe.transpose(T[:, t * P:(t + 1) * P], xn[:, t, :], ident[:])
                    mm.then_inc(s_xT, 1)

                def sum_T(i, a):
                    pe.wait_ge(s_yc, 2 * i + a + 1)
                    if a == 0:
                        pe.wait_ge(s_xl, 2 * (i + 1) + 2)
                    else:
                        pe.wait_ge(s_x, 2 * i + 1)
                    for t in range(TPB):
                        mm = pe.transpose(T[:, t * P:(t + 1) * P], outT[:, a, t * P:(t + 1) * P], ident[:])
                    mm.then_inc(s_aT, 1)

                def pair(i, first=False):
                    for a in range(2):
                        if first and a == 0:
                            pe.wait_ge(s_wsp, 2)
                        stage(i, 0, a)
                        if not first:
                            sum_T(i - 1, a)
                    for a in range(2):
                        stage(i, 1, a, first)
                        norm_T(i + 1, a)
                    stage(i, 2, 0, first)
                    stage(i, 2, 1, first)
                    if first:
                        pe.wait_ge(s_wsp, NW)
                    output(i, 0)
                    output(i, 1)

                norm_T(0, 0)
                norm_T(0, 1)
                pair(0, first=True)
                with pe.Fori(1, NPAIR) as i:
                    pair(i)
                sum_T(NPAIR - 1, 0)
                sum_T(NPAIR - 1, 1)

            @block.scalar
            def _(act):
                def split_x(i, a):
                    act.wait_ge(s_xT, 2 * i + a + 1)
                    wait(act, s_up, (i - 1) * NPROD + first_prod[0, a] + 2 * KC)
                    act.activation(xh[:, a, :], T[:], ACT.Copy).then_inc(s_xh, 1)

                def high(i, a, k):
                    act.wait_ge(s_ud, i * DVE_READS + KC * a + k + 1)
                    act.activation(hh[:, a, 0, k, :], hf[:, k, :], ACT.Copy).then_inc(s_hh, 1)

                def split(n):
                    act.wait_ge(s_wst[n % 4], 16 * (n // 4 + 1))
                    act.activation(wh[:, n, :], wst[:, n % 4, :], ACT.Copy).then_inc(s_wsc, 1)

                def stage(i, s, a, first=False):
                    for k in range(KC):
                        h = hid(s, a, k)
                        n = first_prod[s, a] + (2 * k if s == 0 else k)
                        sc = scal[:, (0, 2 * KC, 3 * KC)[s] + k:(0, 2 * KC, 3 * KC)[s] + k + 1]
                        act.wait_ge(s_up, i * NPROD + n + 1)
                        wait(act, s_hl, i * NHID + h - 3)
                        if s == 0:
                            ins = act.activation(raw[:, k, :], U[:, n % 4, :], ACT.Silu, scale=sc)
                            ins.then_inc(s_ua, 1)
                            if k:
                                high(i, a, k - 1)
                        else:
                            act.activation(raw[:, k, :], U[:, n % 4, :], ACT.Gelu, scale=sc).then_inc(s_raw, 1)
                            act.activation(hh[:, a, s % 2, k, :], U[:, n % 4, :], ACT.Gelu, scale=sc)\
                               .then_inc(s_ua, 1)
                        if first and piece(s, a, k) < NW:
                            split(piece(s, a, k))
                    if s == 0:
                        high(i, a, KC - 1)

                def output(i, a):
                    act.wait_ge(s_y, 2 * i + a + 1)
                    wait(act, s_aT, 2 * (i - 1) + a + 1)
                    act.activation(outT[:, a, :], Y[:, a, :], ACT.Copy, scale=scal[:, 4 * KC:4 * KC + 1])\
                       .then_inc(s_yc, 1)

                def pair(i, first=False):
                    for a in range(2):
                        stage(i, 0, a, first)
                    for a in range(2):
                        stage(i, 1, a, first)
                        split_x(i + 1, a)
                    stage(i, 2, 0)
                    stage(i, 2, 1)
                    output(i, 0)
                    output(i, 1)

                split_x(0, 0)
                split_x(0, 1)
                split(0)
                split(1)
                act.wait_ge(s_small, 16)
                pair(0, first=True)
                with act.Fori(1, NPAIR) as i:
                    pair(i)

            @block.vector
            def _(dve):
                def norm(i, a, ch):
                    b = 2 * i + a
                    norm_stats(nc, dve, ch, lambda t: x[:, bass.ds((b * TPB + t) * P, P)], stats, mv, spare)\
                        .then_inc(s_mv, 1)
                    dve.wait_ge(s_rstd, b + 1)
                    wait(dve, s_xT, b)
                    for t in range(TPB):
                        last = dve.tensor_scalar(xn[:, t, :], x[:, bass.ds((b * TPB + t) * P, P)],
                                                 mv[:, t, 0:1], rstd[:, t:t + 1], ALU.subtract, ALU.mult)
                    last.then_inc(s_xn, 1)

                def split_x(i, a):
                    dve.wait_ge(s_xh, 2 * i + a + 1)
                    dve.tensor_tensor(xl[:, a, :], T[:], xh[:, a, :].bitcast(F32), ALU.subtract)\
                       .then_inc(s_xl, 1)

                def split(n):
                    dve.wait_ge(s_wsc, n + 1)
                    dve.tensor_tensor(wl[:, n, :], wst[:, n % 4, :], wh[:, n, :].bitcast(F32), ALU.subtract)\
                       .then_inc(s_wsp, 1)

                def stage(i, s, a, first=False):
                    for k in range(KC):
                        h = hid(s, a, k)
                        if s == 0:
                            n = first_prod[s, a] + 2 * k
                            dve.wait_ge(s_ua, i * ACT_READS + KC * a + k + 1)
                            dve.wait_ge(s_up, i * NPROD + n + 2)
                            wait(dve, s_hl, i * NHID + h - 3)
                            dve.scalar_tensor_tensor(hf[:, k, :], U[:, (n + 1) % 4, :],
                                                     scal[:, KC + k:KC + k + 1], raw[:, k, :],
                                                     ALU.mult, ALU.mult).then_inc(s_ud, 1)
                            if k:
                                low(i, s, a, k - 1)
                        else:
                            low(i, s, a, k)
                        if first and piece(s, a, k) < NW:
                            split(piece(s, a, k))
                    if s == 0:
                        low(i, s, a, KC - 1)

                def low(i, s, a, k):
                    if s == 0:
                        dve.wait_ge(s_hh, i * 2 * KC + KC * a + k + 1)
                    else:
                        dve.wait_ge(s_ua, i * ACT_READS + 2 * KC + (2 * (s - 1) + a) * KC + k + 1)
                    src = hf if s == 0 else raw
                    dve.tensor_tensor(hl[:, a, s % 2, k, :], src[:, k, :], hh[:, a, s % 2, k, :].bitcast(F32),
                                      ALU.subtract).then_inc(s_hl, 1)

                def update(i, a):
                    dve.wait_ge(s_aT, 2 * i + a + 1)
                    xb = x[:, bass.ds((2 * i + a) * BLK, BLK)]
                    dve.scalar_tensor_tensor(xb, T[:], 0.5, xb, ALU.mult, ALU.add).then_inc(s_x, 1)

                def pair(i, first=False):
                    ch = Chain(dve, s_gch, 2 + 2 * i)
                    for a in range(2):
                        stage(i, 0, a, first)
                        if not first:
                            update(i - 1, a)
                    for a in range(2):
                        norm(i + 1, a, ch)
                        stage(i, 1, a, first)
                        split_x(i + 1, a)
                    stage(i, 2, 0)
                    stage(i, 2, 1)

                ch = Chain(dve, s_gch)
                norm(0, 0, ch)
                split_x(0, 0)
                norm(0, 1, ch)
                split_x(0, 1)
                split(0)
                split(1)
                dve.wait_ge(s_small, 16)
                pair(0, first=True)
                with dve.Fori(1, NPAIR) as i:
                    pair(i)
                update(NPAIR - 1, 0)
                update(NPAIR - 1, 1)

            @block.gpsimd
            def _(pool):
                def rstd_of(b):
                    pool.wait_ge(s_mv, b + 1)
                    pool.tensor_tensor(veps[:], mv[:, :, 1], eps[:], ALU.add).then_inc(s_ve, 1)
                    pool.wait_ge(s_ve, b + 1)
                    wait(pool, s_xn, b)
                    pool.tensor_tensor(rstd[:], veps[:], mhalf[:], ALU.pow).then_inc(s_rstd, 1)

                pool.memset(mhalf[:], -0.5).then_inc(s_cst, 1)
                pool.memset(eps[:], EPS).then_inc(s_cst, 1)
                pool.wait_ge(s_cst, 2)
                rstd_of(0)
                rstd_of(1)
                with pool.Fori(1, NPAIR + 1) as i:
                    rstd_of(2 * i)
                    rstd_of(2 * i + 1)
        ph.clear()
def mamba(nc, tag, x, ident, w):
    NS = 16
    DBC = 2 * 2 * NS
    DBL = DBC + 8
    HALF = 2
    NCH = SEQ // BLK
    TPS = SEQ // P
    PADW = 3
    PAIRS = NS * NCH
    UNITS = PAIRS * HALF
    TAPS = 4

    CONV = {0: 0, 1: 10}
    SILU = {0: 14, 1: 19}
    XPROJ = {0: (15, 16), 1: (20, 21)}
    DTPROJ = {0: (18, 20, 22, 24), 1: (22, 24, 26, 28)}
    SKIP = {0: 14, 1: 19}
    GATE = 1

    def uses_of(stage, d):
        uses = {}
        if d == 0 and stage in ("mid", "last", "tail"):
            uses.update({4: ("out", 0, 0), 6: ("out", 0, 1)})
        if d == 0 and stage in ("first", "mid", "last"):
            uses.update({8: ("z", 0, 0), 9: ("z", 0, 1), 10: ("z", 1, 0), 11: ("z", 1, 1)})
        if d == 1 and stage != "last":
            uses.update({1: ("T", 0, 0), 3: ("T", 0, 1), 5: ("x", 0, 0), 6: ("x", 0, 1),
                         7: ("x", 1, 0), 8: ("x", 1, 1)})
        if has_side(stage, d):
            uses.update({v: ("xproj", 0, c) for c, v in enumerate(XPROJ[d])})
            uses.update({v: ("dt", m % 2, m // 2) for m, v in enumerate(DTPROJ[d])})
        return uses

    def has_side(stage, d):
        return stage in ("first", "mid") or (stage, d) in (("pre", 1), ("last", 0))

    def has_scan(stage):
        return stage not in ("pre", "tail")

    HALVES = {"pre": [1], "first": [0, 1], "mid": [0, 1], "last": [0, 1], "tail": [0]}
    LIST = {st: [(d, v, u) for d in ds for v, u in sorted(uses_of(st, d).items())] for st, ds in HALVES.items()}
    COUNTED = {"O": lambda k: True, "D": lambda k: k in ("T", "out"), "A": lambda k: k not in ("T", "out")}

    def through(what, stage, i, d, v):
        n = lambda st: sum(COUNTED[what](u[0]) for _, _, u in LIST[st])
        base = 0
        if stage != "pre":
            base += n("pre")
        if stage in ("mid", "last", "tail"):
            base += n("first") + (i - 1) * n("mid")
        if stage == "tail":
            base += n("last") - n("mid")
        return base + sum(COUNTED[what](u[0]) for dd, vv, u in LIST[stage] if (dd, vv) <= (d, v))

    def all_halves(half, eng):
        half("pre", -1, 1)
        half("first", 0, 0)
        half("first", 0, 1)
        with eng.Fori(1, NBATCH - 1) as i:
            half("mid", i, 0)
            half("mid", i, 1)
        half("last", NBATCH - 1, 0)
        half("last", NBATCH - 1, 1)
        half("tail", NBATCH, 0)

    def side(i, d):
        return (i, 1, 2 * i + 1) if d == 0 else (i + 1, 0, 2 * (i + 1))

    with ExitStack() as ctx:
        ph = Phase(nc, ctx, tag)
        sb, sem = ph.sb, ph.sem
        wi = sb("wi", [P, 512])
        wih, wil = sb("wih", [P, 512], F32R), sb("wil", [P, 512], F32R)
        convw = sb("convw", [P, 2, HALF, 4])
        vecs = sb("vecs", [P, 3, 2, HALF])
        xpw = sb("xpw", [P, 2, HALF, DBL])
        dtw = sb("dtw", [DBL, 2, HALF, P])
        alog, aneg = sb("alog", [P, 2, HALF, NS]), sb("aneg", [P, 2, HALF, NS])
        wo = sb("wo", [P, HALF, P])
        sel = sb("sel", [DBC, 2 * NS, P], F32R)
        mhalf, one = sb("mhalf", [P, TILES]), sb("one", [P, 1])
        stats, mv = sb("stats", [P, TILES, 6]), sb("mv", [P, TILES, 2])
        veps, rstd = sb("veps", [P, TILES]), sb("rstd", [P, TILES])
        xn = sb("xn", [P, TPS, P])
        xh, xl = sb("xh", [P, SEQ], F32R), sb("xl", [P, SEQ], F32R)
        xpad = sb("xpad", [P, HALF, SEQ + 2 * PADW])
        zs = sb("zs", [P, HALF, SEQ])
        xs = sb("xs", [P, 2, HALF, SEQ])
        dbl = sb("dbl", [DBL, SEQ])
        bcs = sb("bcs", [DBC, 2, SEQ], F32R)
        dt, u = sb("dt", [P, 2, HALF, SEQ]), sb("u", [P, 2, HALF, SEQ])
        RING = 4
        ARING = 8
        dA, bx = sb("dA", [P, ARING, BLK]), sb("bx", [P, RING, BLK])
        H, hc = sb("H", [P, RING, BLK]), sb("hc", [P, RING, BLK])
        cb = sb("cb", [P, RING, BLK])
        ab, ee, ln, uu = (sb(n, [P, BLK]) for n in ("ab", "ee", "ln", "uu"))
        co, rl = sb("co", [P, BLK]), sb("rl", [P, 2, BLK])
        ys = sb("ys", [P, HALF, NCH, BLK])

        Y = ph.ps("Y", [P, 4, BLK])
        Bp = ph.ps("Bp", [P, 2, BLK])
        Cp = ph.ps("Cp", [P, BLK])
        O = ph.ps("O", [P, BLK])

        s_ld, s_sel = sem("ld"), sem("sel")
        s_cst, s_aexp, s_pre = sem("cst"), sem("aexp"), sem("pre")
        s_mv, s_ve, s_rstd = sem("mv"), sem("ve"), sem("rstd")
        s_gch = sem("gch")
        s_xn, s_xh = sem("xn"), sem("xh")
        s_O, s_Od, s_Oa = sem("O"), sem("Od"), sem("Oa")
        s_cv, s_xs, s_zs = sem("cv"), sem("xs"), sem("zs")
        s_bcs = sem("bcs")
        s_ab, s_rl, s_ee, s_ln = sem("ab"), sem("rl"), sem("ee"), sem("ln")
        s_sr = sem("sr")
        s_dt, s_u = sem("dt"), sem("u")
        s_B, s_C, s_cb = sem("B"), sem("C"), sem("cb")
        s_dA, s_bx, s_scan = sem("dA"), sem("bx"), sem("scan")
        s_hc, s_y = sem("hc"), sem("y")
        s_ye, s_g = sem("ye"), sem("g")

        LOADS = ((wi[:], w["in_proj"]), (convw[:], w["conv_w"]), (vecs[:], w["vecs"]),
                 (xpw[:], w["x_proj"]), (dtw[:], w["dt_proj"]), (alog[:], w["A_log"]),
                 (wo[:], w["out_proj"]))
        sels = [t[0:DBC, :, :].rearrange("p a (n c) -> p (a n) c", c=P) for t in (H, hc)]
        units = {d: [(n, c, h) for n in range(NS) for c in (range(NCH) if d == 0 else range(NCH - 1, -1, -1))
                     for h in range(HALF)] for d in range(2)}

        def chunk(c):
            return slice(c * BLK, (c + 1) * BLK)

        with nc.Block() as block:
            @block.sync
            def _(sp):
                for dst, src in LOADS:
                    sp.dma_start(dst, src).then_inc(s_ld, 16)
                for k in range(2):
                    sp.dma_start(sels[k], w["bc_sel"][:, NS * k:NS * (k + 1), :]).then_inc(s_sel, 16)

            @block.tensor
            def _(pe):
                def rows(i, d, q):
                    n, c, _ = units[d][2 * q]
                    Q = (2 * i + d) * PAIRS + q
                    if q == 0:
                        pe.wait_ge(s_bcs, 2 * i + d + 1)
                    wait(pe, s_bx, 2 * (Q - 1))
                    pe.matmul(Bp[:, q % 2, :], sel[:, n, :], bcs[:, d, chunk(c)], start=True, stop=True)\
                      .then_inc(s_B, 1)
                    wait(pe, s_cb, Q)
                    pe.matmul(Cp[:], sel[:, NS + n, :], bcs[:, d, chunk(c)], start=True, stop=True)\
                      .then_inc(s_C, 1)

                def o_use(stage, i, d, v, use):
                    kind, part, c = use
                    ii, e, k = side(i, d)
                    wait(pe, s_Od, through("D", stage, i, d, v - 1))
                    wait(pe, s_Oa, through("A", stage, i, d, v - 1))
                    if kind == "T":
                        pe.wait_ge(s_xn, ii + 1)
                        for t in range(TPB):
                            mm = pe.transpose(O[:, t * P:(t + 1) * P], xn[:, TPB * c + t, :], ident[:])
                    elif kind in ("x", "z"):
                        f = slice(part * P + (256 if kind == "z" else 0), (part + 1) * P + (256 if kind == "z" else 0))
                        pe.matmul(O[:], wih[:, f], xh[:, chunk(c)], start=True, stop=False)
                        pe.matmul(O[:], wil[:, f], xh[:, chunk(c)], start=False, stop=False)
                        mm = pe.matmul(O[:], wih[:, f], xl[:, chunk(c)], start=False, stop=True)
                    elif kind == "xproj":
                        pe.wait_ge(s_xs, k + 1)
                        for h in range(HALF):
                            mm = pe.matmul(O[0:DBL, :], xpw[:, e, h, :], xs[:, e, h, chunk(c)],
                                           start=h == 0, stop=h == 1)
                    elif kind == "dt":
                        mm = pe.matmul(O[:], dtw[:, e, part, :], dbl[:, chunk(c)], start=True, stop=True)
                    else:
                        pe.wait_ge(s_g, 4 * (i - 1) + 2 * c + 2)
                        for t in range(TPB):
                            for h in range(HALF):
                                mm = pe.matmul(O[:, t * P:(t + 1) * P], ys[:, h, c, t * P:(t + 1) * P],
                                               wo[:, h, :], start=h == 0, stop=h == 1)
                    mm.then_inc(s_O, 1)

                def add_y(i, d, v):
                    for h in range(HALF):
                        g = 2 * v + h
                        n, c, _ = units[d][g]
                        pe.wait_ge(s_hc, (2 * i + d) * UNITS + g + 1)
                        if d == 0 and n == 0:
                            wait(pe, s_ye, 4 * (i - 1) + 2 * c + h + 1)
                        pe.matmul(Y[:, 2 * c + h, :], ident[:], hc[:, g % RING, :],
                                  start=d == 0 and n == 0, stop=d == 1 and n == NS - 1).then_inc(s_y, 1)

                def half(stage, i, d):
                    uses = uses_of(stage, d)
                    if (stage, d) == ("first", 0):
                        pe.wait_ge(s_pre, 4)
                    if has_scan(stage):
                        rows(i, d, 0)
                        rows(i, d, 1)
                    for v in range(PAIRS):
                        if stage == "pre" and v == 4:
                            pe.wait_ge(s_pre, 2)
                        if has_scan(stage):
                            if v + 2 < PAIRS:
                                rows(i, d, v + 2)
                        if v in uses:
                            o_use(stage, i, d, v, uses[v])
                        if has_scan(stage) and v:
                            add_y(i, d, v - 1)
                    if has_scan(stage):
                        add_y(i, d, PAIRS - 1)

                all_halves(half, pe)

            @block.scalar
            def _(act):
                nc.scalar.preload_act_table_set("natural_log_exp_and_others")
                act.wait_ge(s_ld, 16 * len(LOADS))
                act.activation(aneg[:], alog[:], ACT.Exp).then_inc(s_aexp, 1)
                act.activation(wih[:], wi[:], ACT.Copy).then_inc(s_aexp, 1)
                act.wait_ge(s_cst, 3)

                def o_read(stage, i, d, v, use):
                    kind, part, c = use
                    ii, e, k = side(i, d)
                    if kind == "out":
                        return
                    act.wait_ge(s_O, through("O", stage, i, d, v))
                    if kind == "T":
                        act.activation(xh[:, chunk(c)], O[:], ACT.Copy).then_inc(s_xh, 1)
                    elif kind == "x":
                        act.activation(xpad[:, part, PADW + c * BLK:PADW + (c + 1) * BLK], O[:], ACT.Copy)\
                           .then_inc(s_Oa, 1)
                    elif kind == "z":
                        act.activation(zs[:, part, chunk(c)], O[:], ACT.Copy).then_inc(s_Oa, 1)
                    elif kind == "xproj":
                        wait(act, s_bcs, k)
                        act.activation(dbl[:, chunk(c)], O[0:DBL, :], ACT.Copy).then_inc(s_Oa, 1)
                    else:
                        m = 2 * c + part
                        b = vecs[:, 1, e, part:part + 1]
                        act.activation(ab[:], O[:], ACT.Abs, bias=b).then_inc(s_ab, 1)
                        wait(act, s_dt, 4 * k + m - 1)
                        act.activation(rl[:, m % 2, :], O[:], ACT.Relu, bias=b).then_inc(s_Oa, 1)

                def softplus(i, d, use):
                    kind, part, c = use
                    ii, e, k = side(i, d)
                    m = 2 * c + part
                    act.wait_ge(s_ab, 4 * k + m + 1)
                    wait(act, s_dt, 4 * k + m)
                    act.activation(ee[:], ab[:], ACT.Exp, scale=-1.0).then_inc(s_ee, 1)
                    act.wait_ge(s_ee, 4 * k + m + 1)
                    act.activation(uu[:], ee[:], ACT.Identity, bias=one[:])
                    act.activation(ln[:], ee[:], ACT.Ln, bias=one[:]).then_inc(s_ln, 1)

                def silus(i, d):
                    ii, e, k = side(i, d)
                    nc.scalar.preload_act_table_set("silu_and_others")
                    act.wait_ge(s_cv, k + 1)
                    for h in range(HALF):
                        last = act.activation(xs[:, e, h, :], xs[:, e, h, :], ACT.Silu, bias=vecs[:, 0, e, h:h + 1])
                    last.then_inc(s_xs, 1)
                    if d == 0:
                        act.wait_ge(s_Oa, through("A", *z_last(i)))
                        act.activation(zs[:], zs[:], ACT.Silu).then_inc(s_zs, 1)
                    nc.scalar.preload_act_table_set("natural_log_exp_and_others")

                def z_last(i):
                    stage = ("last" if i == NBATCH - 1 else "first") if isinstance(i, int) else "mid"
                    return stage, i, 0, 11

                def copy_c(i, d, v):
                    Q = (2 * i + d) * PAIRS + v
                    act.wait_ge(s_C, Q + 1)
                    wait(act, s_hc, 2 * (Q - RING) + 2)
                    act.activation(cb[:, v % RING, :], Cp[:], ACT.Copy).then_inc(s_cb, 1)

                def decays(i, d, v):
                    for g in (2 * v, 2 * v + 1):
                        n, c, h = units[d][g]
                        wait(act, s_scan, (2 * i + d) * UNITS + g - ARING + 1)
                        act.activation(dA[:, g % ARING, :], dt[:, d, h, chunk(c)], ACT.Exp,
                                       scale=aneg[:, d, h, n:n + 1]).then_inc(s_dA, 1)

                def half(stage, i, d):
                    uses = uses_of(stage, d)
                    for v in range(PAIRS):
                        if has_scan(stage):
                            if v == 0:
                                act.wait_ge(s_dt, 4 * (2 * i + d + 1))
                                decays(i, d, 0)
                            copy_c(i, d, v)
                            if v + 1 < PAIRS:
                                decays(i, d, v + 1)
                        if v - 2 in uses:
                            o_read(stage, i, d, v - 2, uses[v - 2])
                        if v - 3 in uses and uses[v - 3][0] == "dt":
                            softplus(i, d, uses[v - 3])
                        if v == SILU[d] and has_side(stage, d):
                            silus(i, d)

                all_halves(half, act)

            @block.vector
            def _(dve):
                def statistics(tiles, ch):
                    for t in tiles:
                        last = dve.bn_stats(stats[:, t, :], x[:, t * P:(t + 1) * P])
                    ch.step(last)
                    ch.join()
                    for t in tiles:
                        last = dve.bn_aggr(mv[:, t, :], stats[:, t, :])
                    last.then_inc(s_mv, 1)

                statistics(range(TPS), Chain(dve, s_gch))
                dve.wait_ge(s_cst, 3)
                dve.wait_ge(s_aexp, 2)
                dve.tensor_scalar(aneg[:], aneg[:], -1.0, None, ALU.mult).then_inc(s_pre, 1)
                dve.tensor_tensor(wil[:], wi[:], wih[:].bitcast(F32), ALU.subtract).then_inc(s_pre, 1)
                dve.wait_ge(s_sel, 32)
                for k in range(2):
                    dve.tensor_copy(sel[:, NS * k:NS * (k + 1), :], sels[k]).then_inc(s_pre, 1)
                dve.wait_ge(s_rstd, 1)

                CH_SIDE, CH_SKIP = HALF * TAPS - 1 + 1 + 4, 4

                def normalize(ii):
                    for t in range(TPS):
                        last = dve.tensor_scalar(xn[:, t, :], x[:, bass.ds((ii * TPS + t) * P, P)],
                                                 mv[:, bass.ds(ii * TPS + t, 1), 0:1].rearrange("p a b -> p (a b)"),
                                                 rstd[:, bass.ds(ii * TPS + t, 1)], ALU.subtract, ALU.mult)
                    last.then_inc(s_xn, 1)

                def conv(i, d, n, ch):
                    ii, e, k = side(i, d)
                    s, h = n // HALF, n % HALF
                    if n == 0:
                        dve.wait_ge(s_Oa, through("A", *x_last(i, d)))
                    off = PADW - s if e == 0 else PADW + s
                    src = xpad[:, h, off:off + SEQ]
                    tap = convw[:, e, h, TAPS - 1 - s:TAPS - s]
                    if s == 0:
                        ins = dve.tensor_scalar(xs[:, e, h, :], src, tap, None, ALU.mult)
                    else:
                        ch.join()
                        ins = dve.scalar_tensor_tensor(xs[:, e, h, :], src, tap, xs[:, e, h, :], ALU.mult, ALU.add)
                    if n < HALF * TAPS - 1:
                        ch.step(ins)
                    else:
                        ins.then_inc(s_cv, 1)

                def x_last(i, d):
                    if isinstance(i, int):
                        if i <= 0:
                            return ("pre", -1, 1, 8) if (i, d) in ((-1, 1), (0, 0)) else ("first", 0, 1, 8)
                        return "mid", i - 1, 1, 8
                    return ("mid", i, 1, 8) if d == 1 else ("mid", i, -1, 0)

                def split_rows(stage, i, d, ch):
                    ii, e, k = side(i, d)
                    dve.wait_ge(s_Oa, through("A", stage, i, d, XPROJ[d][1]))
                    ch.step(dve.tensor_copy(bcs[:, e, :], dbl[0:DBC, :]))
                    ch.join()
                    dve.tensor_tensor(bcs[32:64, e, :], dbl[32:64, :], bcs[32:64, e, :].bitcast(F32), ALU.subtract)\
                       .then_inc(s_bcs, 1)

                def softplus(i, d, use, ch):
                    kind, part, c = use
                    ii, e, k = side(i, d)
                    m = 2 * c + part
                    dve.wait_ge(s_ln, 4 * k + m + 1)
                    ch.step(dve.scalar_tensor_tensor(co[:], uu[:], 1.0, ee[:], ALU.subtract, ALU.subtract))
                    ch.join()
                    dve.wait_ge(s_sr, 4 * k + m + 1)
                    dve.tensor_tensor(dt[:, e, part, chunk(c)], rl[:, m % 2, :], co[:], ALU.subtract).then_inc(s_dt, 1)

                def skip(d, n, ch):
                    h, c = n % 2, n // 2
                    if d == 0:
                        ch.step(dve.tensor_scalar(ys[:, h, c, :], xs[:, 0, h, chunk(c)], vecs[:, 2, 0, h:h + 1],
                                                  None, ALU.mult))
                    else:
                        ch.step(dve.scalar_tensor_tensor(ys[:, h, c, :], xs[:, 1, h, chunk(c)],
                                                         vecs[:, 2, 1, h:h + 1], ys[:, h, c, :],
                                                         ALU.mult, ALU.add))

                def gate(i):
                    dve.wait_ge(s_y, (2 * i + 2) * UNITS)
                    wait(dve, s_gch, 2 + CH_SIDE + (CH_SIDE + CH_SKIP) * (2 * i + 2)
                         - (CH_SIDE if i is NBATCH - 1 else 0))
                    for k in range(4):
                        c, h = k // 2, k % 2
                        dve.tensor_tensor(ys[:, h, c, :], ys[:, h, c, :], Y[:, 2 * c + h, :], ALU.add)\
                           .then_inc(s_ye, 1)
                    dve.wait_ge(s_zs, i + 1)
                    for k in range(4):
                        c, h = k // 2, k % 2
                        dve.wait_ge(s_ye, 4 * i + k + 1)
                        dve.tensor_tensor(ys[:, h, c, :], ys[:, h, c, :], zs[:, h, chunk(c)], ALU.mult)\
                           .then_inc(s_g, 1)

                def half(stage, i, d):
                    uses = uses_of(stage, d)
                    J = 2 * i + d
                    ch = Chain(dve, s_gch, 1 if stage == "pre" else 2 + CH_SIDE + (CH_SIDE + CH_SKIP) * J)
                    for v in range(PAIRS + 1):
                        if v == 0 and d == 1 and has_side(stage, d):
                            if stage == "first":
                                dve.wait_ge(s_rstd, 2)
                            normalize(i + 1)
                        if v == SILU[1] and stage == "pre":
                            statistics(range(TPS, TILES), ch)
                        if has_scan(stage) and v < PAIRS:
                            for g in (2 * v, 2 * v + 1):
                                n, c, h = units[d][g]
                                dve.wait_ge(s_B, J * PAIRS + v + 1)
                                if g == 0:
                                    dve.wait_ge(s_u, 4 * (J + 1))
                                dve.tensor_tensor(bx[:, g % RING, :], u[:, d, h, chunk(c)], Bp[:, v % 2, :],
                                                  ALU.mult).then_inc(s_bx, 1)
                                if g:
                                    scan(J, d, g - 1)
                            if v == PAIRS - 1:
                                scan(J, d, UNITS - 1)
                        if v == GATE and d == 0 and stage != "first":
                            gate(i - 1)
                        if has_side(stage, d):
                            if CONV[d] <= v < CONV[d] + HALF * TAPS:
                                conv(i, d, v - CONV[d], ch)
                            if v == XPROJ[d][1] + 2:
                                split_rows(stage, i, d, ch)
                            if v - 4 in uses and uses[v - 4][0] == "dt":
                                softplus(i, d, uses[v - 4], ch)
                        if has_scan(stage) and v == SKIP[d]:
                            if d == 1:
                                ch.join()
                            for n in range(4):
                                skip(d, n, ch)
                        if v - 2 in uses and uses[v - 2][0] == "T":
                            c = uses[v - 2][2]
                            dve.wait_ge(s_xh, 2 * (i + 1) + c + 1)
                            dve.tensor_tensor(xl[:, chunk(c)], O[:], xh[:, chunk(c)].bitcast(F32), ALU.subtract)\
                               .then_inc(s_Od, 1)
                        if v - 2 in uses and uses[v - 2][0] == "out":
                            c = uses[v - 2][2]
                            dve.wait_ge(s_O, through("O", stage, i, d, v - 2))
                            xb = x[:, bass.ds((i - 1) * SEQ + c * BLK, BLK)]
                            dve.tensor_tensor(xb, xb, O[:], ALU.add).then_inc(s_Od, 1)

                def scan(J, d, g):
                    n, c, h = units[d][g]
                    G = J * UNITS + g
                    dve.wait_ge(s_dA, G + 1)
                    dve.wait_ge(s_bx, G + 1)
                    wait(dve, s_hc, G - RING + 1)
                    s = g % RING
                    if c == (0 if d == 0 else NCH - 1):
                        init = 0.0
                    else:
                        dve.wait_ge(s_scan, G - 1)
                        prev = (g - 2) % RING
                        init = H[:, prev, BLK - 1:BLK] if d == 0 else H[:, prev, 0:1]
                    if d == 0:
                        dve.tensor_tensor_scan(H[:, s, :], dA[:, g % ARING, :], bx[:, s, :], init, ALU.mult, ALU.add)\
                           .then_inc(s_scan, 1)
                    else:
                        dve.tensor_tensor_scan(H[:, s, ::-1], dA[:, g % ARING, ::-1], bx[:, s, ::-1], init,
                                               ALU.mult, ALU.add).then_inc(s_scan, 1)

                all_halves(half, dve)

            @block.gpsimd
            def _(pool):
                pool.memset(mhalf[:], -0.5).then_inc(s_cst, 1)
                pool.memset(one[:], 1.0).then_inc(s_cst, 1)
                pool.memset(xpad[:], 0.0).then_inc(s_cst, 1)
                pool.wait_ge(s_cst, 3)
                for n, t in enumerate((slice(0, TPS), slice(TPS, TILES))):
                    pool.wait_ge(s_mv, n + 1)
                    pool.tensor_scalar(veps[:, t], mv[:, t, 1], EPS, None, ALU.add).then_inc(s_ve, 1)
                    pool.wait_ge(s_ve, n + 1)
                    pool.tensor_tensor(rstd[:, t], veps[:, t], mhalf[:, t], ALU.pow).then_inc(s_rstd, 1)

                def half(stage, i, d):
                    uses = uses_of(stage, d)
                    ii, e, k = side(i, d)
                    J = 2 * i + d
                    for v in range(PAIRS + 1):
                        if v - 3 in uses and uses[v - 3][0] == "dt":
                            kind, part, c = uses[v - 3]
                            m = 2 * c + part
                            pool.wait_ge(s_ln, 4 * k + m + 1)
                            pool.tensor_tensor(rl[:, m % 2, :], rl[:, m % 2, :], ln[:], ALU.add).then_inc(s_sr, 1)
                        if has_scan(stage) and v < PAIRS:
                            for g in (2 * v, 2 * v + 1):
                                G = J * UNITS + g
                                pool.wait_ge(s_scan, G + 1)
                                pool.wait_ge(s_cb, J * PAIRS + v + 1)
                                wait(pool, s_y, G - RING + 1)
                                pool.tensor_tensor(hc[:, g % RING, :], H[:, g % RING, :], cb[:, v % RING, :],
                                                   ALU.mult).then_inc(s_hc, 1)
                        if v - 4 in uses and uses[v - 4][0] == "dt":
                            kind, part, c = uses[v - 4]
                            pool.wait_ge(s_dt, 4 * k + 2 * c + part + 1)
                            pool.tensor_tensor(u[:, e, part, chunk(c)], dt[:, e, part, chunk(c)],
                                               xs[:, e, part, chunk(c)], ALU.mult).then_inc(s_u, 1)

                all_halves(half, pool)
        ph.clear()
def attention(nc, tag, x, ident, w):
    GROUPS, GH = 4, 4
    HD = 8
    ROWS = P // GH
    NCH, TPS = SEQ // BLK, SEQ // P
    VW = HD + 1
    GV = 2 * GH * VW
    PR = 2 * GH
    SU = [(t, c, j) for t, c in ((3, 0), (2, 0), (0, 0), (1, 0), (4, 0), (5, 0), (5, 1), (6, 0), (4, 1), (6, 1),
                                 (7, 0), (7, 1)) for j in range(GH)]
    STEPS = [(c, kt) for c in range(NCH) for kt in range(TPB * (c + 1))]
    NS, NT = len(SU), len(STEPS)
    SPS = NS // NT
    DIAG = [v for v, (c, kt) in enumerate(STEPS) if kt >= TPB * c]

    def slot_uses(stage, g):
        if stage == "tail":
            return {3: ("norm", -1, 3, 1), 4: ("oT", -1, 0, 0), 5: ("oT", -1, 0, 1),
                    6: ("O", -1, 0, 0), 7: ("O", -1, 0, 1)}
        uses = {}
        if stage == "pre":
            uses.update({-7: ("xT", 0, 0, 0), -6: ("xT", 0, 0, 1), -5: ("Q", 0, 0, 0), -4: ("Q", 0, 0, 1),
                         -3: ("K", 0, 0, 0), -2: ("K", 0, 0, 1), -1: ("V", 0, 0, 0)})
        else:
            uses[1], uses[9] = ("max", 0, g, 1), ("norm", 0, g, 0)
            if g:
                uses[3] = ("norm", 0, g - 1, 1)
            elif stage != "first":
                uses[3] = ("norm", -1, 3, 1)
        if stage != "last" or g + 2 < GROUPS:
            rel, n = (g + 2) // GROUPS, (g + 2) % GROUPS
            uses.update({0: ("Q", rel, n, 0), 2: ("Q", rel, n, 1), 4: ("K", rel, n, 0), 5: ("K", rel, n, 1),
                         6: ("V", rel, n // 2, n % 2)})
        if stage != "last" or g + 1 < GROUPS:
            uses[7] = ("max", (g + 1) // GROUPS, (g + 1) % GROUPS, 0)
        if stage in ("mid", "last"):
            if g == 0:
                uses[8], uses[10], uses[11] = ("oT", -1, 0, 0), ("oT", -1, 0, 1), ("O", -1, 0, 0)
            if g == 1:
                uses[8] = ("O", -1, 0, 1)
        if stage in ("first", "mid") and g == 1:
            uses[10], uses[11] = ("xT", 1, 0, 0), ("xT", 1, 0, 1)
        return uses

    SLOTS = {"pre": [-1], "first": [0, 1, 2, 3], "mid": [0, 1, 2, 3], "last": [0, 1, 2, 3], "tail": [0]}
    LIST = {st: [(g, v, u) for g in gs for v, u in sorted(slot_uses(st, g).items())]
            for st, gs in SLOTS.items()}
    def copies(stage, g, v):
        uses = slot_uses(stage, g)
        use = uses.get(v - 2) if v < 0 else uses.get({9: 0, 10: 2}.get(v))
        return use if use and use[0] == "Q" else None

    WEIGHT = {"M": lambda k: 1, "D": lambda k: k not in ("Q", "K", "oT"), "A": lambda k: k in ("Q", "K", "oT"),
              "C": lambda k: {"norm": 1, "O": 2}.get(k, 0)}

    def total(w, stage, keep=lambda g, v: True):
        return sum(int(WEIGHT[w](u[0])) for g, v, u in LIST[stage] if keep(g, v))

    def base(w, stage, i):
        if stage == "pre":
            return 0
        n = total(w, "pre")
        if stage == "first":
            return n
        n += total(w, "first") + (i - 1) * total(w, "mid")
        return n if stage != "tail" else n - total(w, "mid") + total(w, "last")

    def through(w, stage, i, g, v):
        if g >= SLOTS[stage][0]:
            return base(w, stage, i) + total(w, stage, lambda gg, vv: (gg, vv) <= (g, v))
        prev = {"first": "pre", "mid": "mid", "last": "mid", "tail": "last"}[stage]
        last = SLOTS[prev][-1]
        return base(w, stage, i) - total(w, prev, lambda gg, vv: gg == last and vv > v)

    def steps(stage):
        return range(-7, NT) if stage == "pre" else range(9) if stage == "tail" else range(NT)

    def use_before(stage, g, v, back):
        v -= back
        if v < 0 and stage != "pre":
            g, v = g - 1, v + NT
            if g < SLOTS[stage][0]:
                return None
        use = slot_uses(stage, g).get(v)
        return use and (use, g, v)

    def has_exp(stage):
        return stage not in ("pre", "tail")

    def has_max(stage, g):
        return stage != "tail" and not (stage == "last" and g + 1 == GROUPS)

    def all_slots(slot, eng):
        slot("pre", 0, -1)
        for g in range(GROUPS):
            slot("first", 0, g)
        with eng.Fori(1, NBATCH - 1) as i:
            for g in range(GROUPS):
                slot("mid", i, g)
        for g in range(GROUPS):
            slot("last", NBATCH - 1, g)
        slot("tail", NBATCH, 0)

    with ExitStack() as ctx:
        ph = Phase(nc, ctx, tag)
        sb, sem = ph.sb, ph.sem
        NW = 2 * GROUPS
        wst = sb("wst", [P, NW, P])
        wh, wl = sb("wh", [P, NW, P], F32R), sb("wl", [P, NW, P], F32R)
        wvs = sb("wvs", [P, GROUPS * GH * VW])
        wvh, wvl = sb("wvh", [P, GROUPS * GH * VW], F32R), sb("wvl", [P, GROUPS * GH * VW], F32R)
        vb = sb("vb", [P, GROUPS * GH * VW])
        bias, scale, low = sb("bias", [P, NW]), sb("scale", [P, NW]), sb("low", [P, NW])
        bsc = sb("bsc", [P, NW])
        wo, bo = sb("wo", [P, P]), sb("bo", [P, P])
        mask = sb("mask", [P, P])
        idr, mneg = sb("idr", [P, P], F32R), sb("mneg", [P, P], F32R)
        stk = sb("stk", [P, 2, BLK])
        mhalf, zero = sb("mhalf", [P, TILES]), sb("zero", [P, TPB, GH])
        spare = sb("spare", [P, 4])
        stats, mv = sb("stats", [P, TILES, 6]), sb("mv", [P, TILES, 2])
        veps, rstd = sb("veps", [P, TILES]), sb("rstd", [P, TILES])
        xn = sb("xn", [P, TPS, P])
        xh, xl = sb("xh", [P, SEQ], F32R), sb("xl", [P, SEQ], F32R)
        qf, qh = sb("qf", [P, 2, BLK]), sb("qh", [P, 2, BLK], F32R)
        Q, K = sb("Q", [P, GROUPS * GH, SEQ], F32R), sb("K", [P, GROUPS, SEQ], F32R)
        V = sb("V", [P, TPS, GROUPS * GH, ROWS])
        mx, mx0, mxh = sb("mx", [P, 2, TPS, GH]), sb("mx0", [P, TPS - TPB, GH]), sb("mxh", [P, 2, TPB, GH], F32R)
        mt = sb("mt", [P, NCH, TPB, P])
        pt = sb("pt", [P, PR, BLK])
        ov = sb("ov", [P, NCH, BLK])
        rs = sb("rs", [P, TPB, GH])
        on = sb("on", [P, TPS, P])
        oT = sb("oT", [P, NCH, BLK])
        att, pos = sb("att", [P, BLK]), sb("pos", [P, BLK])

        W = ph.ps("W", [P, 6, BLK])
        PV = ph.ps("PV", [P, BLK])
        M = ph.ps("M", [P, BLK])

        s_ld, s_cst, s_wh, s_pre = sem("ld"), sem("cst"), sem("wh"), sem("pre")
        s_mv, s_ve, s_rstd = sem("mv"), sem("ve"), sem("rstd")
        s_gch, s_pch = sem("gch"), sem("pch")
        s_xn, s_xh = sem("xn"), sem("xh")
        s_M, s_Md, s_Ma = sem("M"), sem("Md"), sem("Ma")
        s_st, s_q = sem("st"), sem("q")
        s_S, s_max = sem("S"), sem("max")
        s_mx, s_sp = sem("mx"), sem("sp")
        s_T, s_exp, s_pm = sem("T"), sem("exp"), sem("pm")
        s_pv, s_ov = sem("pv"), sem("ov")

        LOADS = ((wst[:], w["w_qk"]), (wvs[:], w["w_v"]), (vb[:], w["b_v"]), (bias[:], w["b_qk"]),
                 (scale[:], w["scale"]), (low[:], w["low"]), (wo[:], w["w_out"]), (bo[:], w["b_out"]),
                 (mask[:], w["mask"]))

        def chunk(c):
            return slice(c * BLK, (c + 1) * BLK)

        def tile(t):
            return slice(t * P, (t + 1) * P)

        def head(j):
            return slice(ROWS * j, ROWS * (j + 1))

        with nc.Block() as block:
            @block.sync
            def _(sp):
                for dst, src in LOADS:
                    sp.dma_start(dst, src).then_inc(s_ld, 16)

            @block.tensor
            def _(pe):
                def passes(out, ah, al, bh, bl):
                    pe.matmul(out, ah, bh, start=True, stop=False)
                    pe.matmul(out, al, bh, start=False, stop=False)
                    return pe.matmul(out, ah, bl, start=False, stop=True)

                def max_unit(G, g, s):
                    t, c, j = SU[s]
                    n = G * NS + s
                    cols = min(BLK, (t + 1) * P - c * BLK)
                    diag = c == t // TPB
                    wait(pe, s_max, n - 2)
                    out = W[:, s % 3, 0:cols]
                    mm = pe.matmul(out, Q[:, g * GH + j, tile(t)], K[:, g, c * BLK:c * BLK + cols],
                                   start=True, stop=not diag)
                    if diag:
                        mm = pe.matmul(W[:, s % 3, cols - P:cols], idr[:], mneg[:], start=False, stop=True)
                    mm.then_inc(s_S, 1)

                def exp_unit(stage, i, g, v, j):
                    c, kt = STEPS[v]
                    r = max(0, kt - TPB * c)
                    if kt == 0 and j == 0:
                        pe.wait_ge(s_Md, through("D", stage, i, g, 1) if c else through("D", stage, i, g - 1, 7))
                    u = v * GH + j
                    n = (i * GROUPS + g) * NT * GH + u
                    wait(pe, s_exp, n - 2)
                    pe.matmul(W[:, 3 + u % 3, 0:BLK - r * P], K[:, g, tile(kt)],
                              Q[:, g * GH + j, c * BLK + r * P:(c + 1) * BLK],
                              start=True, stop=True).then_inc(s_T, 1)

                def value_step(G, g, v):
                    c, kt = STEPS[v]
                    r = max(0, kt - TPB * c)
                    if kt == 0:
                        wait(pe, s_ov, 2 * G + c)
                    for j in range(GH):
                        u = v * GH + j
                        n = G * NT * GH + u
                        if v in DIAG:
                            pe.wait_ge(s_pm, G * len(DIAG) + DIAG.index(v) + 1)
                        else:
                            pe.wait_ge(s_exp, n + 1)
                        pe.matmul(PV[head(j), r * P:], V[:, kt, g * GH + j, :], pt[:, u % PR, 0:BLK - r * P],
                                  start=kt == 0, stop=kt == TPB * (c + 1) - 1).then_inc(s_pv, 1)

                def m_use(stage, i, g, v, use):
                    kind, rel, n, c = use
                    G = (i + rel) * GROUPS + n
                    wait(pe, s_Md, through("D", stage, i, g, v - 1))
                    wait(pe, s_Ma, through("A", stage, i, g, v - 1))
                    if kind in ("max", "norm", "xT", "oT"):
                        if kind == "max":
                            pe.wait_ge(s_sp, 2 * G + c + 1)
                            src = [mt[:, c, t, :] for t in range(TPB)]
                        elif kind == "norm":
                            pe.wait_ge(s_ov, 2 * G + c + 1)
                            src = [ov[:, c, tile(t)] for t in range(TPB)]
                        elif kind == "xT":
                            pe.wait_ge(s_xn, i + rel + 1)
                            src = [xn[:, TPB * c + t, :] for t in range(TPB)]
                        else:
                            src = [on[:, TPB * c + t, :] for t in range(TPB)]
                        for t in range(TPB):
                            mm = pe.transpose(M[:, tile(t)], src[t], ident[:])
                    elif kind in ("Q", "K"):
                        k = n if kind == "Q" else GROUPS + n
                        mm = passes(M[:], wh[:, k, :], wl[:, k, :], xh[:, chunk(c)], xl[:, chunk(c)])
                    elif kind == "V":
                        f = slice(n * GV, (n + 1) * GV)
                        for t in range(TPB):
                            tt = tile(TPB * c + t)
                            mm = passes(M[:, t * GV:(t + 1) * GV], xh[:, tt], xl[:, tt],
                                        wvh[:, f], wvl[:, f])
                    else:
                        for t in range(TPB):
                            mm = pe.matmul(M[:, tile(t)], oT[:, c, tile(t)], wo[:], start=True, stop=True)
                    mm.then_inc(s_M, 1)

                def slot(stage, i, g):
                    G = i * GROUPS + g
                    uses = slot_uses(stage, g)
                    for v in steps(stage):
                        if v == -5:
                            pe.wait_ge(s_pre, 3)
                        for j in range(GH):
                            if has_exp(stage):
                                exp_unit(stage, i, g, v, j)
                            if has_max(stage, g) and v >= 0:
                                if v == 0 and j == 0:
                                    pe.wait_ge(s_q, 2 * G + 4)
                                    pe.wait_ge(s_st, 4 * G + 8)
                                max_unit(G + 1, (g + 1) % GROUPS, SPS * v + j)
                            if j == 1 and v > 0 and has_exp(stage):
                                value_step(G, g, v - 1)
                            if j == 1 and v == 0 and stage != "pre" and (stage, g) != ("first", 0):
                                value_step(G - 1, (g - 1) % GROUPS, NT - 1)
                        if v in uses:
                            m_use(stage, i, g, v, uses[v])

                all_slots(slot, pe)

            @block.scalar
            def _(act):
                act.wait_ge(s_ld, 16 * len(LOADS))
                act.activation(wh[:], wst[:], ACT.Copy).then_inc(s_wh, 1)
                act.activation(wvh[:], wvs[:], ACT.Copy).then_inc(s_wh, 1)

                def exp_unit(i, g, v, j):
                    c, kt = STEPS[v]
                    r = max(0, kt - TPB * c)
                    u = v * GH + j
                    n = (i * GROUPS + g) * NT * GH + u
                    act.wait_ge(s_T, n + 1)
                    wait(act, s_pv, n - PR + 1)
                    act.activation(pt[:, u % PR, 0:BLK - r * P], W[:, 3 + u % 3, 0:BLK - r * P],
                                   ACT.Exp).then_inc(s_exp, 1)

                def take_out(stage, i, g, c):
                    G = i * GROUPS + g - c
                    act.wait_ge(s_pv, (G * NT + (TPB if c == 0 else NT)) * GH)
                    if not (isinstance(G, int) and G == 0):
                        act.wait_ge(s_M, through("M", stage, i, g - 1, 9 if c == 0 else 3))
                    act.activation(ov[:, c, :], PV[:], ACT.Copy).then_inc(s_ov, 1)

                def m_read(stage, i, g, v, use, j):
                    kind, rel, n, c = use
                    if kind in ("Q", "K") and j < 2:
                        G = (i + rel) * GROUPS + n
                        m, k = (c, n) if kind == "Q" else (2 + c, GROUPS + n)
                        if j == 0:
                            act.wait_ge(s_M, through("M", stage, i, g, v))
                            wait(act, s_st, 4 * G + m - 1)
                            act.activation(qf[:, m % 2, :], M[:], ACT.Identity,
                                           bias=bsc[:, k:k + 1], scale=scale[:, k:k + 1])
                        else:
                            act.activation(qh[:, m % 2, :], M[:], ACT.Identity,
                                           bias=bsc[:, k:k + 1], scale=scale[:, k:k + 1]).then_inc(s_Ma, 1)
                    if kind in ("xT", "oT") and j == 0:
                        act.wait_ge(s_M, through("M", stage, i, g, v))
                        if kind == "xT":
                            act.activation(xh[:, chunk(c)], M[:], ACT.Copy).then_inc(s_xh, 1)
                        else:
                            act.activation(oT[:, c, :], M[:], ACT.Copy).then_inc(s_Ma, 1)

                def queries(i, use, j):
                    if isinstance(i, int) and i == 0 and use[2] == 1 and j == 0:
                        act.wait_ge(s_cst, 6)
                    kind, rel, n, c = use
                    G = (i + rel) * GROUPS + n
                    if j == 0:
                        act.wait_ge(s_st, 4 * G + c + 1)
                    last = act.activation(Q[head(j), n * GH + j, chunk(c)], stk[head(j), c, :], ACT.Copy)
                    if j == GH - 1:
                        last.then_inc(s_q, 1)

                def slot(stage, i, g):
                    for v in steps(stage):
                        if v == -5:
                            act.wait_ge(s_pre, 1)
                            act.wait_ge(s_cst, 3)
                        if v == 5 and has_exp(stage):
                            take_out(stage, i, g, 0)
                        if v == 1 and stage != "pre" and (stage, g) != ("first", 0):
                            take_out(stage, i, g, 1)
                        for j in range(GH):
                            if has_exp(stage):
                                exp_unit(i, g, v, j)
                            before = use_before(stage, g, v, 1)
                            if before:
                                m_read(stage, i, before[1], before[2], before[0], j)
                            copied = copies(stage, g, v)
                            if copied:
                                queries(i, copied, j)

                all_slots(slot, act)

            @block.vector
            def _(dve):
                def statistics(tiles, ch):
                    for t in tiles:
                        last = dve.bn_stats(stats[:, t, :], x[:, tile(t)])
                    ch.step(last)
                    ch.join()
                    for t in tiles:
                        last = dve.bn_aggr(mv[:, t, :], stats[:, t, :])
                    last.then_inc(s_mv, 1)

                statistics(range(TPS), Chain(dve, s_gch))
                dve.wait_ge(s_ld, 16 * len(LOADS))
                dve.tensor_tensor(bsc[:], bias[:], scale[:], ALU.mult)
                dve.tensor_copy(idr[:], ident[:])
                dve.tensor_copy(mneg[:], mask[:]).then_inc(s_pre, 1)
                dve.wait_ge(s_wh, 2)
                dve.tensor_tensor(wl[:], wst[:], wh[:].bitcast(F32), ALU.subtract).then_inc(s_pre, 1)
                dve.tensor_tensor(wvl[:], wvs[:], wvh[:].bitcast(F32), ALU.subtract).then_inc(s_pre, 1)
                dve.wait_ge(s_rstd, 1)
                def max_unit(G, g, s):
                    t, c, j = SU[s]
                    n = G * NS + s
                    dve.wait_ge(s_S, n + 1)
                    if s == 0:
                        wait(dve, s_sp, 2 * (G - 1))
                    last = c == t // TPB
                    dst = mx[:, g % 2, t, j:j + 1] if last else mx0[:, t - TPB, j:j + 1]
                    dve.tensor_reduce(dst, W[:, s % 3, 0:min(BLK, (t + 1) * P - c * BLK)], AX, ALU.max)\
                       .then_inc(s_max, 1)

                def both_chunks(G, g, t):
                    n = max(s for s in range(NS) if SU[s][0] == t)
                    dve.wait_ge(s_max, G * NS + n + 1)
                    dve.tensor_tensor(mx[:, g % 2, t, :], mx[:, g % 2, t, :], mx0[:, t - TPB, :], ALU.max)\
                       .then_inc(s_mx, 1)

                def m_read(stage, i, g, v, use, ch, j):
                    kind, rel, n, c = use
                    if kind in ("Q", "K", "oT"):
                        return
                    last = None
                    if j == 0:
                        dve.wait_ge(s_M, through("M", stage, i, g, v))
                    if kind == "xT" and j == 0:
                        dve.wait_ge(s_xh, 2 * (i + rel) + c + 1)
                        last = dve.tensor_tensor(xl[:, chunk(c)], M[:], xh[:, chunk(c)].bitcast(F32), ALU.subtract)
                    if kind == "max" and j < 2:
                        for jj in (2 * j, 2 * j + 1):
                            q = Q[head(jj), n * GH + jj, chunk(c)]
                            ins = dve.tensor_tensor(q, q.bitcast(F32), M[head(jj), :], ALU.add)
                        if j == 1:
                            last = ins
                    if kind == "norm":
                        m4 = M[:].rearrange("p (t j r) -> p t j r", t=TPB, j=GH)
                        if j == 0:
                            ch.step(dve.reciprocal(rs[:], m4[:, :, :, HD]))
                        if j == 1:
                            ch.join()
                            out = on[:, TPB * c:TPB * (c + 1), n * GH * HD:(n + 1) * GH * HD]
                            last = dve.tensor_tensor(out.rearrange("p t (j d) -> p t j d", j=GH),
                                                     m4[:, :, :, 0:HD],
                                                     rs[:].unsqueeze(3).broadcast_to((P, TPB, GH, HD)), ALU.mult)
                    if kind == "V" and j == 0:
                        last = dve.tensor_tensor(V[:, TPB * c:TPB * (c + 1), n * 2 * GH:(n + 1) * 2 * GH, 0:VW],
                                                 M[:, 0:TPB * GV].rearrange("p (t h e) -> p t h e", t=TPB, e=VW),
                                                 vb[:, n * GV:(n + 1) * GV].rearrange("p (h e) -> p h e", e=VW)
                                                 .unsqueeze(1).broadcast_to((P, TPB, 2 * GH, VW)), ALU.add)
                    if kind == "O":
                        xb = x[:, bass.ds((i + rel) * SEQ + c * BLK, BLK)]
                        if j == 0:
                            ch.step(dve.tensor_tensor(att[:].rearrange("p (t f) -> p t f", t=TPB),
                                                      M[:].rearrange("p (t f) -> p t f", t=TPB),
                                                      bo[:].unsqueeze(1).broadcast_to((P, TPB, P)), ALU.add))
                        if j == 1:
                            ch.join()
                            ch.step(dve.scalar_tensor_tensor(pos[:], att[:], 0.0, xb, ALU.max, ALU.add))
                        if j == 2:
                            ch.join()
                            last = dve.scalar_tensor_tensor(xb, att[:], 0.0, pos[:], ALU.min, ALU.add)
                    if last is not None:
                        last.then_inc(s_Md, 1)

                def stack(stage, i, g, v, use):
                    kind, rel, n, c = use
                    G = (i + rel) * GROUPS + n
                    m, k = (c, n) if kind == "Q" else (2 + c, GROUPS + n)
                    dve.wait_ge(s_Ma, through("A", stage, i, g, v))
                    if kind == "Q":
                        wait(dve, s_q, 2 * (G - 1) + c + 1)
                        out = stk[:, c, :]
                    else:
                        out = K[:, n, chunk(c)]
                    dve.scalar_tensor_tensor(out, qh[:, m % 2, :].bitcast(F32), low[:, k:k + 1],
                                             qf[:, m % 2, :], ALU.mult, ALU.add).then_inc(s_st, 1)

                def normalize(i):
                    for t in range(TPS):
                        last = dve.tensor_scalar(xn[:, t, :], x[:, bass.ds((i * TPS + t) * P, P)],
                                                 mv[:, bass.ds(i * TPS + t, 1), 0:1].rearrange("p a b -> p (a b)"),
                                                 rstd[:, bass.ds(i * TPS + t, 1)], ALU.subtract, ALU.mult)
                    last.then_inc(s_xn, 1)

                def slot(stage, i, g):
                    G = i * GROUPS + g
                    if g == SLOTS[stage][0]:
                        chain[0] = Chain(dve, s_gch, 2 + base("C", stage, i))
                    if stage == "pre":
                        normalize(0)
                    for v in steps(stage):
                        if v == -4:
                            statistics(range(TPS, TILES), Chain(dve, s_gch, 1))
                        if v == -1:
                            dve.wait_ge(s_cst, 4)
                        before = use_before(stage, g, v, 1)
                        for j in range(GH):
                            s = SPS * v + j
                            if has_max(stage, g) and v >= 0:
                                max_unit(G + 1, (g + 1) % GROUPS, s)
                                if j == 0 and s and SU[s - 1][1] == 1:
                                    both_chunks(G + 1, (g + 1) % GROUPS, SU[s - 1][0])
                            if before:
                                m_read(stage, i, before[1], before[2], before[0], chain[0], j)
                        if before and before[0][0] in ("Q", "K"):
                            stack(stage, i, before[1], before[2], before[0])
                        if v == 8 and g == 1 and stage in ("first", "mid"):
                            if stage == "first":
                                dve.wait_ge(s_rstd, 2)
                            normalize(i + 1)
                    if has_max(stage, g):
                        both_chunks(G + 1, (g + 1) % GROUPS, TPS - 1)

                chain = [None]
                all_slots(slot, dve)

            @block.gpsimd
            def _(pool):
                pool.memset(mhalf[:], -0.5).then_inc(s_cst, 1)
                pool.memset(zero[:], 0.0).then_inc(s_cst, 1)
                pool.wait_ge(s_cst, 2)

                def rstd_of(n, t):
                    pool.wait_ge(s_mv, n + 1)
                    pool.tensor_scalar(veps[:, t], mv[:, t, 1], EPS, None, ALU.add).then_inc(s_ve, 1)
                    pool.wait_ge(s_ve, n + 1)
                    pool.tensor_tensor(rstd[:, t], veps[:, t], mhalf[:, t], ALU.pow).then_inc(s_rstd, 1)

                rstd_of(0, slice(0, TPS))
                pool.memset(Q[:, 0:GH, :].bitcast(F32), 0.0).then_inc(s_cst, 1)
                pool.memset(V[:], 0.0).then_inc(s_cst, 1)
                pool.memset(mt[:], 0.0).then_inc(s_cst, 1)
                pool.memset(Q[:, GH:, :].bitcast(F32), 0.0).then_inc(s_cst, 1)
                rstd_of(1, slice(TPS, TILES))
                pool.wait_ge(s_cst, 6)

                def split_max(stage, i, slot, G, g, c):
                    if c == 0:
                        pool.wait_ge(s_max, G * NS + TPB * GH)
                    else:
                        pool.wait_ge(s_mx, (G + 1) * TPB)
                    if not (isinstance(G, int) and G == 0):
                        pool.wait_ge(s_M, through("M", stage, i, slot - 1, 1 if c else 7))
                    src = mx[:, g % 2, TPB * c:TPB * (c + 1), :]
                    m4 = mt[:, c, :, :].rearrange("p t (j r) -> p t j r", j=GH)
                    pool.tensor_tensor(mxh[:, c, :, :], src, zero[:], ALU.add).then_inc(s_pch, 1)
                    pool.wait_ge(s_pch, 2 * G + c + 1)
                    high = mxh[:, c, :, :].bitcast(F32)
                    pool.tensor_tensor(m4[:, :, :, 3 * HD], zero[:], high, ALU.subtract)
                    pool.tensor_tensor(m4[:, :, :, 3 * HD + 1], high, src, ALU.subtract).then_inc(s_sp, 1)

                def mask_step(i, g, v):
                    pool.wait_ge(s_exp, ((i * GROUPS + g) * NT + v + 1) * GH)
                    pool.tensor_tensor(spare[:, DIAG.index(v) % 4:DIAG.index(v) % 4 + 1], zero[:, 0, 0:1], zero[:, 0, 0:1],
                                       ALU.add)
                    d = pt[:, (v % 2) * GH:(v % 2 + 1) * GH, 0:P]
                    pool.affine_select(out=d, in_=d, compare_op=ALU.is_ge, fill=0.0, base=0,
                                       pattern=[[0, GH], [1, P]], channel_multiplier=-1).then_inc(s_pm, 1)

                def slot(stage, i, g):
                    G = i * GROUPS + g
                    if has_exp(stage):
                        split_max(stage, i, g, G, g, 1)
                        for v in DIAG[:TPB]:
                            mask_step(i, g, v)
                    if has_max(stage, g):
                        split_max(stage, i, g, G + 1, (g + 1) % GROUPS, 0)
                    if has_exp(stage):
                        for v in DIAG[TPB:]:
                            mask_step(i, g, v)

                all_slots(slot, pool)
        ph.clear()
def macaron_program(nc, hidden, identity, out, moe, mam, tern, att):
    PAD = 2 * TPB
    with ExitStack() as ctx:
        x = ctx.enter_context(nc.sbuf_tensor("x", [P, (TILES + PAD) * P], F32))
        ident = ctx.enter_context(nc.sbuf_tensor("ident", [P, P], F32))
        s_load = ctx.enter_context(nc.semaphore("load"))
        s_store = ctx.enter_context(nc.semaphore("store"))
        x_tiles = x[:, 0:TOKENS].rearrange("p (t c) -> p t c", t=TILES)

        with nc.Block() as block:
            @block.sync
            def _(sp):
                sp.dma_start(x_tiles, hidden.rearrange("b (t p) c -> p (b t) c", p=P)).then_inc(s_load, 16)
                sp.dma_start(ident[:], identity).then_inc(s_load, 16)
                sp.wait_ge(s_load, 32)

            @block.gpsimd
            def _(pool):
                pool.memset(x[:, TOKENS:], 0.0)

        moe_ffn(nc, "m0", x, ident, moe)
        mamba(nc, "a0", x, ident, mam)
        moe_ffn(nc, "m1", x, ident, moe)
        ternary_ffn(nc, "t0", x, ident, tern)
        attention(nc, "a1", x, ident, att)
        ternary_ffn(nc, "t1", x, ident, tern)

        with nc.Block() as block:
            @block.sync
            def _(sp):
                sp.dma_start(out.rearrange("b (t p) c -> p (b t) c", p=P), x_tiles).then_inc(s_store, 16)
                sp.wait_ge(s_store, 16)


def stacked(a, parts):
    return a.reshape(parts, P, *a.shape[1:]).swapaxes(0, 1)


def moe_layout(inp):
    g = lambda n: inp["L0_ffn_" + n]
    E, H, HID = g("be2").shape[0], g("Wr1").shape[1], g("Ws1").shape[1]
    wr1, wr2, br1 = np.zeros((P, P), np.float32), np.zeros((P, E), np.float32), np.zeros((P, 1), np.float32)
    wr1[:, :H] = g("Wr1")
    wr2[:H] = g("Wr2")
    wr2[H] = g("br2")
    br1[:H, 0] = g("br1")
    br1[H] = 1
    b1 = np.concatenate([g("be1"), g("bs1")[None]])
    w2 = np.concatenate([g("We2"), g("Ws2")[None]])
    sel = np.zeros((2, E, E, P), np.float32)
    for e in range(E):
        sel[:, e, e] = 1
    return {
        "wr1": wr1, "wr2": wr2, "br1": br1,
        "b1": b1.reshape(E + 1, HID // P, P).transpose(2, 0, 1),
        "bs2": g("bs2").reshape(P, 1),
        "be2": np.concatenate([g("be2"), g("be2")]),
        "w1": np.concatenate([g("We1"), g("Ws1")[None]]),
        "w2": w2.reshape(E + 1, HID // P, P, P).transpose(0, 2, 1, 3).reshape(E + 1, P, HID),
        "route_sel": sel.reshape(2 * E, E, P),
        "rank": np.broadcast_to(E - np.arange(E, dtype=np.float32), (P, TPB, E)),
    }


def mamba_layout(inp):
    g = lambda n: inp["L0_attn_" + n]
    both = lambda n: np.stack([g(n + "f"), g(n + "r")])
    ns, rank = g("A_log_f").shape[1], g("dt_proj_w_f").shape[1]
    dbc = 4 * ns
    b, c = np.arange(rank, rank + ns), np.arange(rank + ns, rank + 2 * ns)
    rows = np.concatenate([b, c, b, c, np.arange(rank)])
    dtw = np.zeros((dbc + rank, 2, 2, P), np.float32)
    dtw[dbc:] = both("dt_proj_w_").transpose(2, 0, 1).reshape(rank, 2, 2, P)
    sel = np.zeros((2, 2 * ns, 2 * ns, P), np.float32)
    for n in range(2 * ns):
        sel[:, n, n] = 1
    halves = lambda a: a.reshape(2, 2, P, -1).transpose(2, 0, 1, 3)
    return {
        "in_proj": g("in_proj_w").T,
        "conv_w": halves(both("conv_w_")),
        "vecs": np.stack([halves(both(n))[..., 0] for n in ("conv_b_", "dt_proj_b_", "D_")], 1),
        "x_proj": both("x_proj_w_")[:, rows].reshape(2, dbc + rank, 2, P).transpose(3, 0, 2, 1),
        "dt_proj": dtw,
        "A_log": halves(both("A_log_")),
        "out_proj": stacked(g("out_proj_w").T, 2),
        "bc_sel": sel.reshape(dbc, 2 * ns, P),
    }


def ternary_layout(inp):
    g = lambda n: inp["L1_ffn_" + n]
    square = lambda n: g(n).T.reshape(4, P, 4 * P)
    w3 = stacked(g("w3_w").T, 4).reshape(1, P, 4 * P)
    return {
        "w": np.concatenate([g("w1_w").T[None], g("w2_w").T[None], square("h1_w"), square("h2_w"), w3]),
        "scales": np.concatenate([g(n).reshape(-1, P).T for n in ("w1_s", "w2_s", "h1_s", "h2_s", "w3_s")], 1),
    }


def attention_layout(inp):
    g = lambda n: inp["L1_attn_" + n]
    w_in, b_in = g("w_in"), g("b_in")
    HEADS, HD, GH, ROWS = 16, 8, 4, 32
    GROUPS = HEADS // GH
    wqk = np.zeros((P, 2, GROUPS, GH, ROWS), np.float32)
    bqk, low = np.zeros((2, GROUPS, GH, ROWS), np.float32), np.zeros((2, GROUPS, GH, ROWS), np.float32)
    scale = np.ones((2, GROUPS, GH, ROWS), np.float32)
    for kind in range(2):
        w = w_in[kind * P:(kind + 1) * P].T.reshape(P, GROUPS, GH, HD)
        b = b_in[kind * P:(kind + 1) * P].reshape(GROUPS, GH, HD)
        for part in range(3):
            wqk[:, kind, :, :, part * HD:(part + 1) * HD] = w
            bqk[kind, :, :, part * HD:(part + 1) * HD] = b
    low[0, :, :, HD:2 * HD] = -1
    low[1, :, :, 2 * HD:3 * HD] = -1
    bqk[1, :, :, 3 * HD:3 * HD + 2] = 1
    scale[0] = np.float32(1.0 / np.sqrt(HD))
    wv, bv = np.zeros((P, HEADS, HD + 1), np.float32), np.ones((HEADS, HD + 1), np.float32)
    wv[:, :, :HD] = w_in[2 * P:].T.reshape(P, HEADS, HD)
    bv[:, :HD] = b_in[2 * P:].reshape(HEADS, HD)
    cols = lambda a: a.reshape(2 * GROUPS, P).T
    return {
        "w_qk": wqk.reshape(P, 2 * GROUPS, P), "b_qk": cols(bqk), "scale": cols(scale), "low": cols(low),
        "w_v": wv.reshape(P, -1), "b_v": np.broadcast_to(bv.reshape(1, -1), (P, HEADS * (HD + 1))),
        "w_out": g("w_out").T, "b_out": np.broadcast_to(g("b_out"), (P, P)),
        "mask": np.triu(np.full((P, P), -1e30, np.float32), 1),
    }


def kernel(**inputs):
    import concourse.bacc as bacc
    from concourse.bass_utils import run_bass_kernel_spmd

    inp = {k: np.asarray(v) for k, v in inputs.items()}
    nc = bacc.Bacc("TRN2", target_bir_lowering=False, num_devices=1)
    arrays = {}

    def tensor(name, a):
        arrays[name] = np.ascontiguousarray(a)
        return nc.dram_tensor(name, a.shape, mybir.dt.from_np(a.dtype), kind="ExternalInput").ap()

    hidden = tensor("hidden", inp["L0_attn_hidden_states"])
    identity = tensor("identity", np.eye(P, dtype=np.float32))
    groups = [{k: tensor(f"{tag}_{k}", a) for k, a in layout(inp).items()}
              for tag, layout in (("moe", moe_layout), ("mamba", mamba_layout),
                                  ("ternary", ternary_layout), ("attention", attention_layout))]
    out = nc.dram_tensor("out", (NBATCH, SEQ, P), F32, kind="ExternalOutput").ap()
    macaron_program(nc, hidden, identity, out, *groups)
    return run_bass_kernel_spmd(nc, [arrays], core_ids=[0]).results[0]["out"]
```
